# Optimizing a Trainium2 kernel written in Bass

```python
import numpy as np
import jax
import jax.numpy as jnp

def _softmax(x, axis=-1):
    return jax.nn.softmax(x, axis=axis)

def _gelu(x):
    return jax.nn.gelu(x, approximate=True)

def _silu(x):
    return jax.nn.silu(x)

def _sigmoid(x):
    return jax.nn.sigmoid(x)

def _layernorm(x, axis=-1, eps=1e-05):
    m = jnp.mean(x, axis=axis, keepdims=True)
    v = jnp.var(x, axis=axis, keepdims=True)
    return (x - m) / jnp.sqrt(v + eps)

def _scatter_add(tgt, idx, src, axis=0):
    return tgt.at[idx].add(src)

def _segment_sum(src, seg, n):
    return jax.ops.segment_sum(src, seg, n)
kernel_name = 'mk_sandwich_d1_jaxref_r2_b8a8a7'

def setup_inputs(seed: int=0):
    np.random.seed(seed)
    _w = jnp.asarray

    def _L0_attn_setup():
        import math
        import jax, jax.numpy as jnp
        import numpy as np
        EPS = 1e-06
        NB_FEATURES = 128
        NUM_HEADS = 16

        def fwht(x):
            shape = x.shape
            P = shape[-1]
            h = 1
            while h < P:
                x = x.reshape(shape[:-1] + (-1, 2 * h))
                a, b = (x[..., :h], x[..., h:])
                x = jnp.concatenate([a + b, a - b], axis=-1).reshape(shape)
                h *= 2
            return x

        def apply_rope(q, k):
            C, H, L, D = q.shape
            dtype = q.dtype
            freqs = 10000.0 ** (-jnp.arange(0, D, 2, dtype=dtype) / D)
            pos = jnp.arange(L - 1, dtype=dtype)[:, None]
            ang = pos * freqs
            cos, sin = (jnp.cos(ang), jnp.sin(ang))

            def rot(t):
                ts = t[..., 1:, :]
                t1, t2 = (ts[..., 0::2], ts[..., 1::2])
                re = t1 * cos - t2 * sin
                im = t1 * sin + t2 * cos
                rs = jnp.stack([re, im], axis=-1).reshape(ts.shape)
                return jnp.concatenate([t[..., :1, :], rs], axis=-2)
            return (rot(q), rot(k))

        def sorf_phi(x, signs, scales, m):
            C, H, L, D = x.shape
            R, P = (signs.shape[1], signs.shape[-1])
            x_p = x if D == P else jnp.pad(x, ((0, 0), (0, 0), (0, 0), (0, P - D)))
            inv = 1.0 / math.sqrt(P)
            s1 = signs[None, :, :, 0, None, :]
            s2 = signs[None, :, :, 1, None, :]
            s3 = signs[None, :, :, 2, None, :]
            g = (scales * inv)[None, :, :, None, :]
            t = fwht(x_p[:, :, None, :, :] * s1) * inv
            t = fwht(t * s2) * inv
            t = fwht(t * s3) * inv
            block = t * g
            phi = block.transpose(0, 1, 3, 2, 4).reshape(C, H, L, R * P)[..., :m]
            x_norm_sq = jnp.sum(x * x, axis=-1, keepdims=True) / 2.0
            return jnp.exp(phi - x_norm_sq) / math.sqrt(m)
        key = jax.random.key(seed)
        ks = jax.random.split(key, 5)
        C, L, E = (4, 2048, 512)
        H, D = (NUM_HEADS, 512 // NUM_HEADS)
        P = 64
        R = 4
        x = jax.random.normal(ks[0], (C, L, E), dtype=jnp.float32)
        w_qkv = jax.random.normal(ks[1], (3 * E, E), dtype=jnp.float32) / math.sqrt(E)
        w_out = jax.random.normal(ks[2], (E, E), dtype=jnp.float32) / math.sqrt(E)
        sorf_signs = (2.0 * jax.random.randint(ks[3], (H, R, 3, P), 0, 2) - 1.0).astype(jnp.float32)
        sorf_scales = jax.random.normal(ks[4], (H, R, P), dtype=jnp.float32)
        return {'x': x, 'w_qkv': w_qkv, 'w_out': w_out, 'sorf_signs': sorf_signs, 'sorf_scales': sorf_scales}
    _L0_attn_in = _L0_attn_setup()

    def _L0_ffn_setup():
        import jax, jax.numpy as jnp
        import numpy as np
        D = 512
        I = 256
        E = 32
        K = 4
        T = 2 * 1024
        C = 2 * T * K // E
        key = jax.random.key(seed)
        ks = jax.random.split(key, 9)
        bf = jnp.bfloat16
        std = 0.02
        x = jax.random.normal(ks[0], (2, 1024, D), dtype=jnp.float32).astype(bf)
        gate_w = (std * jax.random.normal(ks[1], (E, D), dtype=jnp.float32)).astype(bf)
        bias = jnp.zeros((E,), jnp.float32)
        W1 = (std * jax.random.normal(ks[2], (E, D, I), dtype=jnp.float32)).astype(bf)
        W3 = (std * jax.random.normal(ks[3], (E, D, I), dtype=jnp.float32)).astype(bf)
        W2 = (std * jax.random.normal(ks[4], (E, I, D), dtype=jnp.float32)).astype(bf)
        sw1 = (std * jax.random.normal(ks[5], (I, D), dtype=jnp.float32)).astype(bf)
        sw3 = (std * jax.random.normal(ks[6], (I, D), dtype=jnp.float32)).astype(bf)
        sw2 = (std * jax.random.normal(ks[7], (D, I), dtype=jnp.float32)).astype(bf)
        return {'x': x, 'gate_w': gate_w, 'bias': bias, 'W1': W1, 'W3': W3, 'W2': W2, 'sw1': sw1, 'sw3': sw3, 'sw2': sw2}
    _L0_ffn_in = _L0_ffn_setup()
    _d = {'L0_attn_x': _L0_attn_in['x'], 'L0_attn_w_qkv': _L0_attn_in['w_qkv'], 'L0_attn_w_out': _L0_attn_in['w_out'], 'L0_attn_sorf_signs': _L0_attn_in['sorf_signs'], 'L0_attn_sorf_scales': _L0_attn_in['sorf_scales'], 'L0_ffn_gate_w': _L0_ffn_in['gate_w'], 'L0_ffn_bias': _L0_ffn_in['bias'], 'L0_ffn_W1': _L0_ffn_in['W1'], 'L0_ffn_W3': _L0_ffn_in['W3'], 'L0_ffn_W2': _L0_ffn_in['W2'], 'L0_ffn_sw1': _L0_ffn_in['sw1'], 'L0_ffn_sw3': _L0_ffn_in['sw3'], 'L0_ffn_sw2': _L0_ffn_in['sw2']}
    _x0 = _d['L0_attn_x']
    _d['L0_attn_x'] = jax.random.normal(jax.random.fold_in(jax.random.key(seed), 1), (4, 2048, 512), dtype=_x0.dtype)
    del _x0
    return _d

def reference(L0_attn_x, L0_attn_w_qkv, L0_attn_w_out, L0_attn_sorf_signs, L0_attn_sorf_scales, L0_ffn_gate_w, L0_ffn_bias, L0_ffn_W1, L0_ffn_W3, L0_ffn_W2, L0_ffn_sw1, L0_ffn_sw3, L0_ffn_sw2):

    def _L0_attn_ref(x, w_qkv, w_out, sorf_signs, sorf_scales):
        import math
        import jax, jax.numpy as jnp
        import numpy as np
        EPS = 1e-06
        NB_FEATURES = 128
        NUM_HEADS = 16

        def fwht(x):
            shape = x.shape
            P = shape[-1]
            h = 1
            while h < P:
                x = x.reshape(shape[:-1] + (-1, 2 * h))
                a, b = (x[..., :h], x[..., h:])
                x = jnp.concatenate([a + b, a - b], axis=-1).reshape(shape)
                h *= 2
            return x

        def apply_rope(q, k):
            C, H, L, D = q.shape
            dtype = q.dtype
            freqs = 10000.0 ** (-jnp.arange(0, D, 2, dtype=dtype) / D)
            pos = jnp.arange(L - 1, dtype=dtype)[:, None]
            ang = pos * freqs
            cos, sin = (jnp.cos(ang), jnp.sin(ang))

            def rot(t):
                ts = t[..., 1:, :]
                t1, t2 = (ts[..., 0::2], ts[..., 1::2])
                re = t1 * cos - t2 * sin
                im = t1 * sin + t2 * cos
                rs = jnp.stack([re, im], axis=-1).reshape(ts.shape)
                return jnp.concatenate([t[..., :1, :], rs], axis=-2)
            return (rot(q), rot(k))

        def sorf_phi(x, signs, scales, m):
            C, H, L, D = x.shape
            R, P = (signs.shape[1], signs.shape[-1])
            x_p = x if D == P else jnp.pad(x, ((0, 0), (0, 0), (0, 0), (0, P - D)))
            inv = 1.0 / math.sqrt(P)
            s1 = signs[None, :, :, 0, None, :]
            s2 = signs[None, :, :, 1, None, :]
            s3 = signs[None, :, :, 2, None, :]
            g = (scales * inv)[None, :, :, None, :]
            t = fwht(x_p[:, :, None, :, :] * s1) * inv
            t = fwht(t * s2) * inv
            t = fwht(t * s3) * inv
            block = t * g
            phi = block.transpose(0, 1, 3, 2, 4).reshape(C, H, L, R * P)[..., :m]
            x_norm_sq = jnp.sum(x * x, axis=-1, keepdims=True) / 2.0
            return jnp.exp(phi - x_norm_sq) / math.sqrt(m)
        C, L, E = x.shape
        H = NUM_HEADS
        D = E // H
        qkv = x @ w_qkv.T
        q, k, v = jnp.split(qkv, 3, axis=-1)
        to_heads = lambda t: t.reshape(C, L, H, D).transpose(0, 2, 1, 3)
        q, k, v = (to_heads(q), to_heads(k), to_heads(v))
        q, k = apply_rope(q, k)
        q_phi = sorf_phi(q, sorf_signs, sorf_scales, NB_FEATURES)
        k_phi = sorf_phi(k, sorf_signs, sorf_scales, NB_FEATURES)
        S = jnp.einsum('chlm,chld->chmd', k_phi, v)
        sum_k = jnp.sum(k_phi, axis=2)
        numer = jnp.einsum('chlm,chmd->chld', q_phi, S)
        denom = jnp.maximum(jnp.einsum('chlm,chm->chl', q_phi, sum_k), EPS)
        out_heads = numer / denom[..., None]
        out = out_heads.transpose(0, 2, 1, 3).reshape(C, L, E)
        return out @ w_out.T

    def _L0_ffn_ref(x, gate_w, bias, W1, W3, W2, sw1, sw3, sw2):
        import jax, jax.numpy as jnp
        import numpy as np
        D = 512
        I = 256
        E = 32
        K = 4
        T = 2 * 1024
        C = 2 * T * K // E
        X = x.reshape(-1, D)
        logits = (X @ gate_w.T).astype(jnp.float32)
        scores = jax.nn.sigmoid(logits)
        _, idx = jax.lax.top_k(scores + bias[None, :], K)
        w = jnp.take_along_axis(scores, idx, axis=-1)
        w = w / jnp.clip(jnp.sum(w, axis=-1, keepdims=True), 1e-12, None)
        w = w.astype(x.dtype)
        eid = idx.reshape(-1)
        onehot = (eid[:, None] == jnp.arange(E)[None, :]).astype(jnp.int32)
        pos = jnp.take_along_axis(jnp.cumsum(onehot, axis=0) - 1, eid[:, None], axis=1)[:, 0]
        valid = pos < C
        posc = jnp.minimum(pos, C - 1)
        Xrep = jnp.repeat(X, K, axis=0)
        xe = jnp.zeros((E, C, D), x.dtype).at[eid, posc].add(jnp.where(valid[:, None], Xrep, jnp.zeros((), x.dtype)))
        h = jax.nn.silu(jnp.einsum('ecd,edi->eci', xe, W1)) * jnp.einsum('ecd,edi->eci', xe, W3)
        ye = jnp.einsum('eci,eid->ecd', h, W2)
        gflat = jnp.where(valid, w.reshape(-1), jnp.zeros((), x.dtype))
        yrows = ye[eid, posc] * gflat[:, None]
        out = yrows.reshape(-1, K, D).sum(axis=1)
        out = out + jax.nn.silu(X @ sw1.T) * (X @ sw3.T) @ sw2.T
        return out.reshape(x.shape)
    x = L0_attn_x
    x = x + _layernorm(_L0_attn_ref(_layernorm(x, axis=-1), L0_attn_w_qkv, L0_attn_w_out, L0_attn_sorf_signs, L0_attn_sorf_scales), axis=-1)
    x = x + _layernorm(_L0_ffn_ref(_layernorm(x, axis=-1), L0_ffn_gate_w, L0_ffn_bias, L0_ffn_W1, L0_ffn_W3, L0_ffn_W2, L0_ffn_sw1, L0_ffn_sw3, L0_ffn_sw2), axis=-1)
    return x

_drawn_inputs = setup_inputs


def setup_inputs(seed=0):
    import zlib

    import numpy as np

    out = dict(_drawn_inputs(seed))
    spreads = {'L0_ffn_bias': (0.0, 0.1)}
    factors = {}
    for name, (base, spread) in spreads.items():
        noise = np.random.default_rng([zlib.crc32(name.encode()), seed]).standard_normal(out[name].shape)
        drawn = base * np.exp(spread * noise) if base else spread * noise
        out[name] = jnp.asarray(drawn.astype(out[name].dtype))
    for name, factor in factors.items():
        out[name] = (out[name] * factor).astype(out[name].dtype)
    return out
```

```python
from contextlib import ExitStack

import concourse.bass as bass
from concourse import mybir

P = 128
C, L, E = 4, 2048, 512
H, D = 16, 32
M = 128
HP = 64
NE, K, I = 32, 4, 256
CAP = 512
T = C * L
G = 512
NG = T // G
A = G // P
EC = E // P
GPC = L // G
NSLOT = NE * CAP
W_SCALE = 256.0
M_SCALE = 64.0
NOWHERE = 1.0e6

ALU = mybir.AluOpType
ACT = mybir.ActivationFunctionType
AX = mybir.AxisListType
F32 = mybir.dt.float32
F16 = mybir.dt.float16
BF16 = mybir.dt.bfloat16
U32 = mybir.dt.uint32


class Tools:

    def __init__(self, nc, ctx, stage):
        self.nc, self.ctx, self.stage, self.sems = nc, ctx, stage, []
        ctx.callback(self.close)

    def close(self):
        self.nc.clear_and_free_semaphores(self.sems)
        self.nc.all_engine_barrier()

    def sb(self, name, shape, dt=F32):
        return self.ctx.enter_context(self.nc.sbuf_tensor(f"{self.stage}_{name}", shape, dt))

    def pair(self, name, shape, dt=F32):
        return [self.sb(f"{name}{k}", shape, dt) for k in range(2)]

    def psum(self, name, banks=1):
        return self.ctx.enter_context(self.nc.psum_tensor(f"{self.stage}_{name}", [P, 512 * banks], F32))

    def sem(self, name):
        self.sems.append(self.nc.alloc_semaphore(f"{self.stage}_{name}"))
        return self.sems[-1]


def hold(eng, sem, value, pace):
    eng.wait_ge(sem, value)
    eng.sem_inc(pace, 1)


def setup_stage(nc, io, keep):
    with ExitStack() as ctx:
        t = Tools(nc, ctx, "s0")
        sb, sem = t.sb, t.sem
        had = sb("had", [HP, HP])
        s3 = sb("s3", [HP, 2 * H])
        s2 = sb("s2", [HP, 2 * H])
        s1 = sb("s1", [96, 2 * H])
        g = sb("g", [96, 2 * H * HP])
        left3 = sb("left3", [HP, 2 * H, HP])
        left2 = sb("left2", [HP, 2 * H, 96])
        y = sb("y", [HP, 2 * H, HP])
        m = sb("m", [96, 2 * H * HP])
        w = sb("w", [P, EC, 3 * E])
        zero = sb("zero", [P, NSLOT // P], U32)
        pY = [t.psum(f"pY{q}") for q in range(4)]
        pZ = [t.psum(f"pZ{q}") for q in range(4)]
        loaded, wloaded, kept = sem("loaded"), sem("wloaded"), sem("kept")
        left_ready, y_ready, y_copied, z_ready = sem("left_ready"), sem("y_ready"), sem("y_copied"), sem("z_ready")
        m_signed, m_ready, hi_ready, w_hi, zeroed, cleared = (
            sem("m_signed"), sem("m_ready"), sem("hi_ready"), sem("w_hi"), sem("zeroed"), sem("cleared"))
        block = ctx.enter_context(nc.Block())

        @block.sync
        def _(sp):
            sp.dma_start(had[:], io["had"]).then_inc(loaded, 16)
            sp.dma_start(s3[:], io["signs"][:, 2, :]).then_inc(loaded, 16)
            sp.dma_start(s2[:], io["signs"][:, 1, :]).then_inc(loaded, 16)
            for r in range(3):
                sp.dma_start(s1[32 * r:32 * r + 32, :], io["signs"][0:D, 0, :]).then_inc(loaded, 16)
            sp.dma_start(g[:], io["scales"].to_broadcast([96, 2 * H * HP])).then_inc(loaded, 16)
            sp.dma_start(w[:], io["w_qkvT"].rearrange("(c p) n -> p c n", p=P)).then_inc(wloaded, 16)
            sp.dma_start(keep["wo"][:], io["w_outT"].rearrange("(c p) n -> p c n", p=P)).then_inc(kept, 16)
            for name in ("ident16", "ident32", "heads", "tri", "ones", "gate", "expert", "bias"):
                src = io[name]
                if src.shape[0] == 1:
                    src = src.to_broadcast([P, src.shape[1]])
                sp.dma_start(keep[name][:], src).then_inc(kept, 16)
            sp.wait_ge(zeroed, 1)
            sp.dma_start(io["slot_token"].rearrange("(p n) o -> p (n o)", p=P), zero[:]).then_inc(cleared, 16)
            sp.wait_ge(kept, 16 * 9)
            sp.wait_ge(cleared, 16)

        @block.vector
        def _(dve):
            nc.vector.memset(zero[:], 0).then_inc(zeroed, 1)
            dve.wait_ge(loaded, 16 * 7)
            nc.vector.tensor_tensor(left3[:], had[:].unsqueeze(1).broadcast_to([HP, 2 * H, HP]),
                                    s3[:].unsqueeze(2).broadcast_to([HP, 2 * H, HP]), ALU.mult).then_inc(left_ready, 1)
            for r in range(3):
                nc.vector.tensor_tensor(left2[:, :, 32 * r:32 * r + 32],
                                        had[:, 0:D].unsqueeze(1).broadcast_to([HP, 2 * H, D]),
                                        s2[:].unsqueeze(2).broadcast_to([HP, 2 * H, D]), ALU.mult).then_inc(left_ready, 1)
            for q in range(4):
                dve.wait_ge(y_ready, q + 1)
                nc.vector.tensor_copy(y[:, 8 * q:8 * q + 8, :].rearrange("p a b -> p (a b)"),
                                      pY[q][0:HP, :]).then_inc(y_copied, 1)
            for q in range(4):
                dve.wait_ge(z_ready, q + 1)
                mq = m[:, 512 * q:512 * q + 512]
                nc.vector.tensor_tensor(mq.rearrange("p (a b) -> p a b", b=HP),
                                        pZ[q][0:96, :].rearrange("p (a b) -> p a b", b=HP),
                                        s1[:, 8 * q:8 * q + 8].unsqueeze(2).broadcast_to([96, 8, HP]),
                                        ALU.mult).then_inc(m_signed, 1)
                dve.wait_ge(m_signed, q + 1)
                nc.vector.scalar_tensor_tensor(out=mq, in0=mq, scalar=M_SCALE / HP ** 2,
                                               in1=g[:, 512 * q:512 * q + 512],
                                               op0=ALU.mult, op1=ALU.mult).then_inc(m_ready, 1)
            dve.wait_ge(hi_ready, 1)
            dve.wait_ge(m_ready, 4)
            feat = keep["feat"][:].rearrange("p h f -> p (h f)")
            nc.vector.tensor_tensor(feat[32:64, :], m[32:64, :], feat[32:64, :], ALU.subtract).then_inc(m_ready, 1)
            for c in range(EC):
                dve.wait_ge(w_hi, c + 1)
                nc.vector.scalar_tensor_tensor(out=keep["wqkv"][:, 1, c, :], in0=w[:, c, :], scalar=W_SCALE,
                                               in1=keep["wqkv"][:, 0, c, :], op0=ALU.mult,
                                               op1=ALU.subtract).then_inc(m_ready, 1)

        @block.scalar
        def _(act):
            act.wait_ge(wloaded, 16)
            for c in range(EC):
                nc.scalar.activation(keep["wqkv"][:, 0, c, :], w[:, c, :], ACT.Copy, scale=W_SCALE).then_inc(w_hi, 1)
            act.wait_ge(m_ready, 4)
            nc.scalar.activation(keep["feat"][:].rearrange("p h f -> p (h f)"), m[:], ACT.Copy).then_inc(hi_ready, 1)

        @block.tensor
        def _(pe):
            pe.wait_ge(left_ready, 4)
            for i in range(2 * H):
                mm = nc.tensor.matmul(pY[i // 8][0:HP, (i % 8) * HP:(i % 8 + 1) * HP], left3[:, i, :], had[:],
                                      start=True, stop=True)
                if i % 8 == 7:
                    mm.then_inc(y_ready, 1)
            for i in range(2 * H):
                if i % 8 == 0:
                    pe.wait_ge(y_copied, i // 8 + 1)
                mm = nc.tensor.matmul(pZ[i // 8][0:96, (i % 8) * HP:(i % 8 + 1) * HP], left2[:, i, :], y[:, i, :],
                                      start=True, stop=True)
                if i % 8 == 7:
                    mm.then_inc(z_ready, 1)


def norm_stage(nc, io, keep, stage, src, dst_T, dst_rows):
    with ExitStack() as ctx:
        t = Tools(nc, ctx, stage)
        x = t.pair("x", [P, A, E])
        hl = t.pair("hl", [P, A, 2, E], F16)
        xT = t.pair("xT", [P, 2, EC, G], F16)
        stats = t.pair("stats", [P, A, 6])
        mv = t.pair("mv", [P, A, 2])
        rstd = t.pair("rstd", [P, A])
        power = t.sb("power", [P, A])
        turned = [t.psum(f"turned{k}") for k in range(2)]
        loaded = [t.sem(f"loaded{k}") for k in range(2)]
        stored = [t.sem(f"stored{k}") for k in range(2)]
        rows_stored = [t.sem(f"rows_stored{k}") for k in range(2)]
        pace = t.sem("pace")
        stats_ready, mv_ready, var_ready, rstd_ready = (
            t.sem("stats_ready"), t.sem("mv_ready"), t.sem("var_ready"), t.sem("rstd_ready"))
        x_ready, hi_ready, lo_ready = t.sem("x_ready"), t.sem("hi_ready"), t.sem("lo_ready")
        turned_ready, xT_ready, power_ready = t.sem("turned_ready"), t.sem("xT_ready"), t.sem("power_ready")
        block = ctx.enter_context(nc.Block())

        @block.sync
        def _(sp):
            with nc.sync.Fori(0, NG // 2) as u:
                for k in range(2):
                    hold(sp, lo_ready, 2 * u + k + 1, pace)
                    sp.dma_start(x[k][:], src[bass.ds((2 * u + k) * G, G), :].rearrange("(a p) e -> p a e", p=P)
                                 ).then_inc(loaded[k], 16)

        @block.vector
        def _(dve):
            dve.sem_inc(lo_ready, 2)
            with nc.vector.Fori(0, NG // 2) as u:
                for k in range(2):
                    hold(dve, loaded[k], 16 * u + 16, pace)
                    for a in range(A):
                        ins = nc.vector.bn_stats(stats[k][:, a, :], x[k][:, a, :])
                    ins.then_inc(stats_ready, 1)
                    hold(dve, stats_ready, 2 * u + k + 1, pace)
                    for a in range(A):
                        ins = nc.vector.bn_aggr(mv[k][:, a, :], stats[k][:, a, :])
                    ins.then_inc(mv_ready, 1)
                    dve.wait_ge(rstd_ready, 2 * u + k + 1)
                    for a in range(A):
                        ins = nc.vector.tensor_scalar(x[k][:, a, :], x[k][:, a, :], mv[k][:, a, 0:1],
                                                      rstd[k][:, a:a + 1], ALU.subtract, ALU.mult)
                    ins.then_inc(x_ready, 1)
                    dve.wait_ge(hi_ready, 2 * u + k + 1)
                    nc.vector.tensor_tensor(hl[k][:, :, 1, :], x[k][:], hl[k][:, :, 0, :],
                                            ALU.subtract).then_inc(lo_ready, 1)

        @block.gpsimd
        def _(pool):
            nc.gpsimd.memset(power[:], -0.5).then_inc(power_ready, 1)
            pool.wait_ge(power_ready, 1)
            with nc.gpsimd.Fori(0, NG // 2) as u:
                for k in range(2):
                    hold(pool, mv_ready, 2 * u + k + 1, pace)
                    nc.gpsimd.tensor_scalar(rstd[k][:], mv[k][:, :, 1], 1e-5, None, ALU.add).then_inc(var_ready, 1)
                    pool.wait_ge(var_ready, 2 * u + k + 1)
                    nc.gpsimd.tensor_tensor(rstd[k][:], rstd[k][:], power[:], ALU.pow).then_inc(rstd_ready, 1)

        @block.scalar
        def _(act):
            for k in range(2):
                act.sem_inc(stored[k], 1)
                act.sem_inc(rows_stored[k], 1)
            act.sem_inc(xT_ready, 2)
            with nc.scalar.Fori(0, NG // 2) as u:
                for k in range(2):
                    act.wait_ge(x_ready, 2 * u + k + 1)
                    if dst_rows is not None:
                        act.wait_ge(rows_stored[k], 16 * u + 1)
                    nc.scalar.activation(hl[k][:, :, 0, :], x[k][:], ACT.Copy).then_inc(hi_ready, 1)
                    act.wait_ge(stored[k], 16 * u + 1)
                    for a in range(A):
                        act.wait_ge(turned_ready, (2 * u + k) * A + a + 1)
                        nc.scalar.activation(
                            xT[k][:, :, :, a * P:(a + 1) * P],
                            turned[a % 2][:].bitcast(F16).rearrange("p (s c q) -> p s c q", s=2, c=EC),
                            ACT.Copy).then_inc(xT_ready, 1)
                    act.wait_ge(xT_ready, (2 * u + k) * A + A + 2)
                    act.dma_start(dst_T[bass.ds(2 * u + k, 1)].rearrange("o p n -> p (o n)"),
                                  xT[k][:].rearrange("p s c q -> p (s c q)")).then_inc(stored[k], 16)
                    if dst_rows is not None:
                        act.wait_ge(lo_ready, 2 * u + k + 3)
                        act.dma_start(dst_rows[bass.ds((2 * u + k) * G, G), :].rearrange("(a p) n -> p a n", p=P),
                                      hl[k][:].rearrange("p a s e -> p a (s e)")).then_inc(rows_stored[k], 16)
            for k in range(2):
                act.wait_ge(stored[k], 1 + 16 * NG // 2)
                if dst_rows is not None:
                    act.wait_ge(rows_stored[k], 1 + 16 * NG // 2)

        @block.tensor
        def _(pe):
            with nc.tensor.Fori(0, NG // 2) as u:
                for k in range(2):
                    pe.wait_ge(lo_ready, 2 * u + k + 3)
                    for a in range(A):
                        pe.wait_ge(xT_ready, (2 * u + k) * A + a + 1)
                        for s in range(2):
                            for c in range(EC):
                                mm = nc.tensor.transpose(
                                    turned[a % 2][:].bitcast(F16)[:, (s * EC + c) * P:(s * EC + c + 1) * P],
                                    hl[k][:, a, s, c * P:(c + 1) * P], keep["ident16"][:])
                        mm.then_inc(turned_ready, 1)


def project_stage(nc, io, keep):
    with ExitStack() as ctx:
        t = Tools(nc, ctx, "s2")
        xT = t.pair("xT", [P, 2, EC, G], F16)
        table = t.sb("table", [P, 2, G])
        raw = t.pair("raw", [P, G])
        cosp = t.pair("cosp", [P, G])
        swap = t.pair("swap", [P, G])
        rot = t.pair("rot", [P, G])
        sq = t.pair("sq", [P, 2 * EC, G])
        hl = t.pair("hl", [P, 2, 2 * EC, G], F16)
        v = t.pair("v", [P, A, E])
        en = t.pair("en", [P, A, 2 * H])
        banks = [t.psum(f"proj{b}") for b in range(4)]
        norms = t.psum("norms")
        x_loaded, hl_stored, v_stored, en_stored = (
            [t.sem(f"{n}{k}") for k in range(2)] for n in ("x_loaded", "hl_stored", "v_stored", "en_stored"))
        table_loaded, pace = t.sem("table_loaded"), t.sem("pace")
        proj_ready, evac, cos_ready, swap_ready, sin_ready = (
            t.sem("proj_ready"), t.sem("evac"), t.sem("cos_ready"), t.sem("swap_ready"), t.sem("sin_ready"))
        rot_ready, hi_ready, sq_ready, lo_ready = (
            t.sem("rot_ready"), t.sem("hi_ready"), t.sem("sq_ready"), t.sem("lo_ready"))
        norms_ready, en_ready = t.sem("norms_ready"), t.sem("en_ready")
        QK = 2 * EC
        OUT = QK + A
        block = ctx.enter_context(nc.Block())

        @block.sync
        def _(sp):
            with nc.sync.Fori(0, GPC) as pg:
                hold(sp, sin_ready, C * QK * pg + 1, pace)
                hold(sp, cos_ready, C * QK * pg + 2, pace)
                sp.dma_start(table[:], io["turns"][bass.ds(pg, 1)].rearrange("o p s n -> p (o s) n")
                             ).then_inc(table_loaded, 16)
                with nc.sync.Fori(0, C // 2) as u:
                    for k in range(2):
                        hold(sp, proj_ready, OUT * C * pg + 2 * OUT * u + OUT * k + 1, pace)
                        sp.dma_start(xT[k][:].rearrange("p s c q -> p (s c q)"),
                                     io["xT"][bass.ds(2 * GPC * u + pg + GPC * k, 1)].rearrange("o p n -> p (o n)")
                                     ).then_inc(x_loaded[k], 16)

        @block.tensor
        def _(pe):
            pe.sem_inc(proj_ready, OUT + 1)
            pe.sem_inc(norms_ready, 2)
            with nc.tensor.Fori(0, GPC) as pg, nc.tensor.Fori(0, C // 2) as u:
                for k in range(2):
                    pe.wait_ge(x_loaded[k], 32 * pg + 16 * u + 16)
                    hi, lo = xT[k][:, 0], xT[k][:, 1]
                    for j in range(OUT):
                        pe.wait_ge(evac, OUT * C * pg + 2 * OUT * u + OUT * k + j + 1)
                        for c in range(EC):
                            if j < QK:
                                w = keep["wqkv"][:, :, c, j * P:(j + 1) * P]
                                parts = ((w[:, 0], hi[:, c]), (w[:, 0], lo[:, c]), (w[:, 1], hi[:, c]))
                            else:
                                w = keep["wqkv"][:, :, c, 2 * E:3 * E]
                                q = slice((j - QK) * P, (j - QK + 1) * P)
                                parts = ((hi[:, c, q], w[:, 0]), (hi[:, c, q], w[:, 1]), (lo[:, c, q], w[:, 0]))
                            for i, (left, right) in enumerate(parts):
                                mm = nc.tensor.matmul(banks[j % 4][:], left, right, start=(c == 0 and i == 0),
                                                      stop=(c == EC - 1 and i == 2))
                        mm.then_inc(proj_ready, 1)
                    pe.wait_ge(sq_ready, QK * C * pg + 2 * QK * u + QK * k + QK + 2)
                    pe.wait_ge(en_ready, C * pg + 2 * u + k + 1)
                    for a in range(A):
                        for j in range(QK):
                            mm = nc.tensor.matmul(norms[:, a * 2 * H:(a + 1) * 2 * H], sq[k][:, j, a * P:(a + 1) * P],
                                                  keep["heads"][:, j * 2 * H:(j + 1) * 2 * H],
                                                  start=(j == 0), stop=(j == QK - 1))
                    mm.then_inc(norms_ready, 1)

        @block.gpsimd
        def _(pool):
            pool.sem_inc(cos_ready, 2)
            with nc.gpsimd.Fori(0, GPC) as pg, nc.gpsimd.Fori(0, C // 2) as u:
                for k in range(2):
                    for j in range(QK):
                        if k == 0 and j == 0:
                            pool.wait_ge(table_loaded, 16 * pg + 16)
                        n = QK * C * pg + 2 * QK * u + QK * k + j
                        pool.wait_ge(rot_ready, n + 1)
                        pool.wait_ge(evac, OUT * C * pg + 2 * OUT * u + OUT * k + j + 5)
                        nc.gpsimd.tensor_tensor(cosp[j % 2][:], raw[j % 2][:], table[:, 0, :],
                                                ALU.mult).then_inc(cos_ready, 1)

        @block.vector
        def _(dve):
            dve.sem_inc(rot_ready, 2)
            dve.sem_inc(swap_ready, 2)
            dve.sem_inc(sin_ready, 1)
            pairs = [i ^ 1 for i in range(32)]
            with nc.vector.Fori(0, GPC) as pg, nc.vector.Fori(0, C // 2) as u:
                for k in range(2):
                    if k == 0:
                        dve.wait_ge(table_loaded, 16 * pg + 16)
                    for j in range(QK + 1):
                        n = QK * C * pg + 2 * QK * u + QK * k + j
                        if j < QK:
                            hold(dve, evac, OUT * C * pg + 2 * OUT * u + OUT * k + j + 5, pace)
                            nc.vector.stream_shuffle(swap[j % 2][:], raw[j % 2][:], pairs).then_inc(swap_ready, 1)
                            dve.wait_ge(swap_ready, n + 3)
                            nc.vector.tensor_tensor(swap[j % 2][:], swap[j % 2][:], table[:, 1, :],
                                                    ALU.mult).then_inc(sin_ready, 1)
                        if j >= 1:
                            dve.wait_ge(hi_ready, n)
                            nc.vector.tensor_tensor(hl[k][:, 1, j - 1, :], rot[(j - 1) % 2][:],
                                                    hl[k][:, 0, j - 1, :], ALU.subtract).then_inc(lo_ready, 1)
                        if j < QK:
                            dve.wait_ge(sin_ready, n + 2)
                            dve.wait_ge(cos_ready, n + 3)
                            dve.wait_ge(sq_ready, n + 1)
                            nc.vector.tensor_tensor(rot[j % 2][:], cosp[j % 2][:], swap[j % 2][:],
                                                    ALU.add).then_inc(rot_ready, 1)

        @block.scalar
        def _(act):
            act.sem_inc(evac, 4)
            act.sem_inc(sq_ready, 2)
            act.sem_inc(en_ready, 1)
            for s in (*v_stored, *en_stored, *hl_stored):
                act.sem_inc(s, 1)
            with nc.scalar.Fori(0, GPC) as pg, nc.scalar.Fori(0, C // 2) as u:
                for k in range(2):
                    act.wait_ge(hl_stored[k], 64 * pg + 32 * u + 1)
                    act.wait_ge(v_stored[k], 32 * pg + 16 * u + 1)
                    act.wait_ge(norms_ready, C * pg + 2 * u + k + 1)
                    for j in range(OUT):
                        n = QK * C * pg + 2 * QK * u + QK * k + j
                        act.wait_ge(proj_ready, OUT * C * pg + 2 * OUT * u + OUT * k + OUT + j + 2)
                        if j < QK:
                            act.wait_ge(swap_ready, n + 1)
                            act.wait_ge(cos_ready, n + 1)
                            dst = raw[j % 2][:]
                        else:
                            dst = v[k][:, j - QK, :]
                        nc.scalar.activation(dst, banks[j % 4][:], ACT.Copy, scale=1.0 / W_SCALE).then_inc(evac, 1)
                        if 1 <= j <= QK:
                            act.wait_ge(rot_ready, n + 2)
                            nc.scalar.activation(hl[k][:, 0, j - 1, :], rot[(j - 1) % 2][:],
                                                 ACT.Copy).then_inc(hi_ready, 1)
                            nc.scalar.activation(sq[k][:, j - 1, :], rot[(j - 1) % 2][:],
                                                 ACT.Square).then_inc(sq_ready, 1)
                    group = bass.ds(2 * GPC * u + pg + GPC * k, 1)
                    act.wait_ge(evac, OUT * C * pg + 2 * OUT * u + OUT * k + OUT + 4)
                    act.dma_start(io["v"][group].rearrange("o p a e -> p (o a) e"), v[k][:]).then_inc(v_stored[k], 16)
                    act.wait_ge(lo_ready, QK * C * pg + 2 * QK * u + QK * k + QK)
                    for s in range(2):
                        act.dma_start(io["qk"][group, s:s + 1].rearrange("o s (c p) n -> p (o s c) n", p=P),
                                      hl[k][:, s]).then_inc(hl_stored[k], 16)
                    act.wait_ge(norms_ready, C * pg + 2 * u + k + 3)
                    act.wait_ge(en_stored[k], 32 * pg + 16 * u + 1)
                    nc.scalar.activation(en[k][:].rearrange("p a h -> p (a h)"), norms[:, 0:A * 2 * H], ACT.Exp,
                                         scale=-0.5).then_inc(en_ready, 1)
                    act.wait_ge(en_ready, C * pg + 2 * u + k + 2)
                    act.dma_start(io["en"][group].rearrange("o p a h -> p (o a) h"), en[k][:]).then_inc(en_stored[k], 16)
            for k in range(2):
                act.wait_ge(hl_stored[k], 32 * NG // 2 + 1)
                act.wait_ge(v_stored[k], 16 * NG // 2 + 1)
                act.wait_ge(en_stored[k], 16 * NG // 2 + 1)


def sums_stage(nc, io, keep):
    with ExitStack() as ctx:
        t = Tools(nc, ctx, "s3")
        kT = [t.sb(f"kT{k}", [96, H, G], F16) for k in range(2)]
        v = t.pair("v", [P, A, E])
        en = t.pair("en", [P, A, 2 * H])
        aug = t.pair("aug", [P, A * H, D + 1])
        phi = t.pair("phi", [P, H // 2, M])
        acc = t.sb("acc", [P, 2, H // 2 * (D + 1)])
        scaled = t.sb("scaled", [P, 2, H // 2 * (D + 1)])
        logits = [t.psum(f"logits{b}", 2) for b in range(2)]
        parts = [t.psum(f"parts{b}", 2) for b in range(2)]
        k_loaded, v_loaded = ([t.sem(f"{n}{k}") for k in range(2)] for n in ("k_loaded", "v_loaded"))
        logits_ready, phi_ready, aug_ready, part_ready = (
            t.sem("logits_ready"), t.sem("phi_ready"), t.sem("aug_ready"), t.sem("part_ready"))
        cleared, added, scaled_ready, stored, pace = (
            t.sem("cleared"), t.sem("added"), t.sem("scaled_ready"), t.sem("stored"), t.sem("pace"))
        HALF = H // 2
        block = ctx.enter_context(nc.Block())

        @block.sync
        def _(sp):
            with nc.sync.Fori(0, C) as ch:
                with nc.sync.Fori(0, GPC // 2) as u:
                    for k in range(2):
                        group = bass.ds(GPC * ch + 2 * u + k, 1)
                        hold(sp, logits_ready, 32 * ch + 16 * u + 8 * k + 1, pace)
                        for r, s in enumerate((0, 0, 1)):
                            sp.dma_start(kT[k][32 * r:32 * r + 32],
                                         io["qk"][group, s, E:2 * E, :].rearrange("o (h d) n -> d (o h) n", d=D)
                                         ).then_inc(k_loaded[k], 16)
                        hold(sp, aug_ready, GPC * ch + 2 * u + k + 1, pace)
                        sp.dma_start(v[k][:], io["v"][group].rearrange("o p a e -> p (o a) e")).then_inc(v_loaded[k], 16)
                        sp.dma_start(en[k][:], io["en"][group].rearrange("o p a h -> p (o a) h")).then_inc(v_loaded[k], 16)
                hold(sp, scaled_ready, ch + 2, pace)
                sp.dma_start(io["sums"][bass.ds(ch, 1)].rearrange("o p h d -> p (o h d)"),
                             scaled[:].rearrange("p b n -> p (b n)")).then_inc(stored, 16)
            sp.wait_ge(stored, 16 * C + 1)

        @block.vector
        def _(dve):
            dve.sem_inc(aug_ready, 2)
            dve.sem_inc(added, 2)
            dve.sem_inc(scaled_ready, 1)
            with nc.vector.Fori(0, C) as ch:
                dve.wait_ge(scaled_ready, ch + 1)
                nc.vector.memset(acc[:].rearrange("p b n -> p (b n)"), 0.0).then_inc(cleared, 1)
                with nc.vector.Fori(0, GPC // 2) as u:
                    for k in range(2):
                        n = GPC * ch + 2 * u + k
                        dve.wait_ge(v_loaded[k], 64 * ch + 32 * u + 32)
                        dve.wait_ge(part_ready, 32 * ch + 16 * u + 8 * k + 2)
                        weight = en[k][:, :, H:2 * H]
                        nc.vector.tensor_tensor(aug[k][:, :, 0:D].rearrange("p (a h) d -> p a h d", a=A),
                                                v[k][:].rearrange("p a (h d) -> p a h d", d=D),
                                                weight.unsqueeze(3).broadcast_to([P, A, H, D]), ALU.mult)
                        nc.vector.tensor_copy(aug[k][:, :, D:D + 1].rearrange("p (a h) d -> p a (h d)", a=A),
                                              weight).then_inc(aug_ready, 1)
                        dve.wait_ge(cleared, ch + 1)
                        dve.wait_ge(added, n + 2)
                        dve.wait_ge(part_ready, 32 * ch + 16 * u + 8 * k + 8 + 10)
                        nc.vector.tensor_tensor(acc[:], acc[:],
                                                parts[k][:].rearrange("p (b n) -> p b n", b=2)[:, :, 0:HALF * (D + 1)],
                                                ALU.add).then_inc(added, 1)
                dve.wait_ge(added, GPC * ch + GPC + 2)
                dve.wait_ge(stored, 16 * ch + 1)
                nc.vector.tensor_scalar(scaled[:].rearrange("p b n -> p (b n)"), acc[:].rearrange("p b n -> p (b n)"),
                                        1.0 / M, None, ALU.mult).then_inc(scaled_ready, 1)

        @block.scalar
        def _(act):
            act.sem_inc(phi_ready, 2)
            with nc.scalar.Fori(0, C) as ch, nc.scalar.Fori(0, GPC // 2) as u:
                for k in range(2):
                    for i in range(2 * A):
                        n = 32 * ch + 16 * u + 8 * k + i
                        act.wait_ge(logits_ready, n + 10)
                        act.wait_ge(part_ready, n + 9)
                        nc.scalar.activation(phi[i % 2][:].rearrange("p h m -> p (h m)"), logits[i % 2][:], ACT.Exp,
                                             scale=1.0 / M_SCALE).then_inc(phi_ready, 1)

        @block.tensor
        def _(pe):
            pe.sem_inc(logits_ready, 9)
            pe.sem_inc(part_ready, 10)
            pe.sem_inc(stored, 1)

            def make_logits(n, k, i):
                a, half = i // 2, i % 2
                pe.wait_ge(phi_ready, n + i + 1)
                for h in range(HALF):
                    mm = nc.tensor.matmul(logits[i % 2][:, h * M:(h + 1) * M],
                                          kT[k][:, HALF * half + h, a * P:(a + 1) * P],
                                          keep["feat"][:, HALF * half + h, :], start=True, stop=True)
                mm.then_inc(logits_ready, 1)

            with nc.tensor.Fori(0, C) as ch, nc.tensor.Fori(0, GPC // 2) as u:
                for k in range(2):
                    n = 32 * ch + 16 * u + 8 * k
                    pe.wait_ge(k_loaded[k], 96 * ch + 48 * u + 48)
                    make_logits(n, k, 0)
                    for i in range(2 * A):
                        a, half = i // 2, i % 2
                        if i + 1 < 2 * A:
                            make_logits(n, k, i + 1)
                        if i == 0:
                            pe.wait_ge(aug_ready, GPC * ch + 2 * u + k + 3)
                            pe.wait_ge(added, GPC * ch + 2 * u + k + 1)
                        pe.wait_ge(phi_ready, n + i + 3)
                        for h in range(HALF):
                            mm = nc.tensor.matmul(
                                parts[k][:, 512 * half + h * (D + 1):512 * half + (h + 1) * (D + 1)],
                                phi[i % 2][:, h, :], aug[k][:, a * H + HALF * half + h, :],
                                start=(a == 0 and h == 0), stop=(a == A - 1), skip_group_check=True)
                        mm.then_inc(part_ready, 1)


def attend_stage(nc, io, keep):
    with ExitStack() as ctx:
        t = Tools(nc, ctx, "s4")
        qT = [t.sb(f"qT{k}", [96, H, G], F16) for k in range(2)]
        sums = t.pair("sums", [P, H, D + 1])
        en = t.pair("en", [P, A, 2 * H])
        x = t.pair("x", [P, A, E])
        phi = t.pair("phi", [P, H // 2, P])
        den = t.sb("den", [P, H])
        ratio = t.sb("ratio", [P, H])
        at = t.sb("at", [P, E])
        atT = t.sb("atT", [P, EC, P])
        z = t.pair("z", [P, E])
        stats, mv, rstd, power = t.sb("stats", [P, 6]), t.sb("mv", [P, 2]), t.sb("rstd", [P, 1]), t.sb("power", [P, 1])
        logits = [t.psum(f"logits{b}", 2) for b in range(2)]
        numer = t.psum("numer", 2)
        turned = t.psum("turned")
        y = t.psum("y")
        q_loaded, s_loaded, x_stored = ([t.sem(f"{n}{k}") for k in range(2)] for n in ("q_loaded", "s_loaded", "x_stored"))
        logits_ready, phi_ready, numer_ready, den_ready, at_ready = (
            t.sem("logits_ready"), t.sem("phi_ready"), t.sem("numer_ready"), t.sem("den_ready"), t.sem("at_ready"))
        turned_ready, atT_ready, y_ready, stats_ready, mv_ready = (
            t.sem("turned_ready"), t.sem("atT_ready"), t.sem("y_ready"), t.sem("stats_ready"), t.sem("mv_ready"))
        rstd_ready, z_ready, x1_ready, power_ready, pace = (
            t.sem("rstd_ready"), t.sem("z_ready"), t.sem("x1_ready"), t.sem("power_ready"), t.sem("pace"))
        var_ready = t.sem("var_ready")
        HALF = H // 2
        block = ctx.enter_context(nc.Block())

        @block.sync
        def _(sp):
            with nc.sync.Fori(0, C) as ch, nc.sync.Fori(0, GPC // 2) as u:
                for k in range(2):
                    group = bass.ds(GPC * ch + 2 * u + k, 1)
                    hold(sp, logits_ready, 32 * ch + 16 * u + 8 * k + 1, pace)
                    for r, s in enumerate((0, 0, 1)):
                        sp.dma_start(qT[k][32 * r:32 * r + 32],
                                     io["qk"][group, s, 0:E, :].rearrange("o (h d) n -> d (o h) n", d=D)
                                     ).then_inc(q_loaded[k], 16)
                    hold(sp, x_stored[k], 32 * ch + 16 * u + 1, pace)
                    sp.dma_start(sums[k][:], io["sums"][bass.ds(ch, 1)].rearrange("o p h d -> p (o h) d")
                                 ).then_inc(s_loaded[k], 16)
                    sp.dma_start(en[k][:], io["en"][group].rearrange("o p a h -> p (o a) h")).then_inc(s_loaded[k], 16)
                    sp.dma_start(x[k][:], io["x"][bass.ds((GPC * ch + 2 * u + k) * G, G), :]
                                 .rearrange("(a p) e -> p a e", p=P)).then_inc(s_loaded[k], 16)

        @block.tensor
        def _(pe):
            pe.sem_inc(logits_ready, 9)
            pe.sem_inc(numer_ready, 2)
            pe.sem_inc(turned_ready, 1)
            pe.sem_inc(y_ready, 1)

            def project(n, a):
                pe.wait_ge(at_ready, n + a + 2)
                pe.wait_ge(atT_ready, n + a + 1)
                for c in range(EC):
                    mm = nc.tensor.transpose(turned[:, c * P:(c + 1) * P], at[:, c * P:(c + 1) * P], keep["ident32"][:])
                mm.then_inc(turned_ready, 1)
                pe.wait_ge(atT_ready, n + a + 2)
                pe.wait_ge(z_ready, n + a + 2)
                for c in range(EC):
                    mm = nc.tensor.matmul(y[:], atT[:, c, :], keep["wo"][:, c, :], start=(c == 0), stop=(c == EC - 1))
                mm.then_inc(y_ready, 1)

            with nc.tensor.Fori(0, C) as ch, nc.tensor.Fori(0, GPC // 2) as u:
                for k in range(2):
                    i0 = 32 * ch + 16 * u + 8 * k
                    n = 16 * ch + 8 * u + 4 * k
                    pe.wait_ge(q_loaded[k], 96 * ch + 48 * u + 48)
                    for a in range(A):
                        for half in range(2):
                            pe.wait_ge(phi_ready, i0 + 2 * a + half + 1)
                            for h in range(HALF):
                                mm = nc.tensor.matmul(logits[half][:, h * P:(h + 1) * P],
                                                      keep["feat"][:, HALF * half + h, :],
                                                      qT[k][:, HALF * half + h, a * P:(a + 1) * P],
                                                      start=True, stop=True)
                            mm.then_inc(logits_ready, 1)
                        if a:
                            project(n, a - 1)
                        else:
                            pe.wait_ge(s_loaded[k], 96 * ch + 48 * u + 48)
                        pe.wait_ge(at_ready, n + a + 1)
                        for half in range(2):
                            pe.wait_ge(phi_ready, i0 + 2 * a + half + 3)
                            for h in range(HALF):
                                mm = nc.tensor.matmul(numer[:, 512 * half + h * (D + 1):512 * half + (h + 1) * (D + 1)],
                                                      phi[half][:, h, :], sums[k][:, HALF * half + h, :],
                                                      start=True, stop=True)
                            mm.then_inc(numer_ready, 1)
                    project(n, A - 1)

        @block.scalar
        def _(act):
            act.sem_inc(phi_ready, 2)
            act.sem_inc(atT_ready, 1)
            for k in range(2):
                act.sem_inc(x_stored[k], 1)

            def copy_turned(n, a):
                act.wait_ge(turned_ready, n + a + 2)
                act.wait_ge(y_ready, n + a + 1)
                nc.scalar.activation(atT[:].rearrange("p c q -> p (c q)"), turned[:], ACT.Copy).then_inc(atT_ready, 1)

            with nc.scalar.Fori(0, C) as ch, nc.scalar.Fori(0, GPC // 2) as u:
                for k in range(2):
                    i0 = 32 * ch + 16 * u + 8 * k
                    n = 16 * ch + 8 * u + 4 * k
                    for a in range(A):
                        for half in range(2):
                            act.wait_ge(logits_ready, i0 + 2 * a + half + 10)
                            act.wait_ge(numer_ready, i0 + 2 * a + half + 1)
                            nc.scalar.activation(phi[half][:].rearrange("p h m -> p (h m)"), logits[half][:], ACT.Exp,
                                                 scale=1.0 / M_SCALE).then_inc(phi_ready, 1)
                        if a:
                            copy_turned(n, a - 1)
                    copy_turned(n, A - 1)
                    act.wait_ge(x1_ready, n + A + 2)
                    act.dma_start(io["x1"][bass.ds((GPC * ch + 2 * u + k) * G, G), :].rearrange("(a p) e -> p a e", p=P),
                                  x[k][:]).then_inc(x_stored[k], 16)
            for k in range(2):
                act.wait_ge(x_stored[k], 16 * NG // 2 + 1)

        @block.vector
        def _(dve):
            dve.sem_inc(at_ready, 1)
            dve.sem_inc(z_ready, 2)
            dve.sem_inc(den_ready, 1)

            def normalize(n, a):
                hold(dve, y_ready, n + a + 2, pace)
                nc.vector.bn_stats(stats[:], y[:]).then_inc(stats_ready, 1)
                hold(dve, stats_ready, n + a + 1, pace)
                nc.vector.bn_aggr(mv[:], stats[:]).then_inc(mv_ready, 1)
                dve.wait_ge(rstd_ready, n + a + 1)
                dve.wait_ge(x1_ready, n + a + 1)
                nc.vector.tensor_scalar(z[a % 2][:], y[:], mv[:, 0:1], rstd[:], ALU.subtract,
                                        ALU.mult).then_inc(z_ready, 1)

            with nc.vector.Fori(0, C) as ch, nc.vector.Fori(0, GPC // 2) as u:
                for k in range(2):
                    i0 = 32 * ch + 16 * u + 8 * k
                    n = 16 * ch + 8 * u + 4 * k
                    dve.wait_ge(s_loaded[k], 96 * ch + 48 * u + 48)
                    for a in range(A):
                        if a:
                            normalize(n, a - 1)
                        d0 = 4 * n + 4 * a + 1
                        heads = numer[:].rearrange("p (b n) -> p b n", b=2)[:, :, 0:HALF * (D + 1)].rearrange(
                            "p b (h d) -> p b h d", d=D + 1)
                        weight = en[k][:, a, 0:H]
                        dve.wait_ge(numer_ready, i0 + 2 * a + 4)
                        nc.vector.tensor_tensor(den[:].rearrange("p (b h o) -> p b h o", b=2, o=1),
                                                heads[:, :, :, D:D + 1],
                                                weight.rearrange("p (b h o) -> p b h o", b=2, o=1),
                                                ALU.mult).then_inc(den_ready, 1)
                        dve.wait_ge(den_ready, d0 + 1)
                        nc.vector.tensor_scalar(den[:], den[:], 1e-6, None, ALU.max).then_inc(den_ready, 1)
                        dve.wait_ge(den_ready, d0 + 2)
                        nc.vector.reciprocal(den[:], den[:]).then_inc(den_ready, 1)
                        dve.wait_ge(den_ready, d0 + 3)
                        nc.vector.tensor_tensor(ratio[:], den[:], weight, ALU.mult).then_inc(den_ready, 1)
                        dve.wait_ge(den_ready, d0 + 4)
                        dve.wait_ge(turned_ready, n + a + 1)
                        nc.vector.tensor_tensor(at[:].rearrange("p (b h d) -> p b h d", b=2, d=D), heads[:, :, :, 0:D],
                                                ratio[:].rearrange("p (b h) -> p b h", b=2).unsqueeze(3)
                                                .broadcast_to([P, 2, HALF, D]), ALU.mult).then_inc(at_ready, 1)
                    normalize(n, A - 1)

        @block.gpsimd
        def _(pool):
            nc.gpsimd.memset(power[:], -0.5).then_inc(power_ready, 1)
            pool.wait_ge(power_ready, 1)
            pool.sem_inc(x1_ready, 2)
            with nc.gpsimd.Fori(0, C) as ch, nc.gpsimd.Fori(0, GPC // 2) as u:
                for k in range(2):
                    n = 16 * ch + 8 * u + 4 * k
                    for a in range(A):
                        hold(pool, mv_ready, n + a + 1, pace)
                        nc.gpsimd.tensor_scalar(rstd[:], mv[:, 1:2], 1e-5, None, ALU.add).then_inc(var_ready, 1)
                        pool.wait_ge(var_ready, n + a + 1)
                        nc.gpsimd.tensor_tensor(rstd[:], rstd[:], power[:], ALU.pow).then_inc(rstd_ready, 1)
                        pool.wait_ge(z_ready, n + a + 3)
                        pool.wait_ge(s_loaded[k], 96 * ch + 48 * u + 48)
                        nc.gpsimd.tensor_tensor(x[k][:, a, :], x[k][:, a, :], z[a % 2][:], ALU.add).then_inc(x1_ready, 1)


def route_stage(nc, io, keep):
    with ExitStack() as ctx:
        t = Tools(nc, ctx, "s6")
        xT = t.pair("xT", [P, 2, EC, G], F16)
        token = t.pair("token", [P, A], U32)
        slots = t.pair("slots", [P, A * K], U32)
        weights = t.pair("weights", [P, A, K])
        score, biased = t.sb("score", [P, A, NE]), t.sb("biased", [P, A, NE])
        top, index, chosen = t.sb("top", [P, A, 8]), t.sb("index", [P, A, 8], U32), t.sb("chosen", [P, A, K])
        onehot, picked = t.sb("onehot", [P, A, K, NE]), t.sb("picked", [P, A, K, NE])
        mask = t.sb("mask", [P, A, NE], F16)
        before, ours = t.sb("before", [P, NE], F16), t.sb("ours", [P, NE])
        slot, far, place = t.sb("slot", [P, A, NE]), t.sb("far", [P, A, NE]), t.sb("place", [P, A, K])
        w, total = t.sb("w", [P, A, K]), t.sb("total", [P, A])
        logits = [t.psum(f"logits{k}") for k in range(2)]
        position = t.psum("position")
        x_loaded, token_loaded, scattered, slots_stored, weights_stored = (
            [t.sem(f"{n}{k}") for k in range(2)]
            for n in ("x_loaded", "token_loaded", "scattered", "slots_stored", "weights_stored"))
        logits_ready, score_ready, position_ready, mask_ready, step, slots_ready, sent, pace = (
            t.sem(n) for n in ("logits_ready", "score_ready", "position_ready", "mask_ready", "step", "slots_ready",
                               "sent", "pace"))
        STEPS = 19
        block = ctx.enter_context(nc.Block())

        @block.sync
        def _(sp):
            with nc.sync.Fori(0, NG // 2) as u:
                for k in range(2):
                    hold(sp, logits_ready, 2 * u + k + 1, pace)
                    sp.dma_start(xT[k][:].rearrange("p s c q -> p (s c q)"),
                                 io["xT2"][bass.ds(2 * u + k, 1)].rearrange("o p n -> p (o n)")).then_inc(x_loaded[k], 16)
                    hold(sp, sent, 2 * u + k + 1, pace)
                    sp.dma_start(token[k][:], io["token"][bass.ds(2 * u + k, 1)].rearrange("o p a -> p (o a)")
                                 ).then_inc(token_loaded[k], 16)

        @block.tensor
        def _(pe):
            pe.sem_inc(logits_ready, 2)
            with nc.tensor.Fori(0, NG // 2) as u:
                for k in range(2):
                    pe.wait_ge(x_loaded[k], 16 * u + 16)
                    pe.wait_ge(score_ready, 2 * u + k + 1)
                    for a in range(A):
                        for c in range(EC):
                            for s in range(2):
                                mm = nc.tensor.matmul(logits[k][:, a * NE:(a + 1) * NE],
                                                      xT[k][:, s, c, a * P:(a + 1) * P],
                                                      keep["gate"][:, c * NE:(c + 1) * NE],
                                                      start=(c == 0 and s == 0), stop=(c == EC - 1 and s == 1))
                    mm.then_inc(logits_ready, 1)
                    pe.wait_ge(mask_ready, 2 * u + k + 2)
                    for a in range(A):
                        out = position[:, a * NE:(a + 1) * NE]
                        nc.tensor.matmul(out, keep["tri"][:], mask[:, a, :], start=True, stop=False)
                        for b in range(a):
                            nc.tensor.matmul(out, keep["ones"][:], mask[:, b, :], start=False, stop=False)
                        mm = nc.tensor.matmul(out, keep["ones"][:], before[:], start=False, stop=True)
                    mm.then_inc(position_ready, 1)

        @block.scalar
        def _(act):
            act.sem_inc(score_ready, 2)
            for k in range(2):
                act.sem_inc(slots_stored[k], 1)
                act.sem_inc(weights_stored[k], 1)
            with nc.scalar.Fori(0, NG // 2) as u:
                for k in range(2):
                    act.wait_ge(logits_ready, 2 * u + k + 3)
                    act.wait_ge(slots_ready, 2 * u + k + 1)
                    nc.scalar.activation(score[:].rearrange("p a e -> p (a e)"), logits[k][:, 0:A * NE],
                                         ACT.Sigmoid).then_inc(score_ready, 1)
                    act.wait_ge(slots_ready, 2 * u + k + 2)
                    act.dma_start(io["slots"][bass.ds(2 * u + k, 1)].rearrange("o p n -> p (o n)"),
                                  slots[k][:]).then_inc(slots_stored[k], 16)
                    act.dma_start(io["weights"][bass.ds(2 * u + k, 1)].rearrange("o p n -> p (o n)"),
                                  weights[k][:].rearrange("p a j -> p (a j)")).then_inc(weights_stored[k], 16)
            for k in range(2):
                act.wait_ge(slots_stored[k], 16 * NG // 2 + 1)
                act.wait_ge(weights_stored[k], 16 * NG // 2 + 1)

        @block.vector
        def _(dve):
            nc.vector.memset(before[:], 0.0).then_inc(mask_ready, 1)
            dve.wait_ge(mask_ready, 1)
            dve.sem_inc(slots_ready, 1)
            dve.sem_inc(step, 1)
            number = keep["expert"][:, 0:NE].unsqueeze(1).unsqueeze(1).broadcast_to([P, A, K, NE])
            first = keep["expert"][:, NE:2 * NE].unsqueeze(1).broadcast_to([P, A, NE])
            bias = keep["bias"][:].unsqueeze(1).broadcast_to([P, A, NE])

            def per_choice(x):
                return x.unsqueeze(2).broadcast_to([P, A, K, NE])

            with nc.vector.Fori(0, NG // 2) as u:
                for k in range(2):
                    done = [2 * STEPS * u + STEPS * k + 1]

                    def then(ins):
                        ins.then_inc(step, 1)
                        done[0] = done[0] + 1
                        hold(dve, step, done[0], pace)

                    dve.wait_ge(score_ready, 2 * u + k + 3)
                    then(nc.vector.tensor_tensor(biased[:], score[:], bias, ALU.add))
                    for a in range(A):
                        ins = nc.vector.max(top[:, a, :], biased[:, a, :])
                    then(ins)
                    for a in range(A):
                        ins = nc.vector.max_index(index[:, a, :], top[:, a, :], biased[:, a, :])
                    then(ins)
                    then(nc.vector.tensor_copy(chosen[:], index[:, :, 0:K]))
                    then(nc.vector.tensor_tensor(onehot[:], number, chosen[:].unsqueeze(3).broadcast_to([P, A, K, NE]),
                                                 ALU.is_equal))
                    with nc.allow_low_precision(reason="sums of zeros and one 1"):
                        ins = nc.vector.tensor_reduce(mask[:], onehot[:].rearrange("p a j e -> p a e j"), AX.X, ALU.add)
                    ins.then_inc(mask_ready, 1)
                    then(nc.vector.tensor_tensor(picked[:], onehot[:], per_choice(score[:]), ALU.mult))
                    then(nc.vector.tensor_reduce(w[:], picked[:], AX.X, ALU.add))
                    then(nc.vector.tensor_reduce(total[:], w[:], AX.X, ALU.add))
                    then(nc.vector.tensor_scalar(total[:], total[:], 1e-12, None, ALU.max))
                    then(nc.vector.reciprocal(total[:], total[:]))
                    then(nc.vector.tensor_tensor(w[:], w[:], total[:].unsqueeze(2).broadcast_to([P, A, K]), ALU.mult))
                    dve.wait_ge(position_ready, 2 * u + k + 1)
                    then(nc.vector.tensor_reduce(ours[:], mask[:].rearrange("p a e -> p e a"), AX.X, ALU.add))
                    then(nc.vector.tensor_tensor(before[:], before[:], ours[:], ALU.add))
                    where = position[:, 0:A * NE].rearrange("p (a e) -> p a e", e=NE)
                    then(nc.vector.tensor_scalar(far[:], where, float(CAP), NOWHERE, ALU.is_ge, ALU.mult))
                    then(nc.vector.tensor_tensor(slot[:], where, first, ALU.add))
                    then(nc.vector.tensor_tensor(slot[:], slot[:], far[:], ALU.add))
                    then(nc.vector.tensor_tensor(picked[:], onehot[:], per_choice(slot[:]), ALU.mult))
                    then(nc.vector.tensor_reduce(place[:], picked[:], AX.X, ALU.add))
                    dve.wait_ge(weights_stored[k], 16 * u + 1)
                    then(nc.vector.scalar_tensor_tensor(out=weights[k][:], in0=place[:], scalar=NOWHERE / 2, in1=w[:],
                                                        op0=ALU.is_lt, op1=ALU.mult))
                    dve.wait_ge(slots_stored[k], 16 * u + 1)
                    dve.wait_ge(sent, 2 * u + k + 1)
                    ins = nc.vector.tensor_copy(slots[k][:], place[:].rearrange("p a j -> p (a j)"))
                    ins.then_inc(slots_ready, 1)
                    dve.wait_ge(slots_ready, 2 * u + k + 2)

        @block.gpsimd
        def _(pool):
            pool.sem_inc(sent, 2)
            with nc.gpsimd.Fori(0, NG // 2) as u:
                for k in range(2):
                    hold(pool, token_loaded[k], 16 * u + 16, pace)
                    hold(pool, slots_ready, 2 * u + k + 2, pace)
                    for a in range(A):
                        for j in range(K):
                            nc.gpsimd.indirect_dma_start(
                                out=io["slot_token"],
                                out_offset=bass.IndirectOffsetOnAxis(ap=slots[k][:, a * K + j:a * K + j + 1], axis=0),
                                in_=token[k][:, a:a + 1], in_offset=None, bounds_check=NSLOT - 1, oob_is_err=False,
                            ).then_inc(scattered[k], 16)
                    hold(pool, scattered[k], 16 * A * K * (u + 1), pace)
                    pool.sem_inc(sent, 1)


def expert_stage(nc, io, keep, shared):
    with ExitStack() as ctx:
        t = Tools(nc, ctx, "s8" if shared else "s7")
        N = NG if shared else NE
        IC = I // P
        w1, w3 = (t.pair(n, [P, EC, I], BF16) for n in ("w1", "w3"))
        w2 = t.pair("w2", [P, IC, E], BF16)
        token = t.pair("token", [P, A], U32)
        rows = t.pair("rows", [P, A, 2 * E], F16)
        xT = t.pair("xT", [P, 2, EC, G], F16)
        gate, h = t.pair("gate", [P, G]), t.pair("h", [P, G])
        parts = t.pair("parts", [P, IC, 3, G], BF16)
        y = t.pair("y", [P, A, E])
        turned = [t.psum(f"turned{b}") for b in range(2)]
        gates = [t.psum(f"gates{b}") for b in range(2)]
        ups = [t.psum(f"ups{b}") for b in range(2)]
        ys = [t.psum(f"ys{b}") for b in range(2)]
        w_loaded, token_loaded, gathered, x_loaded, stored = (
            [t.sem(f"{n}{k}") for k in range(2)] for n in ("w_loaded", "token_loaded", "gathered", "x_loaded", "stored"))
        gather_sent = t.sem("gather_sent")
        turned_ready, xT_ready, up_ready, gate_ready, h_ready, split, mid_ready, low_ready = (
            t.sem(n) for n in ("turned_ready", "xT_ready", "up_ready", "gate_ready", "h_ready", "split", "mid_ready",
                               "low_ready"))
        rest_ready, y_ready, y_copied, pace = t.sem("rest_ready"), t.sem("y_ready"), t.sem("y_copied"), t.sem("pace")
        if shared:
            dst = io["ysh"].rearrange("(n a p) e -> n p a e", a=A, p=P)
        else:
            dst = io["ye"].rearrange("(n p a) e -> n p a e", a=A, p=P)
            ids = io["slot_token"].rearrange("(n p a) o -> n p (a o)", p=P, a=A)
        block = ctx.enter_context(nc.Block())

        def load_weights(sp, k, W1, W3, W2):
            sp.dma_start(w1[k][:], W1.rearrange("(c p) i -> p c i", p=P)).then_inc(w_loaded[k], 16)
            sp.dma_start(w3[k][:], W3.rearrange("(c p) i -> p c i", p=P)).then_inc(w_loaded[k], 16)
            sp.dma_start(w2[k][:], W2.rearrange("(c p) e -> p c e", p=P)).then_inc(w_loaded[k], 16)

        @block.sync
        def _(sp):
            if shared:
                load_weights(sp, 0, io["sw1"], io["sw3"], io["sw2"])
            with nc.sync.Fori(0, N // 2) as u:
                for k in range(2):
                    hold(sp, y_ready, 8 * u + 4 * k + 1, pace)
                    if shared:
                        sp.dma_start(xT[k][:].rearrange("p s c q -> p (s c q)"),
                                     io["xT2"][bass.ds(2 * u + k, 1)].rearrange("o p n -> p (o n)")
                                     ).then_inc(x_loaded[k], 16)
                    else:
                        e = bass.ds(2 * u + k, 1)
                        sp.dma_start(token[k][:], ids[e].rearrange("o p a -> p (o a)")).then_inc(token_loaded[k], 16)
                        load_weights(sp, k, *(io[n][e].rearrange("o d i -> (o d) i") for n in ("W1", "W3", "W2")))

        @block.gpsimd
        def _(pool):
            if not shared:
                with nc.gpsimd.Fori(0, N // 2) as u:
                    for k in range(2):
                        hold(pool, token_loaded[k], 16 * u + 16, pace)
                        hold(pool, turned_ready, 8 * u + 4 * k + 1, pace)
                        for a in range(A):
                            nc.gpsimd.indirect_dma_start(
                                out=rows[k][:, a, :], out_offset=None, in_=io["rows"],
                                in_offset=bass.IndirectOffsetOnAxis(ap=token[k][:, a:a + 1], axis=0),
                                bounds_check=T - 1, oob_is_err=False).then_inc(gathered[k], 16)

        @block.tensor
        def _(pe):
            pe.sem_inc(turned_ready, 5)
            pe.sem_inc(up_ready, 3)
            pe.sem_inc(y_ready, 5)
            with nc.tensor.Fori(0, N // 2) as u:
                for k in range(2):
                    if shared:
                        pe.wait_ge(x_loaded[k], 16 * u + 16)
                    else:
                        pe.wait_ge(gathered[k], 16 * A * u + 16 * A)
                        for a in range(A):
                            pe.wait_ge(xT_ready, 8 * u + 4 * k + a + 1)
                            for s in range(2):
                                for c in range(EC):
                                    mm = nc.tensor.transpose(
                                        turned[a % 2][:].bitcast(F16)[:, (s * EC + c) * P:(s * EC + c + 1) * P],
                                        rows[k][:, a, (s * EC + c) * P:(s * EC + c + 1) * P], keep["ident16"][:])
                            mm.then_inc(turned_ready, 1)
                        pe.wait_ge(xT_ready, 8 * u + 4 * k + 4 + 2)
                    if shared:
                        pe.wait_ge(w_loaded[0], 48)
                    else:
                        pe.wait_ge(w_loaded[k], 48 * u + 48)
                    wk = 0 if shared else k
                    for i in range(IC):
                        pe.wait_ge(h_ready, 4 * u + 2 * k + i + 1)
                        for bank, w in ((gates[i], w1[wk]), (ups[i], w3[wk])):
                            for c in range(EC):
                                for s in range(2):
                                    mm = nc.tensor.matmul(bank[:], w[:, c, i * P:(i + 1) * P], xT[k][:, s, c, :],
                                                          start=(c == 0 and s == 0), stop=(c == EC - 1 and s == 1))
                        mm.then_inc(up_ready, 1)
                    pe.wait_ge(low_ready, 4 * u + 2 * k + 2)
                    for a in range(A):
                        pe.wait_ge(y_copied, 8 * u + 4 * k + a + 1)
                        for i in range(IC):
                            for s in range(3):
                                mm = nc.tensor.matmul(ys[a % 2][:], parts[k][:, i, s, a * P:(a + 1) * P], w2[wk][:, i, :],
                                                      start=(i == 0 and s == 0), stop=(i == IC - 1 and s == 2))
                        mm.then_inc(y_ready, 1)

        @block.scalar
        def _(act):
            act.sem_inc(xT_ready, 2)
            act.sem_inc(y_copied, 2)
            for k in range(2):
                act.sem_inc(stored[k], 1)
            with nc.scalar.Fori(0, N // 2) as u:
                for k in range(2):
                    if not shared:
                        for a in range(A):
                            act.wait_ge(turned_ready, 8 * u + 4 * k + a + 6)
                            if a == 0:
                                act.wait_ge(up_ready, 4 * u + 2 * k + 1)
                            nc.scalar.activation(
                                xT[k][:, :, :, a * P:(a + 1) * P],
                                turned[a % 2][:].bitcast(F16).rearrange("p (s c q) -> p s c q", s=2, c=EC),
                                ACT.Copy).then_inc(xT_ready, 1)
                    for i in range(IC):
                        n = 4 * u + 2 * k + i
                        act.wait_ge(up_ready, n + 4)
                        act.wait_ge(h_ready, n + 1)
                        nc.scalar.activation(gate[i][:], gates[i][:], ACT.Silu).then_inc(gate_ready, 1)
                        if i == 0:
                            act.wait_ge(y_ready, 8 * u + 4 * k + 1)
                        act.wait_ge(h_ready, n + 3)
                        nc.scalar.activation(parts[k][:, i, 0, :], h[i][:], ACT.Copy).then_inc(split, 1)
                        act.wait_ge(rest_ready, n + 1)
                        nc.scalar.activation(parts[k][:, i, 1, :], h[i][:], ACT.Copy).then_inc(mid_ready, 1)
                    act.wait_ge(stored[k], 16 * u + 1)
                    for a in range(A):
                        act.wait_ge(y_ready, 8 * u + 4 * k + a + 6)
                        nc.scalar.activation(y[k][:, a, :], ys[a % 2][:], ACT.Copy).then_inc(y_copied, 1)
                    act.wait_ge(y_copied, 8 * u + 4 * k + 4 + 2)
                    act.dma_start(dst[bass.ds(2 * u + k, 1)].rearrange("o p a e -> p (o a) e"),
                                  y[k][:]).then_inc(stored[k], 16)
            for k in range(2):
                act.wait_ge(stored[k], 16 * N // 2 + 1)

        @block.vector
        def _(dve):
            dve.sem_inc(h_ready, 2)
            with nc.vector.Fori(0, N // 2) as u:
                for k in range(2):
                    for i in range(IC):
                        n = 4 * u + 2 * k + i
                        dve.wait_ge(gate_ready, n + 1)
                        nc.vector.tensor_tensor(h[i][:], gate[i][:], ups[i][:], ALU.mult).then_inc(h_ready, 1)
                        dve.wait_ge(split, n + 1)
                        nc.vector.tensor_tensor(h[i][:], h[i][:], parts[k][:, i, 0, :], ALU.subtract).then_inc(rest_ready, 1)
                        dve.wait_ge(mid_ready, n + 1)
                        nc.vector.tensor_tensor(parts[k][:, i, 2, :], h[i][:], parts[k][:, i, 1, :],
                                                ALU.subtract).then_inc(low_ready, 1)


def combine_stage(nc, io, keep):
    with ExitStack() as ctx:
        t = Tools(nc, ctx, "s9")
        slots = t.pair("slots", [P, A * K], U32)
        weights = t.pair("weights", [P, A * K])
        ysh = t.pair("ysh", [P, A, E])
        x1 = t.pair("x1", [P, A, E])
        picked = [t.sb(f"picked{b}", [P, K, E]) for b in range(2)]
        stats, mv = t.sb("stats", [P, A, 6]), t.sb("mv", [P, A, 2])
        var, root, rstd, fix = (t.sb(n, [P, A]) for n in ("var", "root", "rstd", "fix"))
        s_loaded, loaded, gathered, out_stored = (
            [t.sem(f"{n}{k}") for k in range(2)] for n in ("s_loaded", "loaded", "gathered", "out_stored"))
        cleared, summed, stats_ready, step, var_ready, root_ready, z_ready, out_ready, pace = (
            t.sem(n) for n in ("cleared", "summed", "stats_ready", "step", "var_ready", "root_ready", "z_ready",
                               "out_ready", "pace"))
        STEPS = 6
        block = ctx.enter_context(nc.Block())

        @block.sync
        def _(sp):
            with nc.sync.Fori(0, NG // 2) as u:
                for k in range(2):
                    g = bass.ds(2 * u + k, 1)
                    rows = bass.ds((2 * u + k) * G, G)
                    hold(sp, out_stored[k], 16 * u + 1, pace)
                    sp.dma_start(slots[k][:], io["slots"][g].rearrange("o p n -> p (o n)")).then_inc(s_loaded[k], 16)
                    sp.dma_start(weights[k][:], io["weights"][g].rearrange("o p n -> p (o n)")).then_inc(loaded[k], 16)
                    sp.dma_start(ysh[k][:], io["ysh"][rows, :].rearrange("(a p) e -> p a e", p=P)).then_inc(loaded[k], 16)
                    sp.dma_start(x1[k][:], io["x1"][rows, :].rearrange("(a p) e -> p a e", p=P)).then_inc(loaded[k], 16)

        @block.gpsimd
        def _(pool):
            pool.wait_ge(cleared, 2)
            with nc.gpsimd.Fori(0, NG // 2) as u:
                for k in range(2):
                    hold(pool, s_loaded[k], 16 * u + 16, pace)
                    for a in range(A):
                        hold(pool, summed, (2 * u + k) * A * K + a * K + 1, pace)
                        for j in range(K):
                            nc.gpsimd.indirect_dma_start(
                                out=picked[a % 2][:, j, :], out_offset=None, in_=io["ye"],
                                in_offset=bass.IndirectOffsetOnAxis(ap=slots[k][:, a * K + j:a * K + j + 1], axis=0),
                                bounds_check=NSLOT - 1, oob_is_err=False).then_inc(gathered[a % 2], 16)

        @block.vector
        def _(dve):
            for b in range(2):
                nc.vector.memset(picked[b][:].rearrange("p j e -> p (j e)"), 0.0).then_inc(cleared, 1)
            dve.wait_ge(cleared, 2)
            dve.sem_inc(summed, K + 1)
            with nc.vector.Fori(0, NG // 2) as u:
                for k in range(2):
                    dve.wait_ge(loaded[k], 48 * u + 48)
                    for a in range(A):
                        n = (2 * u + k) * A + a
                        dve.wait_ge(gathered[a % 2], (2 * u + k) * (A // 2) * K * 16 + (a // 2 + 1) * K * 16)
                        for j in range(K):
                            nc.vector.scalar_tensor_tensor(out=ysh[k][:, a, :], in0=picked[a % 2][:, j, :],
                                                           scalar=weights[k][:, a * K + j:a * K + j + 1],
                                                           in1=ysh[k][:, a, :], op0=ALU.mult,
                                                           op1=ALU.add).then_inc(summed, 1)
                            hold(dve, summed, n * K + j + 1 + K + 1, pace)
                        ins = nc.vector.bn_stats(stats[:, a, :], ysh[k][:, a, :])
                    ins.then_inc(stats_ready, 1)
                    g = 2 * u + k
                    hold(dve, stats_ready, g + 1, pace)
                    for a in range(A):
                        ins = nc.vector.bn_aggr(mv[:, a, :], stats[:, a, :])
                    ins.then_inc(step, 1)
                    dve.wait_ge(step, STEPS * g + 1)
                    nc.vector.tensor_scalar(var[:], mv[:, :, 1], 1e-5, None, ALU.add).then_inc(var_ready, 1)
                    dve.wait_ge(root_ready, g + 1)
                    nc.vector.reciprocal(rstd[:], root[:]).then_inc(step, 1)
                    dve.wait_ge(step, STEPS * g + 2)
                    nc.vector.tensor_tensor(fix[:], rstd[:], rstd[:], ALU.mult).then_inc(step, 1)
                    dve.wait_ge(step, STEPS * g + 3)
                    nc.vector.tensor_tensor(fix[:], fix[:], var[:], ALU.mult).then_inc(step, 1)
                    dve.wait_ge(step, STEPS * g + 4)
                    nc.vector.tensor_scalar(fix[:], fix[:], -0.5, 1.5, ALU.mult, ALU.add).then_inc(step, 1)
                    dve.wait_ge(step, STEPS * g + 5)
                    nc.vector.tensor_tensor(rstd[:], rstd[:], fix[:], ALU.mult).then_inc(step, 1)
                    dve.wait_ge(step, STEPS * g + 6)
                    for a in range(A):
                        ins = nc.vector.tensor_scalar(ysh[k][:, a, :], ysh[k][:, a, :], mv[:, a, 0:1], rstd[:, a:a + 1],
                                                      ALU.subtract, ALU.mult)
                    ins.then_inc(z_ready, 1)
                    dve.wait_ge(z_ready, g + 1)
                    nc.vector.tensor_tensor(x1[k][:], x1[k][:], ysh[k][:], ALU.add).then_inc(out_ready, 1)

        @block.scalar
        def _(act):
            for k in range(2):
                act.sem_inc(out_stored[k], 1)
            with nc.scalar.Fori(0, NG // 2) as u:
                for k in range(2):
                    act.wait_ge(var_ready, 2 * u + k + 1)
                    nc.scalar.activation(root[:], var[:], ACT.Sqrt).then_inc(root_ready, 1)
                    act.wait_ge(out_ready, 2 * u + k + 1)
                    act.dma_start(io["out"][bass.ds((2 * u + k) * G, G), :].rearrange("(a p) e -> p a e", p=P),
                                  x1[k][:]).then_inc(out_stored[k], 16)
            for k in range(2):
                act.wait_ge(out_stored[k], 16 * NG // 2 + 1)


SCRATCH = {
    "xT": ([NG, P, 2 * EC * G], F16),
    "qk": ([NG, 2, 2 * E, G], F16),
    "v": ([NG, P, A, E], F32),
    "en": ([NG, P, A, 2 * H], F32),
    "sums": ([C, P, H, D + 1], F32),
    "x1": ([T, E], F32),
    "xT2": ([NG, P, 2 * EC * G], F16),
    "rows": ([T, 2 * E], F16),
    "slot_token": ([NSLOT, 1], U32),
    "slots": ([NG, P, A * K], U32),
    "weights": ([NG, P, A * K], F32),
    "ye": ([NSLOT, E], F32),
    "ysh": ([T, E], F32),
}
CONSTS = {
    "ident16": ([P, P], F16), "ident32": ([P, P], F32), "heads": ([P, 2 * EC * 2 * H], F32),
    "tri": ([P, P], F16), "ones": ([P, P], F16), "gate": ([P, EC * NE], BF16), "expert": ([P, 2 * NE], F32),
    "bias": ([P, NE], F32),
}


def build(nc, io, stages=None, debug=()):
    for name, (shape, dt) in SCRATCH.items():
        kind = "ExternalOutput" if name in debug else "Internal"
        io[name] = nc.dram_tensor(f"{name}_dram", shape, dt, kind=kind).ap()
    with ExitStack() as ctx:
        keep = {n: ctx.enter_context(nc.sbuf_tensor(f"keep_{n}", s, d)) for n, (s, d) in CONSTS.items()}
        keep["wqkv"] = ctx.enter_context(nc.sbuf_tensor("keep_wqkv", [P, 2, EC, 3 * E], F16))
        keep["wo"] = ctx.enter_context(nc.sbuf_tensor("keep_wo", [P, EC, E], F32))
        keep["feat"] = ctx.enter_context(nc.sbuf_tensor("keep_feat", [96, H, M], F16))
        todo = [
            lambda: setup_stage(nc, io, keep),
            lambda: norm_stage(nc, io, keep, "s1", io["x"], io["xT"], None),
            lambda: project_stage(nc, io, keep),
            lambda: sums_stage(nc, io, keep),
            lambda: attend_stage(nc, io, keep),
            lambda: norm_stage(nc, io, keep, "s5", io["x1"], io["xT2"], io["rows"]),
            lambda: route_stage(nc, io, keep),
            lambda: expert_stage(nc, io, keep, False),
            lambda: expert_stage(nc, io, keep, True),
            lambda: combine_stage(nc, io, keep),
        ]
        for f in todo[:stages]:
            f()


def shape_constants():
    import numpy as np

    had = np.ones((1, 1), np.float32)
    while had.shape[0] < HP:
        had = np.block([[had, had], [had, -had]])
    d = np.arange(P) % D
    freq = (np.float32(10000.0) ** (-np.arange(0, D, 2, dtype=np.float32) / np.float32(D))).astype(np.float32)
    angle = np.arange(L - 1, dtype=np.float32)[:, None] * freq
    cos = np.concatenate([np.ones((1, D // 2), np.float32), np.cos(angle)]).T[d // 2]
    sin = np.concatenate([np.zeros((1, D // 2), np.float32), np.sin(angle)]).T[d // 2]
    sin = sin * np.where(d % 2 == 0, -1, 1)[:, None]
    turns = np.stack([cos, sin], 1).reshape(P, 2, GPC, G).transpose(2, 0, 1, 3)
    heads = np.zeros((P, 2 * EC, 2 * H), np.float32)
    for j in range(2 * EC):
        heads[np.arange(P), j, 4 * j + np.arange(P) // D] = 1
    expert = np.concatenate([np.arange(NE), np.arange(NE) * CAP])[None].astype(np.float32)
    token = np.arange(T, dtype=np.uint32).reshape(NG, A, P).transpose(0, 2, 1)
    return {
        "had": had.astype(np.float32), "turns": turns.astype(np.float32), "ident16": np.eye(P, dtype=np.float16),
        "ident32": np.eye(P, dtype=np.float32), "heads": heads.reshape(P, -1),
        "tri": np.triu(np.ones((P, P)), 1).astype(np.float16),
        "ones": np.ones((P, P), np.float16), "expert": expert, "token": token,
    }


def kernel(**inputs):
    import concourse.bacc as _bacc
    import numpy as np
    from concourse.bass_utils import run_bass_kernel_spmd as _run

    v = {n[3:]: np.asarray(a) for n, a in inputs.items()}
    signs, scales = v["attn_sorf_signs"], v["attn_sorf_scales"]
    laid = {
        "x": v["attn_x"].reshape(T, E),
        "w_qkvT": v["attn_w_qkv"].T,
        "w_outT": v["attn_w_out"].T,
        "signs": signs[:, :M // HP].transpose(3, 2, 0, 1).reshape(HP, 3, H * M // HP),
        "scales": scales[:, :M // HP].reshape(1, -1),
        "gate": v["ffn_gate_w"].T.reshape(EC, P, NE).transpose(1, 0, 2).reshape(P, -1),
        "bias": v["ffn_bias"].reshape(1, -1),
        "W1": v["ffn_W1"], "W3": v["ffn_W3"], "W2": v["ffn_W2"],
        "sw1": v["ffn_sw1"].T, "sw3": v["ffn_sw3"].T, "sw2": v["ffn_sw2"].T,
        **shape_constants(),
    }
    nc = _bacc.Bacc("TRN2", target_bir_lowering=False, num_devices=1)
    arrays, io = {}, {}
    for name, a in laid.items():
        a = np.ascontiguousarray(a)
        arrays[f"{name}_in"] = a
        io[name] = nc.dram_tensor(f"{name}_in", a.shape, mybir.dt.from_np(a.dtype), kind="ExternalInput").ap()
    io["out"] = nc.dram_tensor("out_dram", [T, E], F32, kind="ExternalOutput").ap()
    build(nc, io)
    return _run(nc, [arrays], core_ids=[0]).results[0]["out_dram"].reshape(C, L, E)
```

```python
from contextlib import ExitStack

import concourse.bass as bass
from concourse import mybir

P = 128
C, L, E = 4, 2048, 512
H, D = 16, 32
M = 128
HP = 64
NE, K, I = 32, 4, 256
CAP = 512
T = C * L
G = 512
NG = T // G
A = G // P
EC = E // P
GPC = L // G
NSLOT = NE * CAP
W_SCALE = 256.0
M_SCALE = 64.0
F16_MAX = 65504.0
NOWHERE = 1.0e6

ALU = mybir.AluOpType
ACT = mybir.ActivationFunctionType
AX = mybir.AxisListType
F32 = mybir.dt.float32
F16 = mybir.dt.float16
BF16 = mybir.dt.bfloat16
U32 = mybir.dt.uint32


class Tools:

    def __init__(self, nc, ctx, stage):
        self.nc, self.ctx, self.stage, self.sems = nc, ctx, stage, []
        ctx.callback(self.close)

    def close(self):
        self.nc.clear_and_free_semaphores(self.sems)
        self.nc.all_engine_barrier()

    def sb(self, name, shape, dt=F32):
        return self.ctx.enter_context(self.nc.sbuf_tensor(f"{self.stage}_{name}", shape, dt))

    def pair(self, name, shape, dt=F32):
        return [self.sb(f"{name}{k}", shape, dt) for k in range(2)]

    def psum(self, name, banks=1):
        return self.ctx.enter_context(self.nc.psum_tensor(f"{self.stage}_{name}", [P, 512 * banks], F32))

    def sem(self, name):
        self.sems.append(self.nc.alloc_semaphore(f"{self.stage}_{name}"))
        return self.sems[-1]


def hold(eng, sem, value, pace):
    eng.wait_ge(sem, value)
    eng.sem_inc(pace, 1)


def setup_stage(nc, io, keep):
    with ExitStack() as ctx:
        t = Tools(nc, ctx, "s0")
        sb, sem = t.sb, t.sem
        had = sb("had", [HP, HP])
        s3 = sb("s3", [HP, 2 * H])
        s2 = sb("s2", [HP, 2 * H])
        s1 = sb("s1", [96, 2 * H])
        g = sb("g", [96, 2 * H * HP])
        left3 = sb("left3", [HP, 2 * H, HP])
        left2 = sb("left2", [HP, 2 * H, 96])
        y = sb("y", [HP, 2 * H, HP])
        m = sb("m", [96, 2 * H * HP])
        w = sb("w", [P, EC, 3 * E])
        zero = sb("zero", [P, NSLOT // P], U32)
        pY = [t.psum(f"pY{q}") for q in range(4)]
        pZ = [t.psum(f"pZ{q}") for q in range(4)]
        loaded, wloaded, kept = sem("loaded"), sem("wloaded"), sem("kept")
        left_ready, y_ready, y_copied, z_ready = sem("left_ready"), sem("y_ready"), sem("y_copied"), sem("z_ready")
        m_signed, m_ready, hi_ready, w_hi, zeroed, cleared = (
            sem("m_signed"), sem("m_ready"), sem("hi_ready"), sem("w_hi"), sem("zeroed"), sem("cleared"))
        block = ctx.enter_context(nc.Block())

        @block.sync
        def _(sp):
            sp.dma_start(had[:], io["had"]).then_inc(loaded, 16)
            sp.dma_start(s3[:], io["signs"][:, 2, :]).then_inc(loaded, 16)
            sp.dma_start(s2[:], io["signs"][:, 1, :]).then_inc(loaded, 16)
            for r in range(3):
                sp.dma_start(s1[32 * r:32 * r + 32, :], io["signs"][0:D, 0, :]).then_inc(loaded, 16)
            sp.dma_start(g[:], io["scales"].to_broadcast([96, 2 * H * HP])).then_inc(loaded, 16)
            sp.dma_start(w[:], io["w_qkvT"].rearrange("(c p) n -> p c n", p=P)).then_inc(wloaded, 16)
            sp.dma_start(keep["wo"][:], io["w_outT"].rearrange("(c p) n -> p c n", p=P)).then_inc(kept, 16)
            for name in ("ident16", "ident32", "heads", "tri", "ones", "gate", "expert", "bias"):
                src = io[name]
                if src.shape[0] == 1:
                    src = src.to_broadcast([P, src.shape[1]])
                sp.dma_start(keep[name][:], src).then_inc(kept, 16)
            sp.wait_ge(zeroed, 1)
            sp.dma_start(io["slot_token"].rearrange("(p n) o -> p (n o)", p=P), zero[:]).then_inc(cleared, 16)
            sp.wait_ge(kept, 16 * 9)
            sp.wait_ge(cleared, 16)

        @block.vector
        def _(dve):
            nc.vector.memset(zero[:], 0).then_inc(zeroed, 1)
            dve.wait_ge(loaded, 16 * 7)
            nc.vector.tensor_tensor(left3[:], had[:].unsqueeze(1).broadcast_to([HP, 2 * H, HP]),
                                    s3[:].unsqueeze(2).broadcast_to([HP, 2 * H, HP]), ALU.mult).then_inc(left_ready, 1)
            for r in range(3):
                nc.vector.tensor_tensor(left2[:, :, 32 * r:32 * r + 32],
                                        had[:, 0:D].unsqueeze(1).broadcast_to([HP, 2 * H, D]),
                                        s2[:].unsqueeze(2).broadcast_to([HP, 2 * H, D]), ALU.mult).then_inc(left_ready, 1)
            for q in range(4):
                dve.wait_ge(y_ready, q + 1)
                nc.vector.tensor_copy(y[:, 8 * q:8 * q + 8, :].rearrange("p a b -> p (a b)"),
                                      pY[q][0:HP, :]).then_inc(y_copied, 1)
            for q in range(4):
                dve.wait_ge(z_ready, q + 1)
                mq = m[:, 512 * q:512 * q + 512]
                nc.vector.tensor_tensor(mq.rearrange("p (a b) -> p a b", b=HP),
                                        pZ[q][0:96, :].rearrange("p (a b) -> p a b", b=HP),
                                        s1[:, 8 * q:8 * q + 8].unsqueeze(2).broadcast_to([96, 8, HP]),
                                        ALU.mult).then_inc(m_signed, 1)
                dve.wait_ge(m_signed, q + 1)
                nc.vector.scalar_tensor_tensor(out=mq, in0=mq, scalar=M_SCALE / HP ** 2,
                                               in1=g[:, 512 * q:512 * q + 512],
                                               op0=ALU.mult, op1=ALU.mult).then_inc(m_ready, 1)
            dve.wait_ge(hi_ready, 1)
            dve.wait_ge(m_ready, 4)
            feat = keep["feat"][:].rearrange("p h f -> p (h f)")
            nc.vector.tensor_tensor(feat[32:64, :], m[32:64, :], feat[32:64, :], ALU.subtract).then_inc(m_ready, 1)
            for c in range(EC):
                dve.wait_ge(w_hi, c + 1)
                nc.vector.scalar_tensor_tensor(out=keep["wqkv"][:, 1, c, :], in0=w[:, c, :], scalar=W_SCALE,
                                               in1=keep["wqkv"][:, 0, c, :], op0=ALU.mult,
                                               op1=ALU.subtract).then_inc(m_ready, 1)

        @block.scalar
        def _(act):
            act.wait_ge(wloaded, 16)
            for c in range(EC):
                nc.scalar.activation(keep["wqkv"][:, 0, c, :], w[:, c, :], ACT.Copy, scale=W_SCALE).then_inc(w_hi, 1)
            act.wait_ge(m_ready, 4)
            nc.scalar.activation(keep["feat"][:].rearrange("p h f -> p (h f)"), m[:], ACT.Copy).then_inc(hi_ready, 1)

        @block.tensor
        def _(pe):
            pe.wait_ge(left_ready, 4)
            for i in range(2 * H):
                mm = nc.tensor.matmul(pY[i // 8][0:HP, (i % 8) * HP:(i % 8 + 1) * HP], left3[:, i, :], had[:],
                                      start=True, stop=True)
                if i % 8 == 7:
                    mm.then_inc(y_ready, 1)
            for i in range(2 * H):
                if i % 8 == 0:
                    pe.wait_ge(y_copied, i // 8 + 1)
                mm = nc.tensor.matmul(pZ[i // 8][0:96, (i % 8) * HP:(i % 8 + 1) * HP], left2[:, i, :], y[:, i, :],
                                      start=True, stop=True)
                if i % 8 == 7:
                    mm.then_inc(z_ready, 1)


def norm_stage(nc, io, keep, stage, src, dst_T, dst_rows):
    with ExitStack() as ctx:
        t = Tools(nc, ctx, stage)
        x = t.pair("x", [P, A, E])
        hl = t.pair("hl", [P, A, 2, E], F16)
        xT = t.pair("xT", [P, 2, EC, G], F16)
        stats = t.pair("stats", [P, A, 6])
        mv = t.pair("mv", [P, A, 2])
        rstd = t.pair("rstd", [P, A])
        power = t.sb("power", [P, A])
        turned = [t.psum(f"turned{k}") for k in range(2)]
        loaded = [t.sem(f"loaded{k}") for k in range(2)]
        stored = [t.sem(f"stored{k}") for k in range(2)]
        rows_stored = [t.sem(f"rows_stored{k}") for k in range(2)]
        pace = t.sem("pace")
        stats_ready, mv_ready, var_ready, rstd_ready = (
            t.sem("stats_ready"), t.sem("mv_ready"), t.sem("var_ready"), t.sem("rstd_ready"))
        x_ready, hi_ready, lo_ready = t.sem("x_ready"), t.sem("hi_ready"), t.sem("lo_ready")
        turned_ready, xT_ready, power_ready = t.sem("turned_ready"), t.sem("xT_ready"), t.sem("power_ready")
        block = ctx.enter_context(nc.Block())

        @block.sync
        def _(sp):
            with nc.sync.Fori(0, NG // 2) as u:
                for k in range(2):
                    hold(sp, lo_ready, 2 * u + k + 1, pace)
                    sp.dma_start(x[k][:], src[bass.ds((2 * u + k) * G, G), :].rearrange("(a p) e -> p a e", p=P)
                                 ).then_inc(loaded[k], 16)

        @block.vector
        def _(dve):
            dve.sem_inc(lo_ready, 2)
            with nc.vector.Fori(0, NG // 2) as u:
                for k in range(2):
                    dve.wait_ge(loaded[k], 16 * u + 16)
                    for a in range(A):
                        ins = nc.vector.bn_stats(stats[k][:, a, :], x[k][:, a, :])
                    ins.then_inc(stats_ready, 1)
                    hold(dve, stats_ready, 2 * u + k + 1, pace)
                    for a in range(A):
                        ins = nc.vector.bn_aggr(mv[k][:, a, :], stats[k][:, a, :])
                    ins.then_inc(mv_ready, 1)
                    dve.wait_ge(rstd_ready, 2 * u + k + 1)
                    for a in range(A):
                        ins = nc.vector.tensor_scalar(x[k][:, a, :], x[k][:, a, :], mv[k][:, a, 0:1],
                                                      rstd[k][:, a:a + 1], ALU.subtract, ALU.mult)
                    ins.then_inc(x_ready, 1)
                    dve.wait_ge(hi_ready, 2 * u + k + 1)
                    nc.vector.tensor_tensor(hl[k][:, :, 1, :], x[k][:], hl[k][:, :, 0, :],
                                            ALU.subtract).then_inc(lo_ready, 1)

        @block.gpsimd
        def _(pool):
            nc.gpsimd.memset(power[:], -0.5).then_inc(power_ready, 1)
            pool.wait_ge(power_ready, 1)
            with nc.gpsimd.Fori(0, NG // 2) as u:
                for k in range(2):
                    hold(pool, mv_ready, 2 * u + k + 1, pace)
                    nc.gpsimd.tensor_scalar(rstd[k][:], mv[k][:, :, 1], 1e-5, None, ALU.add).then_inc(var_ready, 1)
                    pool.wait_ge(var_ready, 2 * u + k + 1)
                    nc.gpsimd.tensor_tensor(rstd[k][:], rstd[k][:], power[:], ALU.pow).then_inc(rstd_ready, 1)

        @block.scalar
        def _(act):
            for k in range(2):
                act.sem_inc(stored[k], 1)
                act.sem_inc(rows_stored[k], 1)
            act.sem_inc(xT_ready, 2)
            with nc.scalar.Fori(0, NG // 2) as u:
                for k in range(2):
                    act.wait_ge(x_ready, 2 * u + k + 1)
                    if dst_rows is not None:
                        act.wait_ge(rows_stored[k], 16 * u + 1)
                    nc.scalar.activation(hl[k][:, :, 0, :], x[k][:], ACT.Copy).then_inc(hi_ready, 1)
                    act.wait_ge(stored[k], 16 * u + 1)
                    for a in range(A):
                        act.wait_ge(turned_ready, (2 * u + k) * A + a + 1)
                        nc.scalar.activation(
                            xT[k][:, :, :, a * P:(a + 1) * P],
                            turned[a % 2][:].bitcast(F16).rearrange("p (s c q) -> p s c q", s=2, c=EC),
                            ACT.Copy).then_inc(xT_ready, 1)
                    act.wait_ge(xT_ready, (2 * u + k) * A + A + 2)
                    act.dma_start(dst_T[bass.ds(2 * u + k, 1)].rearrange("o p n -> p (o n)"),
                                  xT[k][:].rearrange("p s c q -> p (s c q)")).then_inc(stored[k], 16)
                    if dst_rows is not None:
                        act.wait_ge(lo_ready, 2 * u + k + 3)
                        act.dma_start(dst_rows[bass.ds((2 * u + k) * G, G), :].rearrange("(a p) n -> p a n", p=P),
                                      hl[k][:].rearrange("p a s e -> p a (s e)")).then_inc(rows_stored[k], 16)
            for k in range(2):
                act.wait_ge(stored[k], 1 + 16 * NG // 2)
                if dst_rows is not None:
                    act.wait_ge(rows_stored[k], 1 + 16 * NG // 2)

        @block.tensor
        def _(pe):
            with nc.tensor.Fori(0, NG // 2) as u:
                for k in range(2):
                    pe.wait_ge(lo_ready, 2 * u + k + 3)
                    for a in range(A):
                        pe.wait_ge(xT_ready, (2 * u + k) * A + a + 1)
                        for s in range(2):
                            for c in range(EC):
                                mm = nc.tensor.transpose(
                                    turned[a % 2][:].bitcast(F16)[:, (s * EC + c) * P:(s * EC + c + 1) * P],
                                    hl[k][:, a, s, c * P:(c + 1) * P], keep["ident16"][:])
                        mm.then_inc(turned_ready, 1)


def project_stage(nc, io, keep):
    with ExitStack() as ctx:
        t = Tools(nc, ctx, "s2")
        xT = t.pair("xT", [P, 2, EC, G], F16)
        table = t.sb("table", [P, 2, G])
        raw = t.pair("raw", [P, G])
        cosp = t.pair("cosp", [P, G])
        swap = t.pair("swap", [P, G])
        rot = t.pair("rot", [P, G])
        sq = t.pair("sq", [P, 2 * EC, G])
        hl = t.pair("hl", [P, 2, 2 * EC, G], F16)
        v = t.pair("v", [P, A, E])
        en = t.pair("en", [P, A, 2 * H])
        banks = [t.psum(f"proj{b}") for b in range(4)]
        norms = t.psum("norms")
        x_loaded, hl_stored, v_stored, en_stored = (
            [t.sem(f"{n}{k}") for k in range(2)] for n in ("x_loaded", "hl_stored", "v_stored", "en_stored"))
        table_loaded, pace = t.sem("table_loaded"), t.sem("pace")
        proj_ready, evac, cos_ready, swap_ready, sin_ready = (
            t.sem("proj_ready"), t.sem("evac"), t.sem("cos_ready"), t.sem("swap_ready"), t.sem("sin_ready"))
        rot_ready, hi_ready, sq_ready, lo_ready = (
            t.sem("rot_ready"), t.sem("hi_ready"), t.sem("sq_ready"), t.sem("lo_ready"))
        norms_ready, en_ready = t.sem("norms_ready"), t.sem("en_ready")
        QK = 2 * EC
        OUT = QK + A
        block = ctx.enter_context(nc.Block())

        @block.sync
        def _(sp):
            with nc.sync.Fori(0, GPC) as pg:
                hold(sp, sin_ready, C * QK * pg + 1, pace)
                hold(sp, cos_ready, C * QK * pg + 2, pace)
                sp.dma_start(table[:], io["turns"][bass.ds(pg, 1)].rearrange("o p s n -> p (o s) n")
                             ).then_inc(table_loaded, 16)
                with nc.sync.Fori(0, C // 2) as u:
                    for k in range(2):
                        hold(sp, proj_ready, OUT * C * pg + 2 * OUT * u + OUT * k + 1, pace)
                        sp.dma_start(xT[k][:].rearrange("p s c q -> p (s c q)"),
                                     io["xT"][bass.ds(2 * GPC * u + pg + GPC * k, 1)].rearrange("o p n -> p (o n)")
                                     ).then_inc(x_loaded[k], 16)

        @block.tensor
        def _(pe):
            pe.sem_inc(proj_ready, OUT + 1)
            pe.sem_inc(norms_ready, 2)
            with nc.tensor.Fori(0, GPC) as pg, nc.tensor.Fori(0, C // 2) as u:
                for k in range(2):
                    pe.wait_ge(x_loaded[k], 32 * pg + 16 * u + 16)
                    hi, lo = xT[k][:, 0], xT[k][:, 1]
                    for j in range(OUT):
                        pe.wait_ge(evac, OUT * C * pg + 2 * OUT * u + OUT * k + j + 1)
                        for c in range(EC):
                            if j < QK:
                                w = keep["wqkv"][:, :, c, j * P:(j + 1) * P]
                                parts = ((w[:, 0], hi[:, c]), (w[:, 0], lo[:, c]), (w[:, 1], hi[:, c]))
                            else:
                                w = keep["wqkv"][:, :, c, 2 * E:3 * E]
                                q = slice((j - QK) * P, (j - QK + 1) * P)
                                parts = ((hi[:, c, q], w[:, 0]), (hi[:, c, q], w[:, 1]), (lo[:, c, q], w[:, 0]))
                            for i, (left, right) in enumerate(parts):
                                mm = nc.tensor.matmul(banks[j % 4][:], left, right, start=(c == 0 and i == 0),
                                                      stop=(c == EC - 1 and i == 2))
                        mm.then_inc(proj_ready, 1)
                    pe.wait_ge(sq_ready, QK * C * pg + 2 * QK * u + QK * k + QK + 2)
                    pe.wait_ge(en_ready, C * pg + 2 * u + k + 1)
                    for a in range(A):
                        for j in range(QK):
                            mm = nc.tensor.matmul(norms[:, a * 2 * H:(a + 1) * 2 * H], sq[k][:, j, a * P:(a + 1) * P],
                                                  keep["heads"][:, j * 2 * H:(j + 1) * 2 * H],
                                                  start=(j == 0), stop=(j == QK - 1))
                    mm.then_inc(norms_ready, 1)

        @block.gpsimd
        def _(pool):
            pool.sem_inc(cos_ready, 2)
            with nc.gpsimd.Fori(0, GPC) as pg, nc.gpsimd.Fori(0, C // 2) as u:
                for k in range(2):
                    for j in range(QK):
                        if k == 0 and j == 0:
                            pool.wait_ge(table_loaded, 16 * pg + 16)
                        n = QK * C * pg + 2 * QK * u + QK * k + j
                        pool.wait_ge(rot_ready, n + 1)
                        pool.wait_ge(evac, OUT * C * pg + 2 * OUT * u + OUT * k + j + 5)
                        nc.gpsimd.tensor_tensor(cosp[j % 2][:], raw[j % 2][:], table[:, 0, :],
                                                ALU.mult).then_inc(cos_ready, 1)

        @block.vector
        def _(dve):
            dve.sem_inc(rot_ready, 2)
            dve.sem_inc(swap_ready, 2)
            dve.sem_inc(sin_ready, 1)
            pairs = [i ^ 1 for i in range(32)]
            with nc.vector.Fori(0, GPC) as pg, nc.vector.Fori(0, C // 2) as u:
                for k in range(2):
                    if k == 0:
                        dve.wait_ge(table_loaded, 16 * pg + 16)
                    for j in range(QK + 1):
                        n = QK * C * pg + 2 * QK * u + QK * k + j
                        if j < QK:
                            hold(dve, evac, OUT * C * pg + 2 * OUT * u + OUT * k + j + 5, pace)
                            nc.vector.stream_shuffle(swap[j % 2][:], raw[j % 2][:], pairs).then_inc(swap_ready, 1)
                            dve.wait_ge(swap_ready, n + 3)
                            nc.vector.tensor_tensor(swap[j % 2][:], swap[j % 2][:], table[:, 1, :],
                                                    ALU.mult).then_inc(sin_ready, 1)
                        if j >= 1:
                            dve.wait_ge(hi_ready, n)
                            nc.vector.tensor_tensor(hl[k][:, 1, j - 1, :], rot[(j - 1) % 2][:],
                                                    hl[k][:, 0, j - 1, :], ALU.subtract).then_inc(lo_ready, 1)
                        if j < QK:
                            dve.wait_ge(sin_ready, n + 2)
                            dve.wait_ge(cos_ready, n + 3)
                            dve.wait_ge(sq_ready, n + 1)
                            nc.vector.tensor_tensor(rot[j % 2][:], cosp[j % 2][:], swap[j % 2][:],
                                                    ALU.add).then_inc(rot_ready, 1)

        @block.scalar
        def _(act):
            act.sem_inc(evac, 4)
            act.sem_inc(sq_ready, 2)
            act.sem_inc(en_ready, 1)
            for s in (*v_stored, *en_stored, *hl_stored):
                act.sem_inc(s, 1)
            with nc.scalar.Fori(0, GPC) as pg, nc.scalar.Fori(0, C // 2) as u:
                for k in range(2):
                    act.wait_ge(hl_stored[k], 64 * pg + 32 * u + 1)
                    act.wait_ge(v_stored[k], 32 * pg + 16 * u + 1)
                    act.wait_ge(norms_ready, C * pg + 2 * u + k + 1)
                    for j in range(OUT):
                        n = QK * C * pg + 2 * QK * u + QK * k + j
                        act.wait_ge(proj_ready, OUT * C * pg + 2 * OUT * u + OUT * k + OUT + j + 2)
                        if j < QK:
                            act.wait_ge(swap_ready, n + 1)
                            act.wait_ge(cos_ready, n + 1)
                            dst = raw[j % 2][:]
                        else:
                            dst = v[k][:, j - QK, :]
                        nc.scalar.activation(dst, banks[j % 4][:], ACT.Copy, scale=1.0 / W_SCALE).then_inc(evac, 1)
                        if 1 <= j <= QK:
                            act.wait_ge(rot_ready, n + 2)
                            nc.scalar.activation(hl[k][:, 0, j - 1, :], rot[(j - 1) % 2][:],
                                                 ACT.Copy).then_inc(hi_ready, 1)
                            nc.scalar.activation(sq[k][:, j - 1, :], rot[(j - 1) % 2][:],
                                                 ACT.Square).then_inc(sq_ready, 1)
                    group = bass.ds(2 * GPC * u + pg + GPC * k, 1)
                    act.wait_ge(evac, OUT * C * pg + 2 * OUT * u + OUT * k + OUT + 4)
                    act.dma_start(io["v"][group].rearrange("o p a e -> p (o a) e"), v[k][:]).then_inc(v_stored[k], 16)
                    act.wait_ge(lo_ready, QK * C * pg + 2 * QK * u + QK * k + QK)
                    for s in range(2):
                        act.dma_start(io["qk"][group, s:s + 1].rearrange("o s (c p) n -> p (o s c) n", p=P),
                                      hl[k][:, s]).then_inc(hl_stored[k], 16)
                    act.wait_ge(norms_ready, C * pg + 2 * u + k + 3)
                    act.wait_ge(en_stored[k], 32 * pg + 16 * u + 1)
                    nc.scalar.activation(en[k][:].rearrange("p a h -> p (a h)"), norms[:, 0:A * 2 * H], ACT.Exp,
                                         scale=-0.5).then_inc(en_ready, 1)
                    act.wait_ge(en_ready, C * pg + 2 * u + k + 2)
                    act.dma_start(io["en"][group].rearrange("o p a h -> p (o a) h"), en[k][:]).then_inc(en_stored[k], 16)
            for k in range(2):
                act.wait_ge(hl_stored[k], 32 * NG // 2 + 1)
                act.wait_ge(v_stored[k], 16 * NG // 2 + 1)
                act.wait_ge(en_stored[k], 16 * NG // 2 + 1)


def sums_stage(nc, io, keep):
    with ExitStack() as ctx:
        t = Tools(nc, ctx, "s3")
        kT = [t.sb(f"kT{k}", [96, H, G], F16) for k in range(2)]
        v = t.pair("v", [P, A, E])
        en = t.pair("en", [P, A, 2 * H])
        aug = t.pair("aug", [P, A * H, D + 1])
        phi = t.pair("phi", [P, H // 2, M])
        zero = t.sb("zero", [P, G], F16)
        sumT = t.sb("sumT", [D + 1, H, M])
        most, largest, share = t.sb("most", [P, H]), t.sb("largest", [P, H]), t.sb("share", [P, H])
        scaled = t.sb("scaled", [P, 2, H // 2, D + 1])
        halves = t.sb("halves", [P, 2, H, D + 1], F16)
        logits = [t.psum(f"logits{b}", 2) for b in range(2)]
        parts = t.psum("parts", 4)
        k_loaded, v_loaded = ([t.sem(f"{n}{k}") for k in range(2)] for n in ("k_loaded", "v_loaded"))
        logits_ready, phi_ready, aug_ready, part_ready = (
            t.sem("logits_ready"), t.sem("phi_ready"), t.sem("aug_ready"), t.sem("part_ready"))
        cleared, sumT_ready, turned_ready, scaled_ready, most_ready, largest_ready, step, halves_ready, stored, pace = (
            t.sem(n) for n in ("cleared", "sumT_ready", "turned_ready", "scaled_ready", "most_ready", "largest_ready",
                               "step", "halves_ready", "stored", "pace"))
        HALF = H // 2
        block = ctx.enter_context(nc.Block())

        @block.sync
        def _(sp):
            with nc.sync.Fori(0, C) as ch:
                with nc.sync.Fori(0, GPC // 2) as u:
                    for k in range(2):
                        group = bass.ds(GPC * ch + 2 * u + k, 1)
                        hold(sp, logits_ready, 32 * ch + 16 * u + 8 * k + 1, pace)
                        for r, s in enumerate((0, 0, 1)):
                            sp.dma_start(kT[k][32 * r:32 * r + 32],
                                         io["qk"][group, s, E:2 * E, :].rearrange("o (h d) n -> d (o h) n", d=D)
                                         ).then_inc(k_loaded[k], 16)
                        hold(sp, aug_ready, GPC * ch + 2 * u + k + 1, pace)
                        sp.dma_start(v[k][:], io["v"][group].rearrange("o p a e -> p (o a) e")).then_inc(v_loaded[k], 16)
                        sp.dma_start(en[k][:], io["en"][group].rearrange("o p a h -> p (o a) h")).then_inc(v_loaded[k], 16)
                hold(sp, halves_ready, ch + 1, pace)
                sp.dma_start(io["sums"][bass.ds(ch, 1)].rearrange("o p n -> p (o n)"),
                             halves[:].rearrange("p s h d -> p (s h d)")).then_inc(stored, 16)
                sp.dma_start(io["largest"][bass.ds(ch, 1)].rearrange("o p h -> p (o h)"), largest[:]
                             ).then_inc(stored, 16)
            sp.wait_ge(stored, 32 * C + 1)

        @block.vector
        def _(dve):
            nc.vector.memset(zero[:], 0.0).then_inc(cleared, 1)
            dve.sem_inc(aug_ready, 2)
            dve.sem_inc(sumT_ready, 1)
            dve.sem_inc(scaled_ready, 1)
            with nc.vector.Fori(0, C) as ch:
                with nc.vector.Fori(0, GPC // 2) as u:
                    for k in range(2):
                        dve.wait_ge(v_loaded[k], 64 * ch + 32 * u + 32)
                        dve.wait_ge(part_ready, 32 * ch + 16 * u + 8 * k + 2)
                        weight = en[k][:, :, H:2 * H]
                        nc.vector.tensor_tensor(aug[k][:, :, 0:D].rearrange("p (a h) d -> p a h d", a=A),
                                                v[k][:].rearrange("p a (h d) -> p a h d", d=D),
                                                weight.unsqueeze(3).broadcast_to([P, A, H, D]), ALU.mult)
                        nc.vector.tensor_copy(aug[k][:, :, D:D + 1].rearrange("p (a h) d -> p a (h d)", a=A),
                                              weight).then_inc(aug_ready, 1)
                dve.wait_ge(part_ready, 32 * ch + 32 + 10)
                nc.vector.tensor_scalar(sumT[:].rearrange("p h m -> p (h m)"), parts[0:D + 1, :], 1.0 / M, None,
                                        ALU.mult).then_inc(sumT_ready, 1)
                dve.wait_ge(turned_ready, ch + 1)
                nc.vector.tensor_copy(
                    scaled[:].rearrange("p b h d -> p b (h d)"),
                    logits[0][:].rearrange("p (b n) -> p b n", b=2)[:, :, 0:HALF * (D + 1)]).then_inc(scaled_ready, 1)
                dve.wait_ge(scaled_ready, ch + 2)
                flat = scaled[:].rearrange("p b h d -> p (b h) d")
                nc.vector.tensor_reduce(most[:], flat, AX.X, ALU.max, apply_absolute_value=True).then_inc(most_ready, 1)
                dve.wait_ge(largest_ready, ch + 1)
                nc.vector.tensor_scalar(share[:], largest[:], 1e-30, None, ALU.max).then_inc(step, 1)
                dve.wait_ge(step, 4 * ch + 1)
                nc.vector.reciprocal(share[:], share[:]).then_inc(step, 1)
                dve.wait_ge(step, 4 * ch + 2)
                nc.vector.tensor_tensor(flat, flat, share[:].unsqueeze(2).broadcast_to([P, H, D + 1]),
                                        ALU.mult).then_inc(step, 1)
                dve.wait_ge(step, 4 * ch + 3)
                dve.wait_ge(stored, 32 * ch + 1)
                nc.vector.tensor_copy(halves[:, 0], flat).then_inc(step, 1)
                dve.wait_ge(step, 4 * ch + 4)
                nc.vector.tensor_tensor(halves[:, 1], flat, halves[:, 0], ALU.subtract).then_inc(halves_ready, 1)

        @block.gpsimd
        def _(pool):
            with nc.gpsimd.Fori(0, C) as ch:
                hold(pool, most_ready, ch + 1, pace)
                hold(pool, stored, 32 * ch + 1, pace)
                nc.gpsimd.partition_all_reduce(largest[:], most[:], P, bass.bass_isa.ReduceOp.max
                                               ).then_inc(largest_ready, 1)

        @block.scalar
        def _(act):
            act.sem_inc(phi_ready, 2)
            with nc.scalar.Fori(0, C) as ch, nc.scalar.Fori(0, GPC // 2) as u:
                for k in range(2):
                    for i in range(2 * A):
                        n = 32 * ch + 16 * u + 8 * k + i
                        act.wait_ge(logits_ready, n + 10)
                        act.wait_ge(part_ready, n + 9)
                        nc.scalar.activation(phi[i % 2][:].rearrange("p h m -> p (h m)"), logits[i % 2][:], ACT.Exp,
                                             scale=1.0 / M_SCALE).then_inc(phi_ready, 1)

        @block.tensor
        def _(pe):
            pe.sem_inc(logits_ready, 9)
            pe.sem_inc(part_ready, 10)
            pe.sem_inc(stored, 1)

            def make_logits(n, k, i):
                a, half = i // 2, i % 2
                pe.wait_ge(phi_ready, n + i + 1)
                for h in range(HALF):
                    mm = nc.tensor.matmul(logits[i % 2][:, h * M:(h + 1) * M],
                                          kT[k][:, HALF * half + h, a * P:(a + 1) * P],
                                          keep["feat"][:, HALF * half + h, :], start=True, stop=True)
                mm.then_inc(logits_ready, 1)

            pe.wait_ge(cleared, 1)
            with nc.tensor.Fori(0, C) as ch:
                pe.wait_ge(sumT_ready, ch + 1)
                for b in range(4):
                    nc.tensor.matmul(parts[0:D + 1, 512 * b:512 * b + 512], zero[:, 0:D + 1], zero[:],
                                     start=True, stop=True)
                hold(pe, scaled_ready, ch + 1, pace)
                with nc.tensor.Fori(0, GPC // 2) as u:
                    for k in range(2):
                        n = 32 * ch + 16 * u + 8 * k
                        pe.wait_ge(k_loaded[k], 96 * ch + 48 * u + 48)
                        make_logits(n, k, 0)
                        for i in range(2 * A):
                            a, half = i // 2, i % 2
                            if i + 1 < 2 * A:
                                make_logits(n, k, i + 1)
                            if i == 0:
                                pe.wait_ge(aug_ready, GPC * ch + 2 * u + k + 3)
                            pe.wait_ge(phi_ready, n + i + 3)
                            for h in range(HALF * half, HALF * half + HALF):
                                mm = nc.tensor.matmul(parts[0:D + 1, h * M:(h + 1) * M], aug[k][:, a * H + h, :],
                                                      phi[half][:, h % HALF, :], start=False, stop=True,
                                                      skip_group_check=True)
                            mm.then_inc(part_ready, 1)
                pe.wait_ge(sumT_ready, ch + 2)
                hold(pe, phi_ready, 32 * ch + 32 + 2, pace)
                for h in range(H):
                    at = 512 * (h // HALF) + (h % HALF) * (D + 1)
                    mm = nc.tensor.transpose(logits[0][:, at:at + D + 1], sumT[:, h, :],
                                             keep["ident32"][0:D + 1, 0:D + 1])
                mm.then_inc(turned_ready, 1)


def skewed(engine, tile):
    for j in range(3):
        tile(0, j)
    with engine.Fori(0, T // P // 8 - 1) as u:
        for j in range(3, 11):
            tile(u, j)
    for j in range(3, 8):
        tile(T // P // 8 - 1, j)


def attend_stage(nc, io, keep):
    with ExitStack() as ctx:
        t = Tools(nc, ctx, "s4")
        HALF = H // 2
        RING = 4
        LAST = T // P - 1
        qT = [t.sb(f"qT{k}", [96, H, G], F16) for k in range(2)]
        sums = t.pair("sums", [P, 2, H, D + 1], F16)
        largest = t.pair("largest", [P, H])
        weight = t.pair("weight", [P, A, H])
        phi = [t.sb(f"phi{r}", [P, HALF, P]) for r in range(RING)]
        high, low = ([t.sb(f"{n}{r}", [P, HALF, P], F16) for r in range(RING)] for n in ("high", "low"))
        en = t.pair("en", [P, A, 2 * H])
        x = t.pair("x", [P, A, E])
        den = t.sb("den", [P, H])
        ratio = t.sb("ratio", [P, H])
        at = t.sb("at", [P, E])
        atT = t.sb("atT", [P, EC, P])
        z = t.pair("z", [P, E])
        stats, mv, rstd, power = t.sb("stats", [P, 6]), t.sb("mv", [P, 2]), t.sb("rstd", [P, 1]), t.sb("power", [P, 1])
        logits = [t.psum(f"logits{b}", 2) for b in range(2)]
        numer = t.psum("numer", 2)
        turned = t.psum("turned")
        y = t.psum("y")
        q_loaded, s_loaded, x_stored = ([t.sem(f"{n}{k}") for k in range(2)] for n in ("q_loaded", "s_loaded", "x_stored"))
        logits_ready, phi_ready, numer_ready, den_ready, at_ready = (
            t.sem("logits_ready"), t.sem("phi_ready"), t.sem("numer_ready"), t.sem("den_ready"), t.sem("at_ready"))
        turned_ready, atT_ready, y_ready, stats_ready, mv_ready = (
            t.sem("turned_ready"), t.sem("atT_ready"), t.sem("y_ready"), t.sem("stats_ready"), t.sem("mv_ready"))
        rstd_ready, z_ready, x1_ready, power_ready, pace = (
            t.sem("rstd_ready"), t.sem("z_ready"), t.sem("x1_ready"), t.sem("power_ready"), t.sem("pace"))
        var_ready, high_ready, low_ready, weight_ready = (
            t.sem(n) for n in ("var_ready", "high_ready", "low_ready", "weight_ready"))
        block = ctx.enter_context(nc.Block())

        def turn(u, j):
            return u + j // 8, j % 8 // A, j % A

        @block.sync
        def _(sp):
            with nc.sync.Fori(0, C) as ch, nc.sync.Fori(0, GPC // 2) as u:
                for k in range(2):
                    group = bass.ds(GPC * ch + 2 * u + k, 1)
                    hold(sp, logits_ready, 32 * ch + 16 * u + 8 * k + 1, pace)
                    for r, s in enumerate((0, 0, 1)):
                        sp.dma_start(qT[k][32 * r:32 * r + 32],
                                     io["qk"][group, s, 0:E, :].rearrange("o (h d) n -> d (o h) n", d=D)
                                     ).then_inc(q_loaded[k], 16)
                    hold(sp, x_stored[k], 32 * ch + 16 * u + 1, pace)
                    sp.dma_start(sums[k][:].rearrange("p s h d -> p (s h d)"),
                                 io["sums"][bass.ds(ch, 1)].rearrange("o p n -> p (o n)")).then_inc(s_loaded[k], 16)
                    sp.dma_start(largest[k][:], io["largest"][bass.ds(ch, 1)].rearrange("o p h -> p (o h)")
                                 ).then_inc(s_loaded[k], 16)
                    sp.dma_start(en[k][:], io["en"][group].rearrange("o p a h -> p (o a) h")).then_inc(s_loaded[k], 16)
                    sp.dma_start(x[k][:], io["x"][bass.ds((GPC * ch + 2 * u + k) * G, G), :]
                                 .rearrange("(a p) e -> p a e", p=P)).then_inc(s_loaded[k], 16)

        @block.tensor
        def _(pe):
            pe.sem_inc(logits_ready, 9)
            pe.sem_inc(numer_ready, 4)
            pe.sem_inc(turned_ready, 1)
            pe.sem_inc(y_ready, 1)

            def make_logits(u, j, half):
                v, k, a = turn(u, j)
                if a == 0 and half == 0:
                    pe.wait_ge(q_loaded[k], 48 * v + 48)
                pe.wait_ge(phi_ready, 16 * u + 2 * j + half + 1)
                for h in range(HALF):
                    mm = nc.tensor.matmul(logits[half][:, h * P:(h + 1) * P],
                                          keep["feat"][:, HALF * half + h, :],
                                          qT[k][:, HALF * half + h, a * P:(a + 1) * P],
                                          start=True, stop=True)
                mm.then_inc(logits_ready, 1)

            def transpose(u, j):
                pe.wait_ge(at_ready, 8 * u + j + 2)
                pe.wait_ge(atT_ready, 8 * u + j + 1)
                for c in range(EC):
                    mm = nc.tensor.transpose(turned[:, c * P:(c + 1) * P], at[:, c * P:(c + 1) * P], keep["ident32"][:])
                mm.then_inc(turned_ready, 1)

            def project(u, j):
                pe.wait_ge(atT_ready, 8 * u + j + 2)
                pe.wait_ge(z_ready, 8 * u + j + 2)
                for c in range(EC):
                    mm = nc.tensor.matmul(y[:], atT[:, c, :], keep["wo"][:, c, :], start=(c == 0), stop=(c == EC - 1))
                mm.then_inc(y_ready, 1)

            def tile(u, j):
                v, k, a = turn(u, j)
                first, last = isinstance(u, int) and u == 0 and j == 0, isinstance(u, int) and 8 * u + j > LAST - 2
                if not first:
                    transpose(u, j - 1)
                if a == 0:
                    pe.wait_ge(s_loaded[k], 64 * v + 64)
                for half in range(2):
                    if not last:
                        make_logits(u, j + 2, half)
                    if half == 0:
                        pe.wait_ge(at_ready, 8 * u + j + 1)
                    pe.wait_ge(low_ready, 16 * u + 2 * j + half + 5)
                    r = (2 * j + half) % RING
                    for h in range(HALF):
                        out = numer[:, 512 * half + h * (D + 1):512 * half + (h + 1) * (D + 1)]
                        s = sums[k][:, :, HALF * half + h, :]
                        nc.tensor.matmul(out, high[r][:, h, :], s[:, 0], start=True, stop=False)
                        nc.tensor.matmul(out, high[r][:, h, :], s[:, 1], start=False, stop=False)
                        mm = nc.tensor.matmul(out, low[r][:, h, :], s[:, 0], start=False, stop=True)
                    mm.then_inc(numer_ready, 1)
                if not first:
                    project(u, j - 1)

            for i in range(4):
                make_logits(0, i // 2, i % 2)
            skewed(nc.tensor, tile)
            transpose(0, LAST)
            project(0, LAST)

        @block.scalar
        def _(act):
            act.sem_inc(phi_ready, 2)
            act.sem_inc(atT_ready, 1)
            for k in range(2):
                act.sem_inc(x_stored[k], 1)

            def make_phi(u, j, half):
                act.wait_ge(logits_ready, 16 * u + 2 * j + half + 10)
                act.wait_ge(low_ready, 16 * u + 2 * j + half + 1)
                nc.scalar.activation(phi[(2 * j + half) % RING][:].rearrange("p h m -> p (h m)"), logits[half][:],
                                     ACT.Exp, scale=1.0 / M_SCALE).then_inc(phi_ready, 1)

            def copy_turned(u, j):
                act.wait_ge(turned_ready, 8 * u + j + 2)
                act.wait_ge(y_ready, 8 * u + j + 1)
                nc.scalar.activation(atT[:].rearrange("p c q -> p (c q)"), turned[:], ACT.Copy).then_inc(atT_ready, 1)

            def store(u, j):
                v, k, a = turn(u, j)
                act.wait_ge(x1_ready, 8 * u + j + 3)
                act.dma_start(io["x1"][bass.ds((2 * v + k) * G, G), :].rearrange("(a p) e -> p a e", p=P),
                              x[k][:]).then_inc(x_stored[k], 16)

            def tile(u, j):
                first, last = isinstance(u, int) and u == 0 and j == 0, isinstance(u, int) and 8 * u + j > LAST - 2
                if not first:
                    copy_turned(u, j - 1)
                if not last:
                    for half in range(2):
                        make_phi(u, j + 2, half)
                if j % A == 2 and j > A:
                    store(u, j - 3)

            for i in range(4):
                make_phi(0, i // 2, i % 2)
            skewed(nc.scalar, tile)
            copy_turned(0, LAST)
            store(0, LAST)
            for k in range(2):
                act.wait_ge(x_stored[k], 16 * NG // 2 + 1)

        @block.vector
        def _(dve):
            dve.sem_inc(at_ready, 1)
            dve.sem_inc(z_ready, 2)
            dve.sem_inc(den_ready, 1)
            dve.sem_inc(low_ready, RING)

            def split(u, j, half):
                r = (2 * j + half) % RING
                dve.wait_ge(high_ready, 16 * u + 2 * j + half + 1)
                dve.wait_ge(numer_ready, 16 * u + 2 * j + half + 1)
                nc.vector.scalar_tensor_tensor(out=low[r][:], in0=phi[r][:], scalar=F16_MAX, in1=high[r][:],
                                               op0=ALU.min, op1=ALU.subtract).then_inc(low_ready, 1)

            def weigh(u, j):
                v, k, a = turn(u, j)
                dve.wait_ge(s_loaded[k], 64 * v + 64)
                nc.vector.tensor_tensor(weight[k][:], en[k][:, :, 0:H],
                                        largest[k][:].unsqueeze(1).broadcast_to([P, A, H]),
                                        ALU.mult).then_inc(weight_ready, 1)
                dve.wait_ge(weight_ready, 2 * v + k + 1)

            def divide(u, j):
                v, k, a = turn(u, j)
                d0 = 32 * u + 4 * j + 1
                heads = numer[:].rearrange("p (b n) -> p b n", b=2)[:, :, 0:HALF * (D + 1)].rearrange(
                    "p b (h d) -> p b h d", d=D + 1)
                w = weight[k][:, a, :]
                dve.wait_ge(numer_ready, 16 * u + 2 * j + 2 + RING)
                nc.vector.tensor_tensor(den[:].rearrange("p (b h o) -> p b h o", b=2, o=1), heads[:, :, :, D:D + 1],
                                        w.rearrange("p (b h o) -> p b h o", b=2, o=1), ALU.mult).then_inc(den_ready, 1)
                dve.wait_ge(den_ready, d0 + 1)
                nc.vector.tensor_scalar(den[:], den[:], 1e-6, None, ALU.max).then_inc(den_ready, 1)
                dve.wait_ge(den_ready, d0 + 2)
                nc.vector.reciprocal(den[:], den[:]).then_inc(den_ready, 1)
                dve.wait_ge(den_ready, d0 + 3)
                nc.vector.tensor_tensor(ratio[:], den[:], w, ALU.mult).then_inc(den_ready, 1)
                dve.wait_ge(den_ready, d0 + 4)
                dve.wait_ge(turned_ready, 8 * u + j + 1)
                nc.vector.tensor_tensor(at[:].rearrange("p (b h d) -> p b h d", b=2, d=D), heads[:, :, :, 0:D],
                                        ratio[:].rearrange("p (b h) -> p b h", b=2).unsqueeze(3)
                                        .broadcast_to([P, 2, HALF, D]), ALU.mult).then_inc(at_ready, 1)

            def normalize(u, j):
                dve.wait_ge(y_ready, 8 * u + j + 2)
                nc.vector.bn_stats(stats[:], y[:]).then_inc(stats_ready, 1)
                hold(dve, stats_ready, 8 * u + j + 1, pace)
                nc.vector.bn_aggr(mv[:], stats[:]).then_inc(mv_ready, 1)
                dve.wait_ge(rstd_ready, 8 * u + j + 1)
                dve.wait_ge(x1_ready, 8 * u + j + 1)
                nc.vector.tensor_scalar(z[j % 2][:], y[:], mv[:, 0:1], rstd[:], ALU.subtract,
                                        ALU.mult).then_inc(z_ready, 1)

            def tile(u, j):
                first, last = isinstance(u, int) and u == 0 and j == 0, isinstance(u, int) and 8 * u + j == LAST
                if not last:
                    for half in range(2):
                        split(u, j + 1, half)
                if j % A == 0:
                    weigh(u, j)
                divide(u, j)
                if not first:
                    normalize(u, j - 1)

            for half in range(2):
                split(0, 0, half)
            skewed(nc.vector, tile)
            normalize(0, LAST)

        @block.gpsimd
        def _(pool):
            nc.gpsimd.memset(power[:], -0.5).then_inc(power_ready, 1)
            pool.wait_ge(power_ready, 1)
            pool.sem_inc(x1_ready, 2)

            def make_high(u, j, half):
                r = (2 * j + half) % RING
                hold(pool, phi_ready, 16 * u + 2 * j + half + 3, pace)
                hold(pool, numer_ready, 16 * u + 2 * j + half + 1, pace)
                nc.gpsimd.tensor_scalar(high[r][:], phi[r][:], F16_MAX, None, ALU.min).then_inc(high_ready, 1)

            def residual(u, j):
                v, k, a = turn(u, j)
                hold(pool, mv_ready, 8 * u + j + 1, pace)
                nc.gpsimd.tensor_scalar(rstd[:], mv[:, 1:2], 1e-5, None, ALU.add).then_inc(var_ready, 1)
                pool.wait_ge(var_ready, 8 * u + j + 1)
                nc.gpsimd.tensor_tensor(rstd[:], rstd[:], power[:], ALU.pow).then_inc(rstd_ready, 1)
                pool.wait_ge(z_ready, 8 * u + j + 3)
                pool.wait_ge(s_loaded[k], 64 * v + 64)
                nc.gpsimd.tensor_tensor(x[k][:, a, :], x[k][:, a, :], z[j % 2][:], ALU.add).then_inc(x1_ready, 1)

            def tile(u, j):
                first, last = isinstance(u, int) and u == 0 and j == 0, isinstance(u, int) and 8 * u + j > LAST - 2
                if not last:
                    for half in range(2):
                        make_high(u, j + 2, half)
                if not first:
                    residual(u, j - 1)

            for i in range(4):
                make_high(0, i // 2, i % 2)
            skewed(nc.gpsimd, tile)
            residual(0, LAST)


def route_stage(nc, io, keep):
    with ExitStack() as ctx:
        t = Tools(nc, ctx, "s6")
        xT = t.pair("xT", [P, 2, EC, G], F16)
        token = t.pair("token", [P, A], U32)
        slots = t.pair("slots", [P, A * K], U32)
        weights = t.pair("weights", [P, A, K])
        score, biased = t.sb("score", [P, A, NE]), t.sb("biased", [P, A, NE])
        top, index, chosen = t.sb("top", [P, A, 8]), t.sb("index", [P, A, 8], U32), t.sb("chosen", [P, A, K])
        onehot, picked = t.sb("onehot", [P, A, K, NE]), t.sb("picked", [P, A, K, NE])
        mask = t.sb("mask", [P, A, NE], F16)
        before, ours = t.sb("before", [P, NE], F16), t.sb("ours", [P, NE])
        slot, far, place = t.sb("slot", [P, A, NE]), t.sb("far", [P, A, NE]), t.sb("place", [P, A, K])
        w, total = t.sb("w", [P, A, K]), t.sb("total", [P, A])
        logits = [t.psum(f"logits{k}") for k in range(2)]
        position = t.psum("position")
        x_loaded, token_loaded, scattered, slots_stored, weights_stored = (
            [t.sem(f"{n}{k}") for k in range(2)]
            for n in ("x_loaded", "token_loaded", "scattered", "slots_stored", "weights_stored"))
        logits_ready, score_ready, position_ready, mask_ready, step, slots_ready, sent, pace = (
            t.sem(n) for n in ("logits_ready", "score_ready", "position_ready", "mask_ready", "step", "slots_ready",
                               "sent", "pace"))
        STEPS = 19
        block = ctx.enter_context(nc.Block())

        @block.sync
        def _(sp):
            with nc.sync.Fori(0, NG // 2) as u:
                for k in range(2):
                    hold(sp, logits_ready, 2 * u + k + 1, pace)
                    sp.dma_start(xT[k][:].rearrange("p s c q -> p (s c q)"),
                                 io["xT2"][bass.ds(2 * u + k, 1)].rearrange("o p n -> p (o n)")).then_inc(x_loaded[k], 16)
                    hold(sp, sent, 2 * u + k + 1, pace)
                    sp.dma_start(token[k][:], io["token"][bass.ds(2 * u + k, 1)].rearrange("o p a -> p (o a)")
                                 ).then_inc(token_loaded[k], 16)

        @block.tensor
        def _(pe):
            pe.sem_inc(logits_ready, 2)
            with nc.tensor.Fori(0, NG // 2) as u:
                for k in range(2):
                    pe.wait_ge(x_loaded[k], 16 * u + 16)
                    pe.wait_ge(score_ready, 2 * u + k + 1)
                    for a in range(A):
                        for c in range(EC):
                            for s in range(2):
                                mm = nc.tensor.matmul(logits[k][:, a * NE:(a + 1) * NE],
                                                      xT[k][:, s, c, a * P:(a + 1) * P],
                                                      keep["gate"][:, c * NE:(c + 1) * NE],
                                                      start=(c == 0 and s == 0), stop=(c == EC - 1 and s == 1))
                    mm.then_inc(logits_ready, 1)
                    pe.wait_ge(mask_ready, 2 * u + k + 2)
                    for a in range(A):
                        out = position[:, a * NE:(a + 1) * NE]
                        nc.tensor.matmul(out, keep["tri"][:], mask[:, a, :], start=True, stop=False)
                        for b in range(a):
                            nc.tensor.matmul(out, keep["ones"][:], mask[:, b, :], start=False, stop=False)
                        mm = nc.tensor.matmul(out, keep["ones"][:], before[:], start=False, stop=True)
                    mm.then_inc(position_ready, 1)

        @block.scalar
        def _(act):
            act.sem_inc(score_ready, 2)
            for k in range(2):
                act.sem_inc(slots_stored[k], 1)
                act.sem_inc(weights_stored[k], 1)
            with nc.scalar.Fori(0, NG // 2) as u:
                for k in range(2):
                    act.wait_ge(logits_ready, 2 * u + k + 3)
                    act.wait_ge(slots_ready, 2 * u + k + 1)
                    nc.scalar.activation(score[:].rearrange("p a e -> p (a e)"), logits[k][:, 0:A * NE],
                                         ACT.Sigmoid).then_inc(score_ready, 1)
                    act.wait_ge(slots_ready, 2 * u + k + 2)
                    act.dma_start(io["slots"][bass.ds(2 * u + k, 1)].rearrange("o p n -> p (o n)"),
                                  slots[k][:]).then_inc(slots_stored[k], 16)
                    act.dma_start(io["weights"][bass.ds(2 * u + k, 1)].rearrange("o p n -> p (o n)"),
                                  weights[k][:].rearrange("p a j -> p (a j)")).then_inc(weights_stored[k], 16)
            for k in range(2):
                act.wait_ge(slots_stored[k], 16 * NG // 2 + 1)
                act.wait_ge(weights_stored[k], 16 * NG // 2 + 1)

        @block.vector
        def _(dve):
            nc.vector.memset(before[:], 0.0).then_inc(mask_ready, 1)
            dve.wait_ge(mask_ready, 1)
            dve.sem_inc(slots_ready, 1)
            dve.sem_inc(step, 1)
            number = keep["expert"][:, 0:NE].unsqueeze(1).unsqueeze(1).broadcast_to([P, A, K, NE])
            first = keep["expert"][:, NE:2 * NE].unsqueeze(1).broadcast_to([P, A, NE])
            bias = keep["bias"][:].unsqueeze(1).broadcast_to([P, A, NE])

            def per_choice(x):
                return x.unsqueeze(2).broadcast_to([P, A, K, NE])

            with nc.vector.Fori(0, NG // 2) as u:
                for k in range(2):
                    done = [2 * STEPS * u + STEPS * k + 1]

                    def then(ins):
                        ins.then_inc(step, 1)
                        done[0] = done[0] + 1
                        hold(dve, step, done[0], pace)

                    dve.wait_ge(score_ready, 2 * u + k + 3)
                    then(nc.vector.tensor_tensor(biased[:], score[:], bias, ALU.add))
                    for a in range(A):
                        ins = nc.vector.max(top[:, a, :], biased[:, a, :])
                    then(ins)
                    for a in range(A):
                        ins = nc.vector.max_index(index[:, a, :], top[:, a, :], biased[:, a, :])
                    then(ins)
                    then(nc.vector.tensor_copy(chosen[:], index[:, :, 0:K]))
                    then(nc.vector.tensor_tensor(onehot[:], number, chosen[:].unsqueeze(3).broadcast_to([P, A, K, NE]),
                                                 ALU.is_equal))
                    with nc.allow_low_precision(reason="sums of zeros and one 1"):
                        ins = nc.vector.tensor_reduce(mask[:], onehot[:].rearrange("p a j e -> p a e j"), AX.X, ALU.add)
                    ins.then_inc(mask_ready, 1)
                    then(nc.vector.tensor_tensor(picked[:], onehot[:], per_choice(score[:]), ALU.mult))
                    then(nc.vector.tensor_reduce(w[:], picked[:], AX.X, ALU.add))
                    then(nc.vector.tensor_reduce(total[:], w[:], AX.X, ALU.add))
                    then(nc.vector.tensor_scalar(total[:], total[:], 1e-12, None, ALU.max))
                    then(nc.vector.reciprocal(total[:], total[:]))
                    then(nc.vector.tensor_tensor(w[:], w[:], total[:].unsqueeze(2).broadcast_to([P, A, K]), ALU.mult))
                    dve.wait_ge(position_ready, 2 * u + k + 1)
                    then(nc.vector.tensor_reduce(ours[:], mask[:].rearrange("p a e -> p e a"), AX.X, ALU.add))
                    then(nc.vector.tensor_tensor(before[:], before[:], ours[:], ALU.add))
                    where = position[:, 0:A * NE].rearrange("p (a e) -> p a e", e=NE)
                    then(nc.vector.tensor_scalar(far[:], where, float(CAP), NOWHERE, ALU.is_ge, ALU.mult))
                    then(nc.vector.tensor_tensor(slot[:], where, first, ALU.add))
                    then(nc.vector.tensor_tensor(slot[:], slot[:], far[:], ALU.add))
                    then(nc.vector.tensor_tensor(picked[:], onehot[:], per_choice(slot[:]), ALU.mult))
                    then(nc.vector.tensor_reduce(place[:], picked[:], AX.X, ALU.add))
                    dve.wait_ge(weights_stored[k], 16 * u + 1)
                    then(nc.vector.scalar_tensor_tensor(out=weights[k][:], in0=place[:], scalar=NOWHERE / 2, in1=w[:],
                                                        op0=ALU.is_lt, op1=ALU.mult))
                    dve.wait_ge(slots_stored[k], 16 * u + 1)
                    dve.wait_ge(sent, 2 * u + k + 1)
                    ins = nc.vector.tensor_copy(slots[k][:], place[:].rearrange("p a j -> p (a j)"))
                    ins.then_inc(slots_ready, 1)
                    dve.wait_ge(slots_ready, 2 * u + k + 2)

        @block.gpsimd
        def _(pool):
            pool.sem_inc(sent, 2)
            with nc.gpsimd.Fori(0, NG // 2) as u:
                for k in range(2):
                    hold(pool, token_loaded[k], 16 * u + 16, pace)
                    hold(pool, slots_ready, 2 * u + k + 2, pace)
                    for a in range(A):
                        for j in range(K):
                            nc.gpsimd.indirect_dma_start(
                                out=io["slot_token"],
                                out_offset=bass.IndirectOffsetOnAxis(ap=slots[k][:, a * K + j:a * K + j + 1], axis=0),
                                in_=token[k][:, a:a + 1], in_offset=None, bounds_check=NSLOT - 1, oob_is_err=False,
                            ).then_inc(scattered[k], 16)
                    hold(pool, scattered[k], 16 * A * K * (u + 1), pace)
                    pool.sem_inc(sent, 1)


def expert_stage(nc, io, keep):
    with ExitStack() as ctx:
        t = Tools(nc, ctx, "s7")
        IC = I // P
        w1, w3 = (t.pair(n, [P, EC, I], BF16) for n in ("w1", "w3"))
        w2 = t.pair("w2", [P, IC, E], BF16)
        token = t.pair("token", [P, A], U32)
        rows = t.pair("rows", [P, A, 2 * E], F16)
        xT = t.pair("xT", [P, 2, EC, G], F16)
        gate, h = t.pair("gate", [P, G]), t.pair("h", [P, G])
        parts = t.pair("parts", [P, IC, 3, G], BF16)
        y = t.pair("y", [P, A, E])
        turned = [t.psum(f"turned{b}") for b in range(2)]
        gates = [t.psum(f"gates{b}") for b in range(2)]
        ups = [t.psum(f"ups{b}") for b in range(2)]
        ys = [t.psum(f"ys{b}") for b in range(2)]
        w_loaded, w2_loaded, token_loaded, gathered, stored = (
            [t.sem(f"{n}{k}") for k in range(2)] for n in ("w_loaded", "w2_loaded", "token_loaded", "gathered", "stored"))
        turned_ready, xT_ready, up_ready, gate_ready, h_ready, high_ready, middle_ready, low_ready = (
            t.sem(n) for n in ("turned_ready", "xT_ready", "up_ready", "gate_ready", "h_ready", "high_ready",
                               "middle_ready", "low_ready"))
        rest_ready, y_ready, y_copied, pace = t.sem("rest_ready"), t.sem("y_ready"), t.sem("y_copied"), t.sem("pace")
        dst = io["ye"].rearrange("(n p a) e -> n p a e", a=A, p=P)
        ids = io["slot_token"].rearrange("(n p a) o -> n p (a o)", p=P, a=A)
        block = ctx.enter_context(nc.Block())

        @block.sync
        def _(sp):
            with nc.sync.Fori(0, NE // 2) as u:
                for k in range(2):
                    e = bass.ds(2 * u + k, 1)
                    hold(sp, up_ready, 4 * u + 2 * k + 1, pace)
                    for w, name in ((w1, "W1"), (w3, "W3")):
                        sp.dma_start(w[k][:], io[name][e].rearrange("o (c p) i -> p (o c) i", p=P)
                                     ).then_inc(w_loaded[k], 16)
                    hold(sp, y_ready, 8 * u + 4 * k + 1, pace)
                    sp.dma_start(w2[k][:], io["W2"][e].rearrange("o (c p) i -> p (o c) i", p=P)
                                 ).then_inc(w2_loaded[k], 16)

        @block.gpsimd
        def _(pool):
            with nc.gpsimd.Fori(0, NE // 2) as u:
                for k in range(2):
                    hold(pool, turned_ready, 8 * u + 4 * k + 1, pace)
                    pool.dma_start(token[k][:], ids[bass.ds(2 * u + k, 1)].rearrange("o p a -> p (o a)")
                                   ).then_inc(token_loaded[k], 16)
                    hold(pool, token_loaded[k], 16 * u + 16, pace)
                    for a in range(A):
                        nc.gpsimd.indirect_dma_start(
                            out=rows[k][:, a, :], out_offset=None, in_=io["rows"],
                            in_offset=bass.IndirectOffsetOnAxis(ap=token[k][:, a:a + 1], axis=0),
                            bounds_check=T - 1, oob_is_err=False).then_inc(gathered[k], 16)

        @block.tensor
        def _(pe):
            pe.sem_inc(turned_ready, 5)
            pe.sem_inc(up_ready, 3)
            pe.sem_inc(y_ready, 5)

            def turn(u, k, a):
                if a == 0:
                    pe.wait_ge(gathered[k], 16 * A * u + 16 * A)
                pe.wait_ge(xT_ready, 8 * u + 4 * k + a + 1)
                for s in range(2):
                    for c in range(EC):
                        mm = nc.tensor.transpose(
                            turned[a % 2][:].bitcast(F16)[:, (s * EC + c) * P:(s * EC + c + 1) * P],
                            rows[k][:, a, (s * EC + c) * P:(s * EC + c + 1) * P], keep["ident16"][:])
                mm.then_inc(turned_ready, 1)

            def up(u, k):
                pe.wait_ge(xT_ready, 8 * u + 4 * k + 4 + 2)
                pe.wait_ge(w_loaded[k], 32 * u + 32)
                for i in range(IC):
                    pe.wait_ge(h_ready, 4 * u + 2 * k + i + 1)
                    for bank, w in ((gates[i], w1[k]), (ups[i], w3[k])):
                        for c in range(EC):
                            for s in range(2):
                                mm = nc.tensor.matmul(bank[:], w[:, c, i * P:(i + 1) * P], xT[k][:, s, c, :],
                                                      start=(c == 0 and s == 0), stop=(c == EC - 1 and s == 1))
                    mm.then_inc(up_ready, 1)

            def down(u, k, a):
                if a == 0:
                    pe.wait_ge(low_ready, 4 * u + 2 * k + 2)
                    pe.wait_ge(w2_loaded[k], 16 * u + 16)
                pe.wait_ge(y_copied, 8 * u + 4 * k + a + 1)
                for i in range(IC):
                    for s in range(3):
                        mm = nc.tensor.matmul(ys[a % 2][:], parts[k][:, i, s, a * P:(a + 1) * P], w2[k][:, i, :],
                                              start=(i == 0 and s == 0), stop=(i == IC - 1 and s == 2))
                mm.then_inc(y_ready, 1)

            for a in range(A):
                turn(0, 0, a)
            up(0, 0)
            for a in range(A):
                turn(0, 1, a)
            with nc.tensor.Fori(0, NE // 2 - 1) as u:
                up(u, 1)
                for a in range(A):
                    down(u, 0, a)
                    turn(u + 1, 0, a)
                up(u + 1, 0)
                for a in range(A):
                    down(u, 1, a)
                    turn(u + 1, 1, a)
            up(NE // 2 - 1, 1)
            for k in range(2):
                for a in range(A):
                    down(NE // 2 - 1, k, a)

        @block.scalar
        def _(act):
            act.sem_inc(xT_ready, 2)
            for k in range(2):
                act.sem_inc(stored[k], 1)

            def turn(u, k):
                act.wait_ge(up_ready, 4 * u + 2 * k + 1)
                for a in range(A):
                    act.wait_ge(turned_ready, 8 * u + 4 * k + a + 6)
                    nc.scalar.activation(
                        xT[k][:, :, :, a * P:(a + 1) * P],
                        turned[a % 2][:].bitcast(F16).rearrange("p (s c q) -> p s c q", s=2, c=EC),
                        ACT.Copy).then_inc(xT_ready, 1)

            def up(u, k):
                for i in range(IC):
                    n = 4 * u + 2 * k + i
                    act.wait_ge(up_ready, n + 4)
                    act.wait_ge(h_ready, n + 1)
                    nc.scalar.activation(gate[i][:], gates[i][:], ACT.Silu).then_inc(gate_ready, 1)
                    if i == 0:
                        act.wait_ge(y_ready, 8 * u + 4 * k + 1)
                    act.wait_ge(h_ready, n + 3)
                    nc.scalar.activation(parts[k][:, i, 0, :], h[i][:], ACT.Copy).then_inc(high_ready, 1)
                    act.wait_ge(rest_ready, n + 1)
                    nc.scalar.activation(parts[k][:, i, 1, :], h[i][:], ACT.Copy).then_inc(middle_ready, 1)

            def store(u, k):
                act.wait_ge(y_copied, 8 * u + 4 * k + 4 + 2)
                act.dma_start(dst[bass.ds(2 * u + k, 1)].rearrange("o p a e -> p (o a) e"),
                              y[k][:]).then_inc(stored[k], 16)

            turn(0, 0)
            up(0, 0)
            turn(0, 1)
            with nc.scalar.Fori(0, NE // 2 - 1) as u:
                up(u, 1)
                turn(u + 1, 0)
                store(u, 0)
                up(u + 1, 0)
                turn(u + 1, 1)
                store(u, 1)
            up(NE // 2 - 1, 1)
            for k in range(2):
                store(NE // 2 - 1, k)
            for k in range(2):
                act.wait_ge(stored[k], 16 * NE // 2 + 1)

        @block.vector
        def _(dve):
            dve.sem_inc(h_ready, 2)
            dve.sem_inc(y_copied, 2)

            def up(u, k):
                for i in range(IC):
                    n = 4 * u + 2 * k + i
                    dve.wait_ge(gate_ready, n + 1)
                    nc.vector.tensor_tensor(h[i][:], gate[i][:], ups[i][:], ALU.mult).then_inc(h_ready, 1)
                    dve.wait_ge(high_ready, n + 1)
                    nc.vector.tensor_tensor(h[i][:], h[i][:], parts[k][:, i, 0, :], ALU.subtract).then_inc(rest_ready, 1)
                    dve.wait_ge(middle_ready, n + 1)
                    nc.vector.tensor_tensor(parts[k][:, i, 2, :], h[i][:], parts[k][:, i, 1, :],
                                            ALU.subtract).then_inc(low_ready, 1)

            def down(u, k):
                dve.wait_ge(stored[k], 16 * u + 1)
                for a in range(A):
                    dve.wait_ge(y_ready, 8 * u + 4 * k + a + 6)
                    nc.vector.tensor_copy(y[k][:, a, :], ys[a % 2][:]).then_inc(y_copied, 1)

            up(0, 0)
            with nc.vector.Fori(0, NE // 2 - 1) as u:
                up(u, 1)
                down(u, 0)
                up(u + 1, 0)
                down(u, 1)
            up(NE // 2 - 1, 1)
            down(NE // 2 - 1, 0)
            down(NE // 2 - 1, 1)


def combine_stage(nc, io, keep):
    with ExitStack() as ctx:
        t = Tools(nc, ctx, "s8")
        IC = I // P
        w1, w3, w2 = t.sb("w1", [P, EC, I], BF16), t.sb("w3", [P, EC, I], BF16), t.sb("w2", [P, IC, E], BF16)
        xT = t.pair("xT", [P, 2, EC, G], F16)
        gate, h = t.pair("gate", [P, G]), t.pair("h", [P, G])
        parts = t.pair("parts", [P, IC, 3, G], BF16)
        slots = t.pair("slots", [P, A * K], U32)
        weights = t.pair("weights", [P, A * K])
        total = t.pair("total", [P, A, E])
        x1 = t.pair("x1", [P, A, E])
        picked = [t.sb(f"picked{b}", [P, K, E]) for b in range(2)]
        stats, mv = t.sb("stats", [P, A, 6]), t.sb("mv", [P, A, 2])
        var, root, rstd, fix, shift = (t.sb(n, [P, A]) for n in ("var", "root", "rstd", "fix", "shift"))
        gates = [t.psum(f"gates{b}") for b in range(2)]
        ups = [t.psum(f"ups{b}") for b in range(2)]
        ys = [t.psum(f"ys{b}") for b in range(2)]
        w_loaded = t.sem("w_loaded")
        x_loaded, s_loaded, loaded, gathered, out_stored = (
            [t.sem(f"{n}{k}") for k in range(2)] for n in ("x_loaded", "s_loaded", "loaded", "gathered", "out_stored"))
        up_ready, gate_ready, h_ready, high_ready, rest_ready, middle_ready, low_ready, y_ready, y_used = (
            t.sem(n) for n in ("up_ready", "gate_ready", "h_ready", "high_ready", "rest_ready", "middle_ready",
                               "low_ready", "y_ready", "y_used"))
        cleared, summed, stats_ready, step, var_ready, root_ready, z_ready, out_ready, pace = (
            t.sem(n) for n in ("cleared", "summed", "stats_ready", "step", "var_ready", "root_ready", "z_ready",
                               "out_ready", "pace"))
        STEPS = 7
        block = ctx.enter_context(nc.Block())

        @block.sync
        def _(sp):
            sp.dma_start(w1[:], io["sw1"].rearrange("(c p) i -> p c i", p=P)).then_inc(w_loaded, 16)
            sp.dma_start(w3[:], io["sw3"].rearrange("(c p) i -> p c i", p=P)).then_inc(w_loaded, 16)
            sp.dma_start(w2[:], io["sw2"].rearrange("(c p) i -> p c i", p=P)).then_inc(w_loaded, 16)
            with nc.sync.Fori(0, NG // 2) as u:
                for k in range(2):
                    g = bass.ds(2 * u + k, 1)
                    rows = bass.ds((2 * u + k) * G, G)
                    hold(sp, up_ready, 4 * u + 2 * k + 1, pace)
                    sp.dma_start(xT[k][:].rearrange("p s c q -> p (s c q)"),
                                 io["xT2"][g].rearrange("o p n -> p (o n)")).then_inc(x_loaded[k], 16)
                    hold(sp, out_stored[k], 16 * u + 1, pace)
                    sp.dma_start(slots[k][:], io["slots"][g].rearrange("o p n -> p (o n)")).then_inc(s_loaded[k], 16)
                    sp.dma_start(weights[k][:], io["weights"][g].rearrange("o p n -> p (o n)")).then_inc(loaded[k], 16)
                    sp.dma_start(x1[k][:], io["x1"][rows, :].rearrange("(a p) e -> p a e", p=P)).then_inc(loaded[k], 16)

        @block.gpsimd
        def _(pool):
            pool.wait_ge(cleared, 2)
            with nc.gpsimd.Fori(0, NG // 2) as u:
                for k in range(2):
                    hold(pool, s_loaded[k], 16 * u + 16, pace)
                    for a in range(A):
                        hold(pool, summed, (2 * u + k) * A * K + a * K + 1, pace)
                        for j in range(K):
                            nc.gpsimd.indirect_dma_start(
                                out=picked[a % 2][:, j, :], out_offset=None, in_=io["ye"],
                                in_offset=bass.IndirectOffsetOnAxis(ap=slots[k][:, a * K + j:a * K + j + 1], axis=0),
                                bounds_check=NSLOT - 1, oob_is_err=False).then_inc(gathered[a % 2], 16)

        @block.tensor
        def _(pe):
            pe.sem_inc(up_ready, 3)
            pe.wait_ge(w_loaded, 48)

            def up(u, k):
                pe.wait_ge(x_loaded[k], 16 * u + 16)
                for i in range(IC):
                    pe.wait_ge(h_ready, 4 * u + 2 * k + i + 1)
                    for bank, w in ((gates[i], w1), (ups[i], w3)):
                        for c in range(EC):
                            for s in range(2):
                                mm = nc.tensor.matmul(bank[:], w[:, c, i * P:(i + 1) * P], xT[k][:, s, c, :],
                                                      start=(c == 0 and s == 0), stop=(c == EC - 1 and s == 1))
                    mm.then_inc(up_ready, 1)

            def down(u, k):
                pe.wait_ge(low_ready, 4 * u + 2 * k + 2)
                for a in range(A):
                    pe.wait_ge(y_used, 8 * u + 4 * k + a + 1)
                    for i in range(IC):
                        for s in range(3):
                            mm = nc.tensor.matmul(ys[a % 2][:], parts[k][:, i, s, a * P:(a + 1) * P], w2[:, i, :],
                                                  start=(i == 0 and s == 0), stop=(i == IC - 1 and s == 2))
                    mm.then_inc(y_ready, 1)

            up(0, 0)
            with nc.tensor.Fori(0, NG // 2 - 1) as u:
                up(u, 1)
                down(u, 0)
                up(u + 1, 0)
                down(u, 1)
            up(NG // 2 - 1, 1)
            down(NG // 2 - 1, 0)
            down(NG // 2 - 1, 1)

        @block.scalar
        def _(act):
            for k in range(2):
                act.sem_inc(out_stored[k], 1)

            def up(u, k):
                for i in range(IC):
                    n = 4 * u + 2 * k + i
                    act.wait_ge(up_ready, n + 4)
                    act.wait_ge(h_ready, n + 1)
                    nc.scalar.activation(gate[i][:], gates[i][:], ACT.Silu).then_inc(gate_ready, 1)
                    act.wait_ge(h_ready, n + 3)
                    nc.scalar.activation(parts[k][:, i, 0, :], h[i][:], ACT.Copy).then_inc(high_ready, 1)
                    act.wait_ge(rest_ready, n + 1)
                    nc.scalar.activation(parts[k][:, i, 1, :], h[i][:], ACT.Copy).then_inc(middle_ready, 1)

            def down(u, k):
                act.wait_ge(var_ready, 2 * u + k + 1)
                nc.scalar.activation(root[:], var[:], ACT.Sqrt).then_inc(root_ready, 1)
                act.wait_ge(step, STEPS * (2 * u + k) + STEPS)
                for a in range(A):
                    ins = nc.scalar.activation(total[k][:, a, :], total[k][:, a, :], ACT.Identity,
                                               bias=shift[:, a:a + 1], scale=rstd[:, a:a + 1])
                ins.then_inc(z_ready, 1)

            def store(u, k):
                act.wait_ge(out_ready, 2 * u + k + 1)
                act.dma_start(io["out"][bass.ds((2 * u + k) * G, G), :].rearrange("(a p) e -> p a e", p=P),
                              x1[k][:]).then_inc(out_stored[k], 16)

            up(0, 0)
            with nc.scalar.Fori(0, NG // 2 - 1) as u:
                up(u, 1)
                down(u, 0)
                store(u, 0)
                up(u + 1, 0)
                down(u, 1)
                store(u, 1)
            up(NG // 2 - 1, 1)
            for k in range(2):
                down(NG // 2 - 1, k)
                store(NG // 2 - 1, k)
            for k in range(2):
                act.wait_ge(out_stored[k], 16 * NG // 2 + 1)

        @block.vector
        def _(dve):
            for b in range(2):
                nc.vector.memset(picked[b][:].rearrange("p j e -> p (j e)"), 0.0).then_inc(cleared, 1)
            dve.wait_ge(cleared, 2)
            dve.sem_inc(summed, K + 1)
            dve.sem_inc(h_ready, 2)
            dve.sem_inc(y_used, 2)

            def up(u, k):
                for i in range(IC):
                    n = 4 * u + 2 * k + i
                    dve.wait_ge(gate_ready, n + 1)
                    nc.vector.tensor_tensor(h[i][:], gate[i][:], ups[i][:], ALU.mult).then_inc(h_ready, 1)
                    dve.wait_ge(high_ready, n + 1)
                    nc.vector.tensor_tensor(h[i][:], h[i][:], parts[k][:, i, 0, :], ALU.subtract).then_inc(rest_ready, 1)
                    dve.wait_ge(middle_ready, n + 1)
                    nc.vector.tensor_tensor(parts[k][:, i, 2, :], h[i][:], parts[k][:, i, 1, :],
                                            ALU.subtract).then_inc(low_ready, 1)

            def down(u, k):
                g = 2 * u + k
                dve.wait_ge(loaded[k], 32 * u + 32)
                dve.wait_ge(out_stored[k], 16 * u + 1)
                for a in range(A):
                    dve.wait_ge(gathered[a % 2], g * (A // 2) * K * 16 + (a // 2 + 1) * K * 16)
                    for j in range(K):
                        if j == 0:
                            dve.wait_ge(y_ready, 4 * g + a + 1)
                        ins = nc.vector.scalar_tensor_tensor(
                            out=total[k][:, a, :], in0=picked[a % 2][:, j, :],
                            scalar=weights[k][:, a * K + j:a * K + j + 1],
                            in1=ys[a % 2][:] if j == 0 else total[k][:, a, :], op0=ALU.mult, op1=ALU.add)
                        ins.then_inc(summed, 1)
                        hold(dve, summed, (g * A + a) * K + j + 1 + K + 1, pace)
                        if j == 0:
                            dve.sem_inc(y_used, 1)
                    ins = nc.vector.bn_stats(stats[:, a, :], total[k][:, a, :])
                ins.then_inc(stats_ready, 1)
                hold(dve, stats_ready, g + 1, pace)
                for a in range(A):
                    ins = nc.vector.bn_aggr(mv[:, a, :], stats[:, a, :])
                ins.then_inc(step, 1)
                dve.wait_ge(step, STEPS * g + 1)
                nc.vector.tensor_scalar(var[:], mv[:, :, 1], 1e-5, None, ALU.add).then_inc(var_ready, 1)
                dve.wait_ge(root_ready, g + 1)
                nc.vector.reciprocal(rstd[:], root[:]).then_inc(step, 1)
                dve.wait_ge(step, STEPS * g + 2)
                nc.vector.tensor_tensor(fix[:], rstd[:], rstd[:], ALU.mult).then_inc(step, 1)
                dve.wait_ge(step, STEPS * g + 3)
                nc.vector.tensor_tensor(fix[:], fix[:], var[:], ALU.mult).then_inc(step, 1)
                dve.wait_ge(step, STEPS * g + 4)
                nc.vector.tensor_scalar(fix[:], fix[:], -0.5, 1.5, ALU.mult, ALU.add).then_inc(step, 1)
                dve.wait_ge(step, STEPS * g + 5)
                nc.vector.tensor_tensor(rstd[:], rstd[:], fix[:], ALU.mult).then_inc(step, 1)
                dve.wait_ge(step, STEPS * g + 6)
                nc.vector.scalar_tensor_tensor(out=shift[:], in0=mv[:, :, 0], scalar=-1.0, in1=rstd[:], op0=ALU.mult,
                                               op1=ALU.mult).then_inc(step, 1)
                dve.wait_ge(z_ready, g + 1)
                nc.vector.tensor_tensor(x1[k][:], x1[k][:], total[k][:], ALU.add).then_inc(out_ready, 1)

            up(0, 0)
            with nc.vector.Fori(0, NG // 2 - 1) as u:
                up(u, 1)
                down(u, 0)
                up(u + 1, 0)
                down(u, 1)
            up(NG // 2 - 1, 1)
            down(NG // 2 - 1, 0)
            down(NG // 2 - 1, 1)


SCRATCH = {
    "xT": ([NG, P, 2 * EC * G], F16),
    "qk": ([NG, 2, 2 * E, G], F16),
    "v": ([NG, P, A, E], F32),
    "en": ([NG, P, A, 2 * H], F32),
    "sums": ([C, P, 2 * H * (D + 1)], F16),
    "largest": ([C, P, H], F32),
    "x1": ([T, E], F32),
    "xT2": ([NG, P, 2 * EC * G], F16),
    "rows": ([T, 2 * E], F16),
    "slot_token": ([NSLOT, 1], U32),
    "slots": ([NG, P, A * K], U32),
    "weights": ([NG, P, A * K], F32),
    "ye": ([NSLOT, E], F32),
}
CONSTS = {
    "ident16": ([P, P], F16), "ident32": ([P, P], F32), "heads": ([P, 2 * EC * 2 * H], F32),
    "tri": ([P, P], F16), "ones": ([P, P], F16), "gate": ([P, EC * NE], BF16), "expert": ([P, 2 * NE], F32),
    "bias": ([P, NE], F32),
}


def build(nc, io, stages=None, debug=()):
    for name, (shape, dt) in SCRATCH.items():
        kind = "ExternalOutput" if name in debug else "Internal"
        io[name] = nc.dram_tensor(f"{name}_dram", shape, dt, kind=kind).ap()
    with ExitStack() as ctx:
        keep = {n: ctx.enter_context(nc.sbuf_tensor(f"keep_{n}", s, d)) for n, (s, d) in CONSTS.items()}
        keep["wqkv"] = ctx.enter_context(nc.sbuf_tensor("keep_wqkv", [P, 2, EC, 3 * E], F16))
        keep["wo"] = ctx.enter_context(nc.sbuf_tensor("keep_wo", [P, EC, E], F32))
        keep["feat"] = ctx.enter_context(nc.sbuf_tensor("keep_feat", [96, H, M], F16))
        todo = [
            lambda: setup_stage(nc, io, keep),
            lambda: norm_stage(nc, io, keep, "s1", io["x"], io["xT"], None),
            lambda: project_stage(nc, io, keep),
            lambda: sums_stage(nc, io, keep),
            lambda: attend_stage(nc, io, keep),
            lambda: norm_stage(nc, io, keep, "s5", io["x1"], io["xT2"], io["rows"]),
            lambda: route_stage(nc, io, keep),
            lambda: expert_stage(nc, io, keep),
            lambda: combine_stage(nc, io, keep),
        ]
        for f in todo[:stages]:
            f()


def shape_constants():
    import numpy as np

    had = np.ones((1, 1), np.float32)
    while had.shape[0] < HP:
        had = np.block([[had, had], [had, -had]])
    d = np.arange(P) % D
    freq = (np.float32(10000.0) ** (-np.arange(0, D, 2, dtype=np.float32) / np.float32(D))).astype(np.float32)
    angle = np.arange(L - 1, dtype=np.float32)[:, None] * freq
    cos = np.concatenate([np.ones((1, D // 2), np.float32), np.cos(angle)]).T[d // 2]
    sin = np.concatenate([np.zeros((1, D // 2), np.float32), np.sin(angle)]).T[d // 2]
    sin = sin * np.where(d % 2 == 0, -1, 1)[:, None]
    turns = np.stack([cos, sin], 1).reshape(P, 2, GPC, G).transpose(2, 0, 1, 3)
    heads = np.zeros((P, 2 * EC, 2 * H), np.float32)
    for j in range(2 * EC):
        heads[np.arange(P), j, 4 * j + np.arange(P) // D] = 1
    expert = np.concatenate([np.arange(NE), np.arange(NE) * CAP])[None].astype(np.float32)
    token = np.arange(T, dtype=np.uint32).reshape(NG, A, P).transpose(0, 2, 1)
    return {
        "had": had.astype(np.float32), "turns": turns.astype(np.float32), "ident16": np.eye(P, dtype=np.float16),
        "ident32": np.eye(P, dtype=np.float32), "heads": heads.reshape(P, -1),
        "tri": np.triu(np.ones((P, P)), 1).astype(np.float16),
        "ones": np.ones((P, P), np.float16), "expert": expert, "token": token,
    }


def kernel(**inputs):
    import concourse.bacc as _bacc
    import numpy as np
    from concourse.bass_utils import run_bass_kernel_spmd as _run

    v = {n[3:]: np.asarray(a) for n, a in inputs.items()}
    signs, scales = v["attn_sorf_signs"], v["attn_sorf_scales"]
    laid = {
        "x": v["attn_x"].reshape(T, E),
        "w_qkvT": v["attn_w_qkv"].T,
        "w_outT": v["attn_w_out"].T,
        "signs": signs[:, :M // HP].transpose(3, 2, 0, 1).reshape(HP, 3, H * M // HP),
        "scales": scales[:, :M // HP].reshape(1, -1),
        "gate": v["ffn_gate_w"].T.reshape(EC, P, NE).transpose(1, 0, 2).reshape(P, -1),
        "bias": v["ffn_bias"].reshape(1, -1),
        "W1": v["ffn_W1"], "W3": v["ffn_W3"], "W2": v["ffn_W2"],
        "sw1": v["ffn_sw1"].T, "sw3": v["ffn_sw3"].T, "sw2": v["ffn_sw2"].T,
        **shape_constants(),
    }
    nc = _bacc.Bacc("TRN2", target_bir_lowering=False, num_devices=1)
    arrays, io = {}, {}
    for name, a in laid.items():
        a = np.ascontiguousarray(a)
        arrays[f"{name}_in"] = a
        io[name] = nc.dram_tensor(f"{name}_in", a.shape, mybir.dt.from_np(a.dtype), kind="ExternalInput").ap()
    io["out"] = nc.dram_tensor("out_dram", [T, E], F32, kind="ExternalOutput").ap()
    build(nc, io)
    return _run(nc, [arrays], core_ids=[0]).results[0]["out_dram"].reshape(C, L, E)
```

```python
from contextlib import ExitStack

import concourse.bass as bass
from concourse import mybir

P = 128
C, L, E = 4, 2048, 512
H, D = 16, 32
M = 128
HP = 64
NE, K, I = 32, 4, 256
CAP = 512
T = C * L
G = 512
NG = T // G
A = G // P
EC = E // P
HPC = P // D
GPC = L // G
NSLOT = NE * CAP
W_SCALE = 256.0
M_SCALE = 64.0
H_SCALE = 64.0
F16_MAX = 65504.0
NOWHERE = 1.0e6

ALU = mybir.AluOpType
ACT = mybir.ActivationFunctionType
AX = mybir.AxisListType
F32 = mybir.dt.float32
F16 = mybir.dt.float16
BF16 = mybir.dt.bfloat16
U32 = mybir.dt.uint32


class Tools:

    def __init__(self, nc, ctx, stage):
        self.nc, self.ctx, self.stage, self.sems = nc, ctx, stage, []
        ctx.callback(self.close)

    def close(self):
        self.nc.clear_and_free_semaphores(self.sems)
        self.nc.all_engine_barrier()

    def sb(self, name, shape, dt=F32):
        return self.ctx.enter_context(self.nc.sbuf_tensor(f"{self.stage}_{name}", shape, dt))

    def pair(self, name, shape, dt=F32):
        return [self.sb(f"{name}{k}", shape, dt) for k in range(2)]

    def psum(self, name, banks=1):
        return self.ctx.enter_context(self.nc.psum_tensor(f"{self.stage}_{name}", [P, 512 * banks], F32))

    def sem(self, name):
        self.sems.append(self.nc.alloc_semaphore(f"{self.stage}_{name}"))
        return self.sems[-1]


def hold(eng, sem, value, pace):
    eng.wait_ge(sem, value)
    eng.sem_inc(pace, 1)


def setup_stage(nc, io, keep):
    with ExitStack() as ctx:
        t = Tools(nc, ctx, "s0")
        sb, sem = t.sb, t.sem
        had = sb("had", [HP, HP])
        s3 = sb("s3", [HP, 2 * H])
        s2 = sb("s2", [HP, 2 * H])
        s1 = sb("s1", [96, 2 * H])
        g = sb("g", [96, 2 * H * HP])
        left3 = sb("left3", [HP, 2 * H, HP])
        left2 = sb("left2", [HP, 2 * H, 96])
        y = sb("y", [HP, 2 * H, HP])
        m = sb("m", [96, 2 * H * HP])
        w = sb("w", [P, EC, 3 * E])
        zero = sb("zero", [P, NSLOT // P], U32)
        pY = [t.psum(f"pY{q}") for q in range(4)]
        pZ = [t.psum(f"pZ{q}") for q in range(4)]
        loaded, wloaded, kept = sem("loaded"), sem("wloaded"), sem("kept")
        left_ready, y_ready, y_copied, z_ready = sem("left_ready"), sem("y_ready"), sem("y_copied"), sem("z_ready")
        m_signed, m_ready, hi_ready, w_hi, zeroed, cleared = (
            sem("m_signed"), sem("m_ready"), sem("hi_ready"), sem("w_hi"), sem("zeroed"), sem("cleared"))
        block = ctx.enter_context(nc.Block())

        @block.sync
        def _(sp):
            sp.dma_start(had[:], io["had"]).then_inc(loaded, 16)
            sp.dma_start(s3[:], io["signs"][:, 2, :]).then_inc(loaded, 16)
            sp.dma_start(s2[:], io["signs"][:, 1, :]).then_inc(loaded, 16)
            for r in range(3):
                sp.dma_start(s1[32 * r:32 * r + 32, :], io["signs"][0:D, 0, :]).then_inc(loaded, 16)
            sp.dma_start(g[:], io["scales"].to_broadcast([96, 2 * H * HP])).then_inc(loaded, 16)
            sp.dma_start(w[:], io["w_qkvT"].rearrange("(c p) n -> p c n", p=P)).then_inc(wloaded, 16)
            sp.dma_start(keep["wo"][:], io["w_outT"].rearrange("(c p) n -> p c n", p=P)).then_inc(kept, 16)
            for name in ("ident16", "ident32", "heads", "tri", "ones", "gate", "expert", "bias"):
                src = io[name]
                if src.shape[0] == 1:
                    src = src.to_broadcast([P, src.shape[1]])
                sp.dma_start(keep[name][:], src).then_inc(kept, 16)
            sp.wait_ge(zeroed, 1)
            sp.dma_start(io["slot_token"].rearrange("(p n) o -> p (n o)", p=P), zero[:]).then_inc(cleared, 16)
            sp.wait_ge(kept, 16 * 9)
            sp.wait_ge(cleared, 16)

        @block.vector
        def _(dve):
            nc.vector.memset(zero[:], 0).then_inc(zeroed, 1)
            dve.wait_ge(loaded, 16 * 7)
            nc.vector.tensor_tensor(left3[:], had[:].unsqueeze(1).broadcast_to([HP, 2 * H, HP]),
                                    s3[:].unsqueeze(2).broadcast_to([HP, 2 * H, HP]), ALU.mult).then_inc(left_ready, 1)
            for r in range(3):
                nc.vector.tensor_tensor(left2[:, :, 32 * r:32 * r + 32],
                                        had[:, 0:D].unsqueeze(1).broadcast_to([HP, 2 * H, D]),
                                        s2[:].unsqueeze(2).broadcast_to([HP, 2 * H, D]), ALU.mult).then_inc(left_ready, 1)
            for q in range(4):
                dve.wait_ge(y_ready, q + 1)
                nc.vector.tensor_copy(y[:, 8 * q:8 * q + 8, :].rearrange("p a b -> p (a b)"),
                                      pY[q][0:HP, :]).then_inc(y_copied, 1)
            for c in range(EC):
                dve.wait_ge(w_hi, c + 1)
                nc.vector.scalar_tensor_tensor(out=keep["wqkv"][:, 1, c, :], in0=w[:, c, :], scalar=W_SCALE,
                                               in1=keep["wqkv"][:, 0, c, :], op0=ALU.mult, op1=ALU.subtract)
            for q in range(4):
                dve.wait_ge(z_ready, q + 1)
                mq = m[:, 512 * q:512 * q + 512]
                nc.vector.tensor_tensor(mq.rearrange("p (a b) -> p a b", b=HP),
                                        pZ[q][0:96, :].rearrange("p (a b) -> p a b", b=HP),
                                        s1[:, 8 * q:8 * q + 8].unsqueeze(2).broadcast_to([96, 8, HP]),
                                        ALU.mult).then_inc(m_signed, 1)
                dve.wait_ge(m_signed, q + 1)
                nc.vector.scalar_tensor_tensor(out=mq, in0=mq, scalar=M_SCALE / HP ** 2,
                                               in1=g[:, 512 * q:512 * q + 512],
                                               op0=ALU.mult, op1=ALU.mult).then_inc(m_ready, 1)
            dve.wait_ge(hi_ready, 1)
            dve.wait_ge(m_ready, 4)
            feat = keep["feat"][:].rearrange("p h f -> p (h f)")
            nc.vector.tensor_tensor(feat[32:64, :], m[32:64, :], feat[32:64, :], ALU.subtract).then_inc(m_ready, 1)

        @block.scalar
        def _(act):
            act.wait_ge(wloaded, 16)
            for c in range(EC):
                nc.scalar.activation(keep["wqkv"][:, 0, c, :], w[:, c, :], ACT.Copy, scale=W_SCALE).then_inc(w_hi, 1)
            act.wait_ge(m_ready, 4)
            nc.scalar.activation(keep["feat"][:].rearrange("p h f -> p (h f)"), m[:], ACT.Copy).then_inc(hi_ready, 1)

        @block.tensor
        def _(pe):
            pe.wait_ge(left_ready, 4)
            for i in range(2 * H):
                mm = nc.tensor.matmul(pY[i // 8][0:HP, (i % 8) * HP:(i % 8 + 1) * HP], left3[:, i, :], had[:],
                                      start=True, stop=True)
                if i % 8 == 7:
                    mm.then_inc(y_ready, 1)
            for i in range(2 * H):
                if i % 8 == 0:
                    pe.wait_ge(y_copied, i // 8 + 1)
                mm = nc.tensor.matmul(pZ[i // 8][0:96, (i % 8) * HP:(i % 8 + 1) * HP], left2[:, i, :], y[:, i, :],
                                      start=True, stop=True)
                if i % 8 == 7:
                    mm.then_inc(z_ready, 1)


def chained(engine, group):
    last = NG // 2 - 1
    group((0, 0), None, (0, 1))
    with engine.Fori(0, last) as u:
        group((u, 1), (u, 0), (u + 1, 0))
        group((u + 1, 0), (u, 1), (u + 1, 1))
    group((last, 1), (last, 0), None)


def project_stage(nc, io, keep):
    with ExitStack() as ctx:
        t = Tools(nc, ctx, "s2")
        x, x_hl = t.sb("x", [P, A, E]), t.sb("x_hl", [P, A, 2, E], F16)
        stats, mv = t.sb("stats", [P, A, 6]), t.sb("mv", [P, A, 2])
        rstd, power = t.sb("rstd", [P, A]), t.sb("power", [P, A])
        xT = t.pair("xT", [P, 2, EC, G], F16)
        table = t.pair("table", [P, 2, G])
        raw = t.pair("raw", [P, G])
        cosp = t.pair("cosp", [P, G])
        swap = t.pair("swap", [P, G])
        rot = t.pair("rot", [P, G])
        sq = t.pair("sq", [P, G])
        sq_hl = t.pair("sq_hl", [P, 2, 2 * EC, G], F16)
        hl = t.pair("hl", [P, 2, 2 * EC, G], F16)
        v = t.pair("v", [P, A, E])
        en = t.pair("en", [P, A, 2 * H])
        banks = [t.psum(f"proj{b}") for b in range(4)]
        norms = t.psum("norms")
        turned = [t.psum(f"turned{b}") for b in range(2)]
        table_loaded, hl_stored, v_stored, en_stored = (
            [t.sem(f"{n}{k}") for k in range(2)] for n in ("table_loaded", "hl_stored", "v_stored", "en_stored"))
        x_loaded, power_ready, stats_ready, mv_ready, var_ready, rstd_ready, x_ready = (
            t.sem(n) for n in ("x_loaded", "power_ready", "stats_ready", "mv_ready", "var_ready", "rstd_ready",
                               "x_ready"))
        x_high_ready, x_low_ready, turned_ready, xT_ready, pace = (
            t.sem(n) for n in ("x_high_ready", "x_low_ready", "turned_ready", "xT_ready", "pace"))
        proj_ready, evac, cos_ready, swap_ready, sin_ready = (
            t.sem("proj_ready"), t.sem("evac"), t.sem("cos_ready"), t.sem("swap_ready"), t.sem("sin_ready"))
        rot_ready, hi_ready, lo_ready = t.sem("rot_ready"), t.sem("hi_ready"), t.sem("lo_ready")
        sq_high_ready, sq_low_ready = t.sem("sq_high_ready"), t.sem("sq_low_ready")
        norms_ready, en_ready = t.sem("norms_ready"), t.sem("en_ready")
        QK = 2 * EC
        OUT = A + QK
        LAST = (NG // 2 - 1, 1)
        block = ctx.enter_context(nc.Block())

        @block.sync
        def _(sp):
            def load_x(n):
                hold(sp, x_low_ready, n * A + 1, pace)
                sp.dma_start(x[:], io["x"][bass.ds(n * G, G), :].rearrange("(a p) e -> p a e", p=P)
                             ).then_inc(x_loaded, 16)

            def load_table(ch, pg):
                n = GPC * ch + pg
                hold(sp, sin_ready, QK * n + 1, pace)
                hold(sp, cos_ready, QK * n + 1, pace)
                sp.dma_start(table[pg % 2][:], io["turns"][pg]).then_inc(table_loaded[pg % 2], 16)

            load_x(0)
            with nc.sync.Fori(0, C - 1) as ch:
                for pg in range(GPC):
                    load_x(GPC * ch + pg + 1)
                    load_table(ch, pg)
            for pg in range(GPC):
                if pg < GPC - 1:
                    load_x(GPC * (C - 1) + pg + 1)
                load_table(C - 1, pg)

        @block.tensor
        def _(pe):
            pe.sem_inc(norms_ready, 2)

            def turn(u, k, a):
                n = (2 * u + k) * A + a
                pe.wait_ge(x_low_ready, n + 2)
                pe.wait_ge(xT_ready, n + 1)
                for s in range(2):
                    for c in range(EC):
                        mm = nc.tensor.transpose(turned[a % 2][:].bitcast(F16)[:, (s * EC + c) * P:(s * EC + c + 1) * P],
                                                 x_hl[:, a, s, c * P:(c + 1) * P], keep["ident16"][:])
                mm.then_inc(turned_ready, 1)

            def output(u, k, o):
                hi, lo = xT[k][:, 0], xT[k][:, 1]
                pe.wait_ge(evac, OUT * (2 * u + k) + o + 1)
                for c in range(EC):
                    if o < A:
                        w = keep["wqkv"][:, :, c, 2 * E:3 * E]
                        q = slice(o * P, (o + 1) * P)
                        parts = ((hi[:, c, q], w[:, 0]), (hi[:, c, q], w[:, 1]), (lo[:, c, q], w[:, 0]))
                    else:
                        w = keep["wqkv"][:, :, c, (o - A) * P:(o - A + 1) * P]
                        parts = ((w[:, 0], hi[:, c]), (w[:, 0], lo[:, c]), (w[:, 1], hi[:, c]))
                    for i, (left, right) in enumerate(parts):
                        mm = nc.tensor.matmul(banks[o % 4][:], left, right, start=(c == 0 and i == 0),
                                              stop=(c == EC - 1 and i == 2))
                mm.then_inc(proj_ready, 1)

            def make_norms(u, k):
                pe.wait_ge(sq_low_ready, QK * (2 * u + k) + QK + 2)
                pe.wait_ge(en_ready, 2 * u + k + 1)
                for a in range(A):
                    for j in range(QK):
                        out = norms[:, a * 2 * H + HPC * j:a * 2 * H + HPC * (j + 1)]
                        for s in range(2):
                            mm = nc.tensor.matmul(out, sq_hl[k][:, s, j, a * P:(a + 1) * P], keep["heads"][:],
                                                  start=(s == 0), stop=(s == 1))
                mm.then_inc(norms_ready, 1)

            def group(this, before, after):
                u, k = this
                pe.wait_ge(xT_ready, (2 * u + k) * A + A + 2)
                for o in range(OUT):
                    output(u, k, o)
                    if before and o == 2:
                        make_norms(*before)
                    if after and A + 2 <= o < 2 * A + 2:
                        turn(*after, o - A - 2)

            for a in range(A):
                turn(0, 0, a)
            chained(nc.tensor, group)
            make_norms(*LAST)

        @block.gpsimd
        def _(pool):
            nc.gpsimd.memset(power[:], -0.5).then_inc(power_ready, 1)
            pool.wait_ge(power_ready, 1)
            pool.sem_inc(cos_ready, QK + 1)
            pool.sem_inc(sq_low_ready, 2)

            def make_rstd(u, k):
                n = 2 * u + k
                hold(pool, mv_ready, n + 1, pace)
                nc.gpsimd.tensor_scalar(rstd[:], mv[:, :, 1], 1e-5, None, ALU.add).then_inc(var_ready, 1)
                pool.wait_ge(var_ready, n + 1)
                nc.gpsimd.tensor_tensor(rstd[:], rstd[:], power[:], ALU.pow).then_inc(rstd_ready, 1)

            def make_cos(u, k, j):
                n = QK * (2 * u + k) + j
                pool.wait_ge(rot_ready, n + 1)
                pool.wait_ge(evac, OUT * (2 * u + k) + A + j + 5)
                nc.gpsimd.tensor_tensor(cosp[j % 2][:], raw[j % 2][:], table[k][:, 0, :], ALU.mult).then_inc(cos_ready, 1)

            def make_sq_low(u, k, j):
                pool.wait_ge(sq_high_ready, QK * (2 * u + k) + j + 3)
                nc.gpsimd.tensor_tensor(sq_hl[k][:, 1, j, :], sq[j % 2][:], sq_hl[k][:, 0, j, :],
                                        ALU.subtract).then_inc(sq_low_ready, 1)

            def group(this, before, after):
                u, k = this
                if before:
                    make_sq_low(*before, QK - 1)
                if after:
                    make_rstd(*after)
                pool.wait_ge(table_loaded[k], 16 * u + 16)
                for j in range(QK):
                    make_cos(u, k, j)
                    if j >= 2:
                        make_sq_low(u, k, j - 2)
                make_sq_low(u, k, QK - 2)

            make_rstd(0, 0)
            chained(nc.gpsimd, group)
            make_sq_low(*LAST, QK - 1)

        @block.vector
        def _(dve):
            dve.sem_inc(x_low_ready, 1)
            dve.sem_inc(rot_ready, 2)
            dve.sem_inc(swap_ready, 2)
            dve.sem_inc(sin_ready, QK + 1)
            pairs = [i ^ 1 for i in range(32)]

            def measure(u, k):
                dve.wait_ge(x_loaded, 16 * (2 * u + k) + 16)
                for a in range(A):
                    ins = nc.vector.bn_stats(stats[:, a, :], x[:, a, :])
                ins.then_inc(stats_ready, 1)

            def normalize(u, k):
                n = 2 * u + k
                hold(dve, stats_ready, n + 1, pace)
                for a in range(A):
                    ins = nc.vector.bn_aggr(mv[:, a, :], stats[:, a, :])
                ins.then_inc(mv_ready, 1)
                dve.wait_ge(rstd_ready, n + 1)
                for a in range(A):
                    nc.vector.tensor_scalar(x[:, a, :], x[:, a, :], mv[:, a, 0:1], rstd[:, a:a + 1], ALU.subtract,
                                            ALU.mult).then_inc(x_ready, 1)
                for a in range(A):
                    dve.wait_ge(x_high_ready, n * A + a + 1)
                    nc.vector.tensor_tensor(x_hl[:, a, 1, :], x[:, a, :], x_hl[:, a, 0, :],
                                            ALU.subtract).then_inc(x_low_ready, 1)

            def make_sin(u, k, j):
                hold(dve, evac, OUT * (2 * u + k) + A + j + 5, pace)
                nc.vector.stream_shuffle(swap[j % 2][:], raw[j % 2][:], pairs).then_inc(swap_ready, 1)
                dve.wait_ge(swap_ready, QK * (2 * u + k) + j + 3)
                nc.vector.tensor_tensor(swap[j % 2][:], swap[j % 2][:], table[k][:, 1, :], ALU.mult).then_inc(sin_ready, 1)

            def make_lo(u, k, j):
                dve.wait_ge(hi_ready, QK * (2 * u + k) + j + 1)
                nc.vector.tensor_tensor(hl[k][:, 1, j, :], rot[j % 2][:], hl[k][:, 0, j, :],
                                        ALU.subtract).then_inc(lo_ready, 1)

            def make_rot(u, k, j):
                n = QK * (2 * u + k) + j
                dve.wait_ge(sin_ready, n + QK + 2)
                dve.wait_ge(cos_ready, n + QK + 2)
                dve.wait_ge(sq_high_ready, n + 1)
                nc.vector.tensor_tensor(rot[j % 2][:], cosp[j % 2][:], swap[j % 2][:], ALU.add).then_inc(rot_ready, 1)

            def group(this, before, after):
                u, k = this
                if after:
                    measure(*after)
                if before:
                    make_lo(*before, QK - 1)
                if after:
                    normalize(*after)
                dve.wait_ge(table_loaded[k], 16 * u + 16)
                for j in range(QK):
                    make_sin(u, k, j)
                    if j >= 1:
                        make_lo(u, k, j - 1)
                    make_rot(u, k, j)

            measure(0, 0)
            normalize(0, 0)
            chained(nc.vector, group)
            make_lo(*LAST, QK - 1)

        @block.scalar
        def _(act):
            act.sem_inc(evac, 4)
            act.sem_inc(xT_ready, 2)
            act.sem_inc(sq_high_ready, 2)
            act.sem_inc(en_ready, 1)
            for s in (*v_stored, *en_stored, *hl_stored):
                act.sem_inc(s, 1)

            def make_x_high(u, k, a):
                act.wait_ge(x_ready, (2 * u + k) * A + a + 1)
                nc.scalar.activation(x_hl[:, a, 0, :], x[:, a, :], ACT.Copy).then_inc(x_high_ready, 1)

            def copy_turned(u, k, a):
                act.wait_ge(turned_ready, (2 * u + k) * A + a + 1)
                nc.scalar.activation(xT[k][:, :, :, a * P:(a + 1) * P],
                                     turned[a % 2][:].bitcast(F16).rearrange("p (s c q) -> p s c q", s=2, c=EC),
                                     ACT.Copy).then_inc(xT_ready, 1)

            def read(u, k, o):
                act.wait_ge(proj_ready, OUT * (2 * u + k) + o + 1)
                if o < A:
                    dst = v[k][:, o, :]
                else:
                    n = QK * (2 * u + k) + o - A
                    act.wait_ge(swap_ready, n + 1)
                    act.wait_ge(cos_ready, n + QK)
                    dst = raw[o % 2][:]
                nc.scalar.activation(dst, banks[o % 4][:], ACT.Copy, scale=1.0 / W_SCALE).then_inc(evac, 1)

            def split(u, k, j):
                n = QK * (2 * u + k) + j
                act.wait_ge(rot_ready, n + 3)
                nc.scalar.activation(hl[k][:, 0, j, :], rot[j % 2][:], ACT.Copy).then_inc(hi_ready, 1)
                act.wait_ge(sq_low_ready, n + 1)
                nc.scalar.activation(sq[j % 2][:], rot[j % 2][:], ACT.Square)
                nc.scalar.activation(sq_hl[k][:, 0, j, :], rot[j % 2][:], ACT.Square).then_inc(sq_high_ready, 1)

            def store_v(u, k):
                act.wait_ge(evac, OUT * (2 * u + k) + A + 4)
                act.dma_start(io["v"][bass.ds(2 * u + k, 1)].rearrange("o p a e -> p (o a) e"), v[k][:]
                              ).then_inc(v_stored[k], 16)

            def store_hl(u, k):
                act.wait_ge(lo_ready, QK * (2 * u + k) + QK)
                for s in range(2):
                    act.dma_start(io["qk"][bass.ds(2 * u + k, 1), s:s + 1].rearrange("o s (c p) n -> p (o s c) n", p=P),
                                  hl[k][:, s]).then_inc(hl_stored[k], 16)

            def make_en(u, k):
                n = 2 * u + k
                act.wait_ge(norms_ready, n + 3)
                act.wait_ge(en_stored[k], 16 * u + 1)
                nc.scalar.activation(en[k][:].rearrange("p a h -> p (a h)"), norms[:, 0:A * 2 * H], ACT.Exp,
                                     scale=-0.5).then_inc(en_ready, 1)
                act.wait_ge(en_ready, n + 2)
                act.dma_start(io["en"][bass.ds(n, 1)].rearrange("o p a h -> p (o a) h"), en[k][:]
                              ).then_inc(en_stored[k], 16)

            def group(this, before, after):
                u, k = this
                act.wait_ge(v_stored[k], 16 * u + 1)
                read(u, k, 0)
                if before:
                    split(*before, QK - 1)
                read(u, k, 1)
                if after:
                    make_x_high(*after, 0)
                if before:
                    store_hl(*before)
                read(u, k, 2)
                if after:
                    make_x_high(*after, 1)
                read(u, k, 3)
                if after:
                    make_x_high(*after, 2)
                    make_x_high(*after, 3)
                store_v(u, k)
                act.wait_ge(hl_stored[k], 32 * u + 1)
                act.wait_ge(norms_ready, 2 * u + k + 1)
                for j in range(QK):
                    read(u, k, A + j)
                    if before and j == 0:
                        make_en(*before)
                    if j >= 1:
                        split(u, k, j - 1)
                    if after and 3 <= j < 3 + A:
                        copy_turned(*after, j - 3)

            for a in range(A):
                make_x_high(0, 0, a)
            for a in range(A):
                copy_turned(0, 0, a)
            chained(nc.scalar, group)
            split(*LAST, QK - 1)
            store_hl(*LAST)
            make_en(*LAST)
            for k in range(2):
                act.wait_ge(hl_stored[k], 32 * NG // 2 + 1)
                act.wait_ge(v_stored[k], 16 * NG // 2 + 1)
                act.wait_ge(en_stored[k], 16 * NG // 2 + 1)


def sums_stage(nc, io, keep):
    with ExitStack() as ctx:
        t = Tools(nc, ctx, "s3")
        kT = [t.sb(f"kT{k}", [96, H, G], F16) for k in range(2)]
        v = t.pair("v", [P, A, E])
        en = t.pair("en", [P, A, 2 * H])
        aug = t.pair("aug", [P, A * H, D + 1])
        phi = t.pair("phi", [P, H // 2, M])
        zero = t.sb("zero", [P, G], F16)
        sumT = t.sb("sumT", [D + 1, H, M])
        most, largest, share = t.sb("most", [P, H]), t.sb("largest", [P, H]), t.sb("share", [P, H])
        scaled = t.sb("scaled", [P, 2, H // 2, D + 1])
        halves = t.sb("halves", [P, 2, H, D + 1], F16)
        logits = [t.psum(f"logits{b}", 2) for b in range(2)]
        parts = t.psum("parts", 4)
        k_loaded, v_loaded = ([t.sem(f"{n}{k}") for k in range(2)] for n in ("k_loaded", "v_loaded"))
        logits_ready, phi_ready, aug_ready, part_ready = (
            t.sem("logits_ready"), t.sem("phi_ready"), t.sem("aug_ready"), t.sem("part_ready"))
        cleared, sumT_ready, turned_ready, scaled_ready, most_ready, largest_ready, step, halves_ready, stored, pace = (
            t.sem(n) for n in ("cleared", "sumT_ready", "turned_ready", "scaled_ready", "most_ready", "largest_ready",
                               "step", "halves_ready", "stored", "pace"))
        HALF = H // 2
        block = ctx.enter_context(nc.Block())

        @block.sync
        def _(sp):
            def load(ch, u):
                for k in range(2):
                    group = bass.ds(GPC * ch + 2 * u + k, 1)
                    hold(sp, logits_ready, 32 * ch + 16 * u + 8 * k + 1, pace)
                    for r, s in enumerate((0, 0, 1)):
                        sp.dma_start(kT[k][32 * r:32 * r + 32],
                                     io["qk"][group, s, E:2 * E, :].rearrange("o (h d) n -> d (o h) n", d=D)
                                     ).then_inc(k_loaded[k], 16)
                    hold(sp, aug_ready, GPC * ch + 2 * u + k + 1, pace)
                    sp.dma_start(v[k][:], io["v"][group].rearrange("o p a e -> p (o a) e")).then_inc(v_loaded[k], 16)
                    sp.dma_start(en[k][:], io["en"][group].rearrange("o p a h -> p (o a) h")).then_inc(v_loaded[k], 16)

            def store(ch):
                hold(sp, halves_ready, ch + 1, pace)
                sp.dma_start(io["sums"][bass.ds(ch, 1)].rearrange("o p n -> p (o n)"),
                             halves[:].rearrange("p s h d -> p (s h d)")).then_inc(stored, 16)
                sp.dma_start(io["largest"][bass.ds(ch, 1)].rearrange("o p h -> p (o h)"), largest[:]
                             ).then_inc(stored, 16)

            load(0, 0)
            with nc.sync.Fori(0, C - 1) as ch:
                for u in range(1, GPC // 2):
                    load(ch, u)
                load(ch + 1, 0)
                store(ch)
            for u in range(1, GPC // 2):
                load(C - 1, u)
            store(C - 1)
            sp.wait_ge(stored, 32 * C + 1)

        @block.vector
        def _(dve):
            nc.vector.memset(zero[:], 0.0).then_inc(cleared, 1)
            dve.sem_inc(aug_ready, 2)
            dve.sem_inc(sumT_ready, 1)
            dve.sem_inc(scaled_ready, 1)
            with nc.vector.Fori(0, C) as ch:
                with nc.vector.Fori(0, GPC // 2) as u:
                    for k in range(2):
                        dve.wait_ge(v_loaded[k], 64 * ch + 32 * u + 32)
                        dve.wait_ge(part_ready, 32 * ch + 16 * u + 8 * k + 2)
                        weight = en[k][:, :, H:2 * H]
                        nc.vector.tensor_tensor(aug[k][:, :, 0:D].rearrange("p (a h) d -> p a h d", a=A),
                                                v[k][:].rearrange("p a (h d) -> p a h d", d=D),
                                                weight.unsqueeze(3).broadcast_to([P, A, H, D]), ALU.mult)
                        nc.vector.tensor_copy(aug[k][:, :, D:D + 1].rearrange("p (a h) d -> p a (h d)", a=A),
                                              weight).then_inc(aug_ready, 1)
                dve.wait_ge(part_ready, 32 * ch + 32 + 10)
                nc.vector.tensor_scalar(sumT[:].rearrange("p h m -> p (h m)"), parts[0:D + 1, :], 1.0 / M, None,
                                        ALU.mult).then_inc(sumT_ready, 1)
                dve.wait_ge(turned_ready, ch + 1)
                nc.vector.tensor_copy(
                    scaled[:].rearrange("p b h d -> p b (h d)"),
                    logits[0][:].rearrange("p (b n) -> p b n", b=2)[:, :, 0:HALF * (D + 1)]).then_inc(scaled_ready, 1)
                dve.wait_ge(scaled_ready, ch + 2)
                flat = scaled[:].rearrange("p b h d -> p (b h) d")
                nc.vector.tensor_reduce(most[:], flat, AX.X, ALU.max, apply_absolute_value=True).then_inc(most_ready, 1)
                dve.wait_ge(largest_ready, ch + 1)
                nc.vector.tensor_scalar(share[:], largest[:], 1e-30, None, ALU.max).then_inc(step, 1)
                dve.wait_ge(step, 4 * ch + 1)
                nc.vector.reciprocal(share[:], share[:]).then_inc(step, 1)
                dve.wait_ge(step, 4 * ch + 2)
                nc.vector.tensor_tensor(flat, flat, share[:].unsqueeze(2).broadcast_to([P, H, D + 1]),
                                        ALU.mult).then_inc(step, 1)
                dve.wait_ge(step, 4 * ch + 3)
                dve.wait_ge(stored, 32 * ch + 1)
                nc.vector.tensor_copy(halves[:, 0], flat).then_inc(step, 1)
                dve.wait_ge(step, 4 * ch + 4)
                nc.vector.tensor_tensor(halves[:, 1], flat, halves[:, 0], ALU.subtract).then_inc(halves_ready, 1)

        @block.gpsimd
        def _(pool):
            with nc.gpsimd.Fori(0, C) as ch:
                hold(pool, most_ready, ch + 1, pace)
                hold(pool, stored, 32 * ch + 1, pace)
                nc.gpsimd.partition_all_reduce(largest[:], most[:], P, bass.bass_isa.ReduceOp.max
                                               ).then_inc(largest_ready, 1)

        @block.scalar
        def _(act):
            act.sem_inc(phi_ready, 2)
            with nc.scalar.Fori(0, C) as ch, nc.scalar.Fori(0, GPC // 2) as u:
                for k in range(2):
                    for i in range(2 * A):
                        n = 32 * ch + 16 * u + 8 * k + i
                        act.wait_ge(logits_ready, n + 10)
                        act.wait_ge(part_ready, n + 9)
                        nc.scalar.activation(phi[i % 2][:].rearrange("p h m -> p (h m)"), logits[i % 2][:], ACT.Exp,
                                             scale=1.0 / M_SCALE).then_inc(phi_ready, 1)

        @block.tensor
        def _(pe):
            pe.sem_inc(logits_ready, 9)
            pe.sem_inc(part_ready, 10)
            pe.sem_inc(stored, 1)

            def make_logits(n, k, i):
                a, half = i // 2, i % 2
                pe.wait_ge(phi_ready, n + i + 1)
                for h in range(HALF):
                    mm = nc.tensor.matmul(logits[i % 2][:, h * M:(h + 1) * M],
                                          kT[k][:, HALF * half + h, a * P:(a + 1) * P],
                                          keep["feat"][:, HALF * half + h, :], start=True, stop=True)
                mm.then_inc(logits_ready, 1)

            pe.wait_ge(cleared, 1)
            with nc.tensor.Fori(0, C) as ch:
                pe.wait_ge(sumT_ready, ch + 1)
                for b in range(4):
                    nc.tensor.matmul(parts[0:D + 1, 512 * b:512 * b + 512], zero[:, 0:D + 1], zero[:],
                                     start=True, stop=True)
                hold(pe, scaled_ready, ch + 1, pace)
                with nc.tensor.Fori(0, GPC // 2) as u:
                    for k in range(2):
                        n = 32 * ch + 16 * u + 8 * k
                        pe.wait_ge(k_loaded[k], 96 * ch + 48 * u + 48)
                        make_logits(n, k, 0)
                        for i in range(2 * A):
                            a, half = i // 2, i % 2
                            if i + 1 < 2 * A:
                                make_logits(n, k, i + 1)
                            if i == 0:
                                pe.wait_ge(aug_ready, GPC * ch + 2 * u + k + 3)
                            pe.wait_ge(phi_ready, n + i + 3)
                            for h in range(HALF * half, HALF * half + HALF):
                                mm = nc.tensor.matmul(parts[0:D + 1, h * M:(h + 1) * M], aug[k][:, a * H + h, :],
                                                      phi[half][:, h % HALF, :], start=False, stop=True,
                                                      skip_group_check=True)
                            mm.then_inc(part_ready, 1)
                pe.wait_ge(sumT_ready, ch + 2)
                hold(pe, phi_ready, 32 * ch + 32 + 2, pace)
                for h in range(H):
                    at = 512 * (h // HALF) + (h % HALF) * (D + 1)
                    mm = nc.tensor.transpose(logits[0][:, at:at + D + 1], sumT[:, h, :],
                                             keep["ident32"][0:D + 1, 0:D + 1])
                mm.then_inc(turned_ready, 1)


def skewed(engine, tile):
    for j in range(3):
        tile(0, j)
    with engine.Fori(0, T // P // 8 - 1) as u:
        for j in range(3, 11):
            tile(u, j)
    for j in range(3, 8):
        tile(T // P // 8 - 1, j)


def attend_stage(nc, io, keep):
    with ExitStack() as ctx:
        t = Tools(nc, ctx, "s4")
        HALF = H // 2
        RING = 4
        LAST = T // P - 1
        qT = [t.sb(f"qT{k}", [96, H, G], F16) for k in range(2)]
        sums = t.pair("sums", [P, 2, H, D + 1], F16)
        largest = t.pair("largest", [P, H])
        weight = t.pair("weight", [P, A, H])
        phi = [t.sb(f"phi{r}", [P, HALF, P]) for r in range(RING)]
        high, low = ([t.sb(f"{n}{r}", [P, HALF, P], F16) for r in range(RING)] for n in ("high", "low"))
        en = t.pair("en", [P, A, 2 * H])
        x = t.pair("x", [P, A, E])
        den = t.sb("den", [P, H])
        ratio = t.sb("ratio", [P, H])
        at = t.sb("at", [P, E])
        atT = t.sb("atT", [P, EC, P])
        z = t.pair("z", [P, E])
        stats, mv, rstd, power = t.sb("stats", [P, 6]), t.sb("mv", [P, 2]), t.sb("rstd", [P, 1]), t.sb("power", [P, 1])
        logits = [t.psum(f"logits{b}", 2) for b in range(2)]
        numer = t.psum("numer", 2)
        turned = t.psum("turned")
        y = t.psum("y")
        q_loaded, s_loaded, x_stored = ([t.sem(f"{n}{k}") for k in range(2)] for n in ("q_loaded", "s_loaded", "x_stored"))
        logits_ready, phi_ready, numer_ready, den_ready, at_ready = (
            t.sem("logits_ready"), t.sem("phi_ready"), t.sem("numer_ready"), t.sem("den_ready"), t.sem("at_ready"))
        turned_ready, atT_ready, y_ready, stats_ready, mv_ready = (
            t.sem("turned_ready"), t.sem("atT_ready"), t.sem("y_ready"), t.sem("stats_ready"), t.sem("mv_ready"))
        rstd_ready, z_ready, x1_ready, power_ready, pace = (
            t.sem("rstd_ready"), t.sem("z_ready"), t.sem("x1_ready"), t.sem("power_ready"), t.sem("pace"))
        var_ready, low_ready, weight_ready = (t.sem(n) for n in ("var_ready", "low_ready", "weight_ready"))
        high_ready = [t.sem(f"high_ready{half}") for half in range(2)]
        block = ctx.enter_context(nc.Block())

        def turn(u, j):
            return u + j // 8, j % 8 // A, j % A

        @block.sync
        def _(sp):
            with nc.sync.Fori(0, C) as ch, nc.sync.Fori(0, GPC // 2) as u:
                for k in range(2):
                    group = bass.ds(GPC * ch + 2 * u + k, 1)
                    hold(sp, logits_ready, 32 * ch + 16 * u + 8 * k + 1, pace)
                    for r, s in enumerate((0, 0, 1)):
                        sp.dma_start(qT[k][32 * r:32 * r + 32],
                                     io["qk"][group, s, 0:E, :].rearrange("o (h d) n -> d (o h) n", d=D)
                                     ).then_inc(q_loaded[k], 16)
                    hold(sp, x_stored[k], 32 * ch + 16 * u + 1, pace)
                    sp.dma_start(sums[k][:].rearrange("p s h d -> p (s h d)"),
                                 io["sums"][bass.ds(ch, 1)].rearrange("o p n -> p (o n)")).then_inc(s_loaded[k], 16)
                    sp.dma_start(largest[k][:], io["largest"][bass.ds(ch, 1)].rearrange("o p h -> p (o h)")
                                 ).then_inc(s_loaded[k], 16)
                    sp.dma_start(en[k][:], io["en"][group].rearrange("o p a h -> p (o a) h")).then_inc(s_loaded[k], 16)
                    sp.dma_start(x[k][:], io["x"][bass.ds((GPC * ch + 2 * u + k) * G, G), :]
                                 .rearrange("(a p) e -> p a e", p=P)).then_inc(s_loaded[k], 16)

        @block.tensor
        def _(pe):
            pe.sem_inc(logits_ready, 9)
            pe.sem_inc(numer_ready, 4)
            pe.sem_inc(turned_ready, 1)
            pe.sem_inc(y_ready, 1)

            def make_logits(u, j, half):
                v, k, a = turn(u, j)
                if a == 0 and half == 0:
                    pe.wait_ge(q_loaded[k], 48 * v + 48)
                pe.wait_ge(phi_ready, 16 * u + 2 * j + half + 1)
                for h in range(HALF):
                    mm = nc.tensor.matmul(logits[half][:, h * P:(h + 1) * P],
                                          keep["feat"][:, HALF * half + h, :],
                                          qT[k][:, HALF * half + h, a * P:(a + 1) * P],
                                          start=True, stop=True)
                mm.then_inc(logits_ready, 1)

            def transpose(u, j):
                pe.wait_ge(at_ready, 8 * u + j + 2)
                pe.wait_ge(atT_ready, 8 * u + j + 1)
                for c in range(EC):
                    mm = nc.tensor.transpose(turned[:, c * P:(c + 1) * P], at[:, c * P:(c + 1) * P], keep["ident32"][:])
                mm.then_inc(turned_ready, 1)

            def project(u, j):
                pe.wait_ge(atT_ready, 8 * u + j + 2)
                pe.wait_ge(z_ready, 8 * u + j + 2)
                for c in range(EC):
                    mm = nc.tensor.matmul(y[:], atT[:, c, :], keep["wo"][:, c, :], start=(c == 0), stop=(c == EC - 1))
                mm.then_inc(y_ready, 1)

            def tile(u, j):
                v, k, a = turn(u, j)
                first, last = isinstance(u, int) and u == 0 and j == 0, isinstance(u, int) and 8 * u + j > LAST - 2
                if not first:
                    transpose(u, j - 1)
                if a == 0:
                    pe.wait_ge(s_loaded[k], 64 * v + 64)
                for half in range(2):
                    if not last:
                        make_logits(u, j + 2, half)
                    if half == 0:
                        pe.wait_ge(at_ready, 8 * u + j + 1)
                    pe.wait_ge(low_ready, 16 * u + 2 * j + half + 5)
                    r = (2 * j + half) % RING
                    for h in range(HALF):
                        out = numer[:, 512 * half + h * (D + 1):512 * half + (h + 1) * (D + 1)]
                        s = sums[k][:, :, HALF * half + h, :]
                        nc.tensor.matmul(out, high[r][:, h, :], s[:, 0], start=True, stop=False)
                        nc.tensor.matmul(out, high[r][:, h, :], s[:, 1], start=False, stop=False)
                        mm = nc.tensor.matmul(out, low[r][:, h, :], s[:, 0], start=False, stop=True)
                    mm.then_inc(numer_ready, 1)
                if not first:
                    project(u, j - 1)

            for i in range(4):
                make_logits(0, i // 2, i % 2)
            skewed(nc.tensor, tile)
            transpose(0, LAST)
            project(0, LAST)

        @block.scalar
        def _(act):
            act.sem_inc(phi_ready, 2)
            act.sem_inc(atT_ready, 1)
            for k in range(2):
                act.sem_inc(x_stored[k], 1)

            def make_phi(u, j, half):
                act.wait_ge(logits_ready, 16 * u + 2 * j + half + 10)
                act.wait_ge(low_ready, 16 * u + 2 * j + half + 1)
                nc.scalar.activation(phi[(2 * j + half) % RING][:].rearrange("p h m -> p (h m)"), logits[half][:],
                                     ACT.Exp, scale=1.0 / M_SCALE).then_inc(phi_ready, 1)

            def copy_turned(u, j):
                act.wait_ge(turned_ready, 8 * u + j + 2)
                act.wait_ge(y_ready, 8 * u + j + 1)
                nc.scalar.activation(atT[:].rearrange("p c q -> p (c q)"), turned[:], ACT.Copy).then_inc(atT_ready, 1)

            def store(u, j):
                v, k, a = turn(u, j)
                act.wait_ge(x1_ready, 8 * u + j + 3)
                act.dma_start(io["x1"][bass.ds((2 * v + k) * G, G), :].rearrange("(a p) e -> p a e", p=P),
                              x[k][:]).then_inc(x_stored[k], 16)

            def tile(u, j):
                first, last = isinstance(u, int) and u == 0 and j == 0, isinstance(u, int) and 8 * u + j > LAST - 2
                if not first:
                    copy_turned(u, j - 1)
                if not last:
                    for half in range(2):
                        make_phi(u, j + 2, half)
                if j % A == 2 and j > A:
                    store(u, j - 3)

            for i in range(4):
                make_phi(0, i // 2, i % 2)
            skewed(nc.scalar, tile)
            copy_turned(0, LAST)
            store(0, LAST)
            for k in range(2):
                act.wait_ge(x_stored[k], 16 * NG // 2 + 1)

        @block.vector
        def _(dve):
            dve.sem_inc(at_ready, 1)
            dve.sem_inc(z_ready, 2)
            dve.sem_inc(den_ready, 1)
            dve.sem_inc(low_ready, RING)

            def split(u, j, half):
                r = (2 * j + half) % RING
                dve.wait_ge(numer_ready, 16 * u + 2 * j + half + 1)
                if half == 0:
                    dve.wait_ge(phi_ready, 16 * u + 2 * j + 3)
                    nc.vector.tensor_scalar(high[r][:], phi[r][:], F16_MAX, None, ALU.min).then_inc(high_ready[0], 1)
                dve.wait_ge(high_ready[half], 8 * u + j + 1)
                nc.vector.scalar_tensor_tensor(out=low[r][:], in0=phi[r][:], scalar=F16_MAX, in1=high[r][:],
                                               op0=ALU.min, op1=ALU.subtract).then_inc(low_ready, 1)

            def weigh(u, j):
                v, k, a = turn(u, j)
                dve.wait_ge(s_loaded[k], 64 * v + 64)
                nc.vector.tensor_tensor(weight[k][:], en[k][:, :, 0:H],
                                        largest[k][:].unsqueeze(1).broadcast_to([P, A, H]),
                                        ALU.mult).then_inc(weight_ready, 1)
                dve.wait_ge(weight_ready, 2 * v + k + 1)

            def divide(u, j):
                v, k, a = turn(u, j)
                d0 = 32 * u + 4 * j + 1
                heads = numer[:].rearrange("p (b n) -> p b n", b=2)[:, :, 0:HALF * (D + 1)].rearrange(
                    "p b (h d) -> p b h d", d=D + 1)
                w = weight[k][:, a, :]
                dve.wait_ge(numer_ready, 16 * u + 2 * j + 2 + RING)
                nc.vector.tensor_tensor(den[:].rearrange("p (b h o) -> p b h o", b=2, o=1), heads[:, :, :, D:D + 1],
                                        w.rearrange("p (b h o) -> p b h o", b=2, o=1), ALU.mult).then_inc(den_ready, 1)
                dve.wait_ge(den_ready, d0 + 1)
                nc.vector.tensor_scalar(den[:], den[:], 1e-6, None, ALU.max).then_inc(den_ready, 1)
                dve.wait_ge(den_ready, d0 + 2)
                nc.vector.reciprocal(den[:], den[:]).then_inc(den_ready, 1)
                dve.wait_ge(den_ready, d0 + 3)
                nc.vector.tensor_tensor(ratio[:], den[:], w, ALU.mult).then_inc(den_ready, 1)
                dve.wait_ge(den_ready, d0 + 4)
                dve.wait_ge(turned_ready, 8 * u + j + 1)
                nc.vector.tensor_tensor(at[:].rearrange("p (b h d) -> p b h d", b=2, d=D), heads[:, :, :, 0:D],
                                        ratio[:].rearrange("p (b h) -> p b h", b=2).unsqueeze(3)
                                        .broadcast_to([P, 2, HALF, D]), ALU.mult).then_inc(at_ready, 1)

            def measure(u, j):
                dve.wait_ge(y_ready, 8 * u + j + 2)
                nc.vector.bn_stats(stats[:], y[:]).then_inc(stats_ready, 1)
                hold(dve, stats_ready, 8 * u + j + 1, pace)
                nc.vector.bn_aggr(mv[:], stats[:]).then_inc(mv_ready, 1)

            def normalize(u, j):
                dve.wait_ge(rstd_ready, 8 * u + j + 1)
                dve.wait_ge(x1_ready, 8 * u + j + 1)
                nc.vector.tensor_scalar(z[j % 2][:], y[:], mv[:, 0:1], rstd[:], ALU.subtract,
                                        ALU.mult).then_inc(z_ready, 1)

            def tile(u, j):
                first, last = isinstance(u, int) and u == 0 and j == 0, isinstance(u, int) and 8 * u + j > LAST - 2
                if j % A == 0:
                    weigh(u, j)
                divide(u, j)
                if not last:
                    split(u, j + 2, 0)
                if not first:
                    measure(u, j - 1)
                if not last:
                    split(u, j + 2, 1)
                if not first:
                    normalize(u, j - 1)

            for i in range(4):
                split(0, i // 2, i % 2)
            skewed(nc.vector, tile)
            measure(0, LAST)
            normalize(0, LAST)

        @block.gpsimd
        def _(pool):
            nc.gpsimd.memset(power[:], -0.5).then_inc(power_ready, 1)
            pool.wait_ge(power_ready, 1)
            pool.sem_inc(x1_ready, 2)

            def make_high(u, j):
                r = (2 * j + 1) % RING
                hold(pool, phi_ready, 16 * u + 2 * j + 4, pace)
                hold(pool, numer_ready, 16 * u + 2 * j + 2, pace)
                nc.gpsimd.tensor_scalar(high[r][:], phi[r][:], F16_MAX, None, ALU.min).then_inc(high_ready[1], 1)

            def residual(u, j):
                v, k, a = turn(u, j)
                hold(pool, mv_ready, 8 * u + j + 1, pace)
                nc.gpsimd.tensor_scalar(rstd[:], mv[:, 1:2], 1e-5, None, ALU.add).then_inc(var_ready, 1)
                pool.wait_ge(var_ready, 8 * u + j + 1)
                nc.gpsimd.tensor_tensor(rstd[:], rstd[:], power[:], ALU.pow).then_inc(rstd_ready, 1)
                pool.wait_ge(z_ready, 8 * u + j + 3)
                pool.wait_ge(s_loaded[k], 64 * v + 64)
                nc.gpsimd.tensor_tensor(x[k][:, a, :], x[k][:, a, :], z[j % 2][:], ALU.add).then_inc(x1_ready, 1)

            def tile(u, j):
                first, last = isinstance(u, int) and u == 0 and j == 0, isinstance(u, int) and 8 * u + j > LAST - 2
                if not last:
                    make_high(u, j + 2)
                if not first:
                    residual(u, j - 1)

            for j in range(2):
                make_high(0, j)
            skewed(nc.gpsimd, tile)
            residual(0, LAST)


def route_stage(nc, io, keep):
    with ExitStack() as ctx:
        t = Tools(nc, ctx, "s5")
        x = t.pair("x", [P, A, E])
        hl = t.pair("hl", [P, A, 2, E], F16)
        xT = t.pair("xT", [P, 2, EC, G], F16)
        stats, mv, rstd = t.pair("stats", [P, A, 6]), t.pair("mv", [P, A, 2]), t.pair("rstd", [P, A])
        power = t.sb("power", [P, A])
        token = t.pair("token", [P, A], U32)
        primed = t.sb("primed", [P, A], U32)
        slots = t.pair("slots", [P, A * K], U32)
        weights = t.pair("weights", [P, A, K])
        score, biased = t.sb("score", [P, A, NE]), t.sb("biased", [P, A, NE])
        top, index, chosen = t.sb("top", [P, A, 8]), t.sb("index", [P, A, 8], U32), t.sb("chosen", [P, A, K])
        onehot, picked = t.sb("onehot", [P, A, K, NE]), t.sb("picked", [P, A, K, NE])
        mask = t.sb("mask", [P, A, NE], F16)
        before_us, ours = t.sb("before_us", [P, NE], F16), t.sb("ours", [P, NE])
        slot, far, place = t.sb("slot", [P, A, NE]), t.sb("far", [P, A, NE]), t.sb("place", [P, A, K])
        w, total = t.sb("w", [P, A, K]), t.sb("total", [P, A])
        logits = [t.psum(f"logits{k}") for k in range(2)]
        position = t.psum("position")
        turned = [t.psum(f"turned{k}") for k in range(2)]
        x_loaded, token_loaded, scattered, xT_stored, rows_stored, slots_stored, weights_stored = (
            [t.sem(f"{n}{k}") for k in range(2)]
            for n in ("x_loaded", "token_loaded", "scattered", "xT_stored", "rows_stored", "slots_stored",
                      "weights_stored"))
        power_ready, stats_ready, mv_ready, var_ready, rstd_ready, x_ready, high_ready, low_ready = (
            t.sem(n) for n in ("power_ready", "stats_ready", "mv_ready", "var_ready", "rstd_ready", "x_ready",
                               "high_ready", "low_ready"))
        turned_ready, xT_ready = t.sem("turned_ready"), t.sem("xT_ready")
        logits_ready, score_ready, position_ready, mask_ready, step, slots_ready, sent, pace = (
            t.sem(n) for n in ("logits_ready", "score_ready", "position_ready", "mask_ready", "step", "slots_ready",
                               "sent", "pace"))
        STEPS = 19
        block = ctx.enter_context(nc.Block())

        @block.sync
        def _(sp):
            def load_x(u, k):
                hold(sp, low_ready, (2 * u + k) * A + A, pace)
                sp.dma_start(x[k][:], io["x1"][bass.ds((2 * u + k) * G, G), :].rearrange("(a p) e -> p a e", p=P)
                             ).then_inc(x_loaded[k], 16)

            def group(this, before, after):
                if after:
                    load_x(*after)
                u, k = this
                hold(sp, sent, 2 * u + k + 1, pace)
                sp.dma_start(token[k][:], io["token"][bass.ds(2 * u + k, 1)].rearrange("o p a -> p (o a)")
                             ).then_inc(token_loaded[k], 16)

            load_x(0, 0)
            chained(nc.sync, group)

        @block.tensor
        def _(pe):
            pe.sem_inc(logits_ready, 2)

            def turn(u, k):
                n = 2 * u + k
                for a in range(A):
                    pe.wait_ge(low_ready, n * A + a + 1 + 2 * A)
                    pe.wait_ge(xT_ready, n * A + a + 1)
                    for s in range(2):
                        for c in range(EC):
                            mm = nc.tensor.transpose(
                                turned[a % 2][:].bitcast(F16)[:, (s * EC + c) * P:(s * EC + c + 1) * P],
                                hl[k][:, a, s, c * P:(c + 1) * P], keep["ident16"][:])
                    mm.then_inc(turned_ready, 1)

            def make_logits(u, k):
                pe.wait_ge(score_ready, 2 * u + k + 1)
                for a in range(A):
                    pe.wait_ge(xT_ready, (2 * u + k) * A + a + 3)
                    for c in range(EC):
                        for s in range(2):
                            mm = nc.tensor.matmul(logits[k][:, a * NE:(a + 1) * NE],
                                                  xT[k][:, s, c, a * P:(a + 1) * P],
                                                  keep["gate"][:, c * NE:(c + 1) * NE],
                                                  start=(c == 0 and s == 0), stop=(c == EC - 1 and s == 1))
                mm.then_inc(logits_ready, 1)

            def group(this, before, after):
                u, k = this
                pe.wait_ge(mask_ready, 2 * u + k + 2)
                for a in range(A):
                    out = position[:, a * NE:(a + 1) * NE]
                    nc.tensor.matmul(out, keep["tri"][:], mask[:, a, :], start=True, stop=False)
                    for b in range(a):
                        nc.tensor.matmul(out, keep["ones"][:], mask[:, b, :], start=False, stop=False)
                    mm = nc.tensor.matmul(out, keep["ones"][:], before_us[:], start=False, stop=True)
                mm.then_inc(position_ready, 1)
                if after:
                    turn(*after)
                    make_logits(*after)

            turn(0, 0)
            make_logits(0, 0)
            chained(nc.tensor, group)

        @block.scalar
        def _(act):
            act.sem_inc(score_ready, 2)
            act.sem_inc(xT_ready, 2)
            for s in (*xT_stored, *rows_stored, *slots_stored, *weights_stored):
                act.sem_inc(s, 1)

            def turn(u, k):
                n = 2 * u + k
                act.wait_ge(rows_stored[k], 16 * u + 1)
                for a in range(A):
                    act.wait_ge(x_ready, n * A + a + 1)
                    nc.scalar.activation(hl[k][:, a, 0, :], x[k][:, a, :], ACT.Copy).then_inc(high_ready, 1)
                act.wait_ge(xT_stored[k], 16 * u + 1)
                for a in range(A):
                    act.wait_ge(turned_ready, n * A + a + 1)
                    nc.scalar.activation(
                        xT[k][:, :, :, a * P:(a + 1) * P],
                        turned[a % 2][:].bitcast(F16).rearrange("p (s c q) -> p s c q", s=2, c=EC),
                        ACT.Copy).then_inc(xT_ready, 1)
                act.wait_ge(xT_ready, n * A + A + 2)
                act.dma_start(io["xT2"][bass.ds(n, 1)].rearrange("o p n -> p (o n)"),
                              xT[k][:].rearrange("p s c q -> p (s c q)")).then_inc(xT_stored[k], 16)
                act.wait_ge(low_ready, n * A + 3 * A)
                act.dma_start(io["rows"][bass.ds(n * G, G), :].rearrange("(a p) n -> p a n", p=P),
                              hl[k][:].rearrange("p a s e -> p a (s e)")).then_inc(rows_stored[k], 16)

            def group(this, before, after):
                u, k = this
                act.wait_ge(logits_ready, 2 * u + k + 3)
                act.wait_ge(slots_ready, 2 * u + k + 1)
                nc.scalar.activation(score[:].rearrange("p a e -> p (a e)"), logits[k][:, 0:A * NE],
                                     ACT.Sigmoid).then_inc(score_ready, 1)
                if after:
                    turn(*after)
                act.wait_ge(slots_ready, 2 * u + k + 2)
                act.dma_start(io["slots"][bass.ds(2 * u + k, 1)].rearrange("o p n -> p (o n)"),
                              slots[k][:]).then_inc(slots_stored[k], 16)
                act.dma_start(io["weights"][bass.ds(2 * u + k, 1)].rearrange("o p n -> p (o n)"),
                              weights[k][:].rearrange("p a j -> p (a j)")).then_inc(weights_stored[k], 16)

            turn(0, 0)
            chained(nc.scalar, group)
            for s in (*xT_stored, *rows_stored, *slots_stored, *weights_stored):
                act.wait_ge(s, 16 * NG // 2 + 1)

        @block.vector
        def _(dve):
            nc.vector.memset(before_us[:], 0.0).then_inc(mask_ready, 1)
            dve.wait_ge(mask_ready, 1)
            dve.sem_inc(slots_ready, 1)
            dve.sem_inc(step, 1)
            dve.sem_inc(low_ready, 2 * A)
            number = keep["expert"][:, 0:NE].unsqueeze(1).unsqueeze(1).broadcast_to([P, A, K, NE])
            first = keep["expert"][:, NE:2 * NE].unsqueeze(1).broadcast_to([P, A, NE])
            bias = keep["bias"][:].unsqueeze(1).broadcast_to([P, A, NE])

            def measure(u, k):
                dve.wait_ge(x_loaded[k], 16 * u + 16)
                for a in range(A):
                    ins = nc.vector.bn_stats(stats[k][:, a, :], x[k][:, a, :])
                ins.then_inc(stats_ready, 1)
                hold(dve, stats_ready, 2 * u + k + 1, pace)
                for a in range(A):
                    ins = nc.vector.bn_aggr(mv[k][:, a, :], stats[k][:, a, :])
                ins.then_inc(mv_ready, 1)

            def normalize(u, k, a):
                dve.wait_ge(rstd_ready, 2 * u + k + 1)
                nc.vector.tensor_scalar(x[k][:, a, :], x[k][:, a, :], mv[k][:, a, 0:1], rstd[k][:, a:a + 1],
                                        ALU.subtract, ALU.mult).then_inc(x_ready, 1)

            def make_low(u, k, a):
                dve.wait_ge(high_ready, (2 * u + k) * A + a + 1)
                nc.vector.tensor_tensor(hl[k][:, a, 1, :], x[k][:, a, :], hl[k][:, a, 0, :],
                                        ALU.subtract).then_inc(low_ready, 1)

            def per_choice(x):
                return x.unsqueeze(2).broadcast_to([P, A, K, NE])

            def group(this, before, after):
                u, k = this
                done = [2 * STEPS * u + STEPS * k + 1]

                def then(ins):
                    ins.then_inc(step, 1)
                    done[0] = done[0] + 1
                    hold(dve, step, done[0], pace)

                if after:
                    measure(*after)
                dve.wait_ge(score_ready, 2 * u + k + 3)
                then(nc.vector.tensor_tensor(biased[:], score[:], bias, ALU.add))
                for a in range(A):
                    ins = nc.vector.max(top[:, a, :], biased[:, a, :])
                then(ins)
                for a in range(A):
                    ins = nc.vector.max_index(index[:, a, :], top[:, a, :], biased[:, a, :])
                then(ins)
                then(nc.vector.tensor_copy(chosen[:], index[:, :, 0:K]))
                then(nc.vector.tensor_tensor(onehot[:], number, chosen[:].unsqueeze(3).broadcast_to([P, A, K, NE]),
                                             ALU.is_equal))
                with nc.allow_low_precision(reason="sums of zeros and one 1"):
                    ins = nc.vector.tensor_reduce(mask[:], onehot[:].rearrange("p a j e -> p a e j"), AX.X, ALU.add)
                ins.then_inc(mask_ready, 1)
                if after:
                    for a in range(A):
                        normalize(*after, a)
                then(nc.vector.tensor_tensor(picked[:], onehot[:], per_choice(score[:]), ALU.mult))
                then(nc.vector.tensor_reduce(w[:], picked[:], AX.X, ALU.add))
                if after:
                    make_low(*after, 0)
                then(nc.vector.tensor_reduce(total[:], w[:], AX.X, ALU.add))
                if after:
                    make_low(*after, 1)
                then(nc.vector.tensor_scalar(total[:], total[:], 1e-12, None, ALU.max))
                if after:
                    make_low(*after, 2)
                then(nc.vector.reciprocal(total[:], total[:]))
                if after:
                    make_low(*after, 3)
                then(nc.vector.tensor_tensor(w[:], w[:], total[:].unsqueeze(2).broadcast_to([P, A, K]), ALU.mult))
                dve.wait_ge(position_ready, 2 * u + k + 1)
                then(nc.vector.tensor_reduce(ours[:], mask[:].rearrange("p a e -> p e a"), AX.X, ALU.add))
                then(nc.vector.tensor_tensor(before_us[:], before_us[:], ours[:], ALU.add))
                where = position[:, 0:A * NE].rearrange("p (a e) -> p a e", e=NE)
                then(nc.vector.tensor_scalar(far[:], where, float(CAP), NOWHERE, ALU.is_ge, ALU.mult))
                then(nc.vector.tensor_tensor(slot[:], where, first, ALU.add))
                then(nc.vector.tensor_tensor(slot[:], slot[:], far[:], ALU.add))
                then(nc.vector.tensor_tensor(picked[:], onehot[:], per_choice(slot[:]), ALU.mult))
                then(nc.vector.tensor_reduce(place[:], picked[:], AX.X, ALU.add))
                dve.wait_ge(weights_stored[k], 16 * u + 1)
                then(nc.vector.scalar_tensor_tensor(out=weights[k][:], in0=place[:], scalar=NOWHERE / 2, in1=w[:],
                                                    op0=ALU.is_lt, op1=ALU.mult))
                dve.wait_ge(slots_stored[k], 16 * u + 1)
                dve.wait_ge(sent, 2 * u + k + 1)
                nc.vector.tensor_copy(slots[k][:], place[:].rearrange("p a j -> p (a j)")).then_inc(slots_ready, 1)
                dve.wait_ge(slots_ready, 2 * u + k + 2)

            measure(0, 0)
            for a in range(A):
                normalize(0, 0, a)
            for a in range(A):
                make_low(0, 0, a)
            chained(nc.vector, group)

        @block.gpsimd
        def _(pool):
            nc.gpsimd.memset(power[:], -0.5).then_inc(power_ready, 1)
            pool.wait_ge(power_ready, 1)
            pool.sem_inc(sent, 1)
            for k in range(2):
                pool.dma_start(primed[:], io["token"][0:1].rearrange("o p a -> p (o a)")
                               ).then_inc(scattered[k], 16)
                hold(pool, scattered[k], 16, pace)

            def make_rstd(u, k):
                n = 2 * u + k
                hold(pool, mv_ready, n + 1, pace)
                nc.gpsimd.tensor_scalar(rstd[k][:], mv[k][:, :, 1], 1e-5, None, ALU.add).then_inc(var_ready, 1)
                pool.wait_ge(var_ready, n + 1)
                nc.gpsimd.tensor_tensor(rstd[k][:], rstd[k][:], power[:], ALU.pow).then_inc(rstd_ready, 1)

            def scatter(u, k, a):
                for j in range(K):
                    nc.gpsimd.indirect_dma_start(
                        out=io["slot_token"],
                        out_offset=bass.IndirectOffsetOnAxis(ap=slots[k][:, a * K + j:a * K + j + 1], axis=0),
                        in_=token[k][:, a:a + 1], in_offset=None, bounds_check=NSLOT - 1, oob_is_err=False,
                    ).then_inc(scattered[k], 16)

            def scatter_all(u, k, after):
                hold(pool, token_loaded[k], 16 * u + 16, pace)
                hold(pool, slots_ready, 2 * u + k + 2, pace)
                if after:
                    make_rstd(*after)
                scatter(u, k, 0)
                hold(pool, scattered[1 - k], 16 * A * K * (u + k) + 16, pace)
                pool.sem_inc(sent, 1)
                for a in range(1, A):
                    scatter(u, k, a)

            def group(this, before, after):
                if before:
                    scatter_all(*before, after)
                elif after:
                    make_rstd(*after)

            make_rstd(0, 0)
            chained(nc.gpsimd, group)
            scatter_all(NG // 2 - 1, 1, None)
            hold(pool, scattered[1], 16 * A * K * NG // 2 + 16, pace)


def expert_stage(nc, io, keep):
    with ExitStack() as ctx:
        t = Tools(nc, ctx, "s6")
        IC = I // P
        w1, w3 = (t.pair(n, [P, EC, I], BF16) for n in ("w1", "w3"))
        w2 = t.pair("w2", [P, IC, E], BF16)
        token = t.pair("token", [P, A], U32)
        rows = t.pair("rows", [P, A, 2 * E], F16)
        xT = t.pair("xT", [P, 2, EC, G], F16)
        gate, h = t.pair("gate", [P, G]), t.pair("h", [P, G])
        parts = t.pair("parts", [P, IC, 2, G], F16)
        y = t.pair("y", [P, A, E])
        turned = [t.psum(f"turned{b}") for b in range(2)]
        gates = [t.psum(f"gates{b}") for b in range(2)]
        ups = [t.psum(f"ups{b}") for b in range(2)]
        ys = [t.psum(f"ys{b}") for b in range(2)]
        w_loaded, w2_loaded, token_loaded, gathered, stored = (
            [t.sem(f"{n}{k}") for k in range(2)] for n in ("w_loaded", "w2_loaded", "token_loaded", "gathered", "stored"))
        turned_ready, xT_ready, up_ready, gate_ready, h_ready, high_ready, low_ready = (
            t.sem(n) for n in ("turned_ready", "xT_ready", "up_ready", "gate_ready", "h_ready", "high_ready",
                               "low_ready"))
        y_ready, y_copied, pace = t.sem("y_ready"), t.sem("y_copied"), t.sem("pace")
        dst = io["ye"].rearrange("(n p a) e -> n p a e", a=A, p=P)
        ids = io["slot_token"].rearrange("(n p a) o -> n p (a o)", p=P, a=A)
        block = ctx.enter_context(nc.Block())

        @block.sync
        def _(sp):
            with nc.sync.Fori(0, NE // 2) as u:
                for k in range(2):
                    e = bass.ds(2 * u + k, 1)
                    hold(sp, up_ready, 4 * u + 2 * k + 1, pace)
                    for w, name in ((w1, "W1"), (w3, "W3")):
                        sp.dma_start(w[k][:], io[name][e].rearrange("o (c p) i -> p (o c) i", p=P)
                                     ).then_inc(w_loaded[k], 16)
                    hold(sp, y_ready, 8 * u + 4 * k + 1, pace)
                    sp.dma_start(w2[k][:], io["W2"][e].rearrange("o (c p) i -> p (o c) i", p=P)
                                 ).then_inc(w2_loaded[k], 16)

        @block.gpsimd
        def _(pool):
            with nc.gpsimd.Fori(0, NE // 2) as u:
                for k in range(2):
                    hold(pool, turned_ready, 8 * u + 4 * k + 1, pace)
                    pool.dma_start(token[k][:], ids[bass.ds(2 * u + k, 1)].rearrange("o p a -> p (o a)")
                                   ).then_inc(token_loaded[k], 16)
                    hold(pool, token_loaded[k], 16 * u + 16, pace)
                    for a in range(A):
                        nc.gpsimd.indirect_dma_start(
                            out=rows[k][:, a, :], out_offset=None, in_=io["rows"],
                            in_offset=bass.IndirectOffsetOnAxis(ap=token[k][:, a:a + 1], axis=0),
                            bounds_check=T - 1, oob_is_err=False).then_inc(gathered[k], 16)

        @block.tensor
        def _(pe):
            pe.sem_inc(turned_ready, 5)
            pe.sem_inc(up_ready, 3)
            pe.sem_inc(y_ready, 5)

            def turn(u, k, a):
                if a == 0:
                    pe.wait_ge(gathered[k], 16 * A * u + 16 * A)
                pe.wait_ge(xT_ready, 8 * u + 4 * k + a + 1)
                for s in range(2):
                    for c in range(EC):
                        mm = nc.tensor.transpose(
                            turned[a % 2][:].bitcast(F16)[:, (s * EC + c) * P:(s * EC + c + 1) * P],
                            rows[k][:, a, (s * EC + c) * P:(s * EC + c + 1) * P], keep["ident16"][:])
                mm.then_inc(turned_ready, 1)

            def up(u, k):
                pe.wait_ge(xT_ready, 8 * u + 4 * k + 4 + 2)
                pe.wait_ge(w_loaded[k], 32 * u + 32)
                for i in range(IC):
                    pe.wait_ge(h_ready, 4 * u + 2 * k + i + 1)
                    for bank, w in ((gates[i], w1[k]), (ups[i], w3[k])):
                        for c in range(EC):
                            for s in range(2):
                                mm = nc.tensor.matmul(bank[:], w[:, c, i * P:(i + 1) * P], xT[k][:, s, c, :],
                                                      start=(c == 0 and s == 0), stop=(c == EC - 1 and s == 1))
                    mm.then_inc(up_ready, 1)

            def down(u, k, a):
                if a == 0:
                    pe.wait_ge(low_ready, 4 * u + 2 * k + 2)
                    pe.wait_ge(w2_loaded[k], 16 * u + 16)
                pe.wait_ge(y_copied, 8 * u + 4 * k + a + 1)
                for i in range(IC):
                    for s in range(2):
                        mm = nc.tensor.matmul(ys[a % 2][:], parts[k][:, i, s, a * P:(a + 1) * P], w2[k][:, i, :],
                                              start=(i == 0 and s == 0), stop=(i == IC - 1 and s == 1))
                mm.then_inc(y_ready, 1)

            for a in range(A):
                turn(0, 0, a)
            up(0, 0)
            for a in range(A):
                turn(0, 1, a)
            with nc.tensor.Fori(0, NE // 2 - 1) as u:
                up(u, 1)
                for a in range(A):
                    turn(u + 1, 0, a)
                    down(u, 0, a)
                up(u + 1, 0)
                for a in range(A):
                    turn(u + 1, 1, a)
                    down(u, 1, a)
            up(NE // 2 - 1, 1)
            for k in range(2):
                for a in range(A):
                    down(NE // 2 - 1, k, a)

        @block.scalar
        def _(act):
            act.sem_inc(xT_ready, 2)
            for k in range(2):
                act.sem_inc(stored[k], 1)

            def turn(u, k):
                act.wait_ge(up_ready, 4 * u + 2 * k + 1)
                for a in range(A):
                    act.wait_ge(turned_ready, 8 * u + 4 * k + a + 6)
                    nc.scalar.activation(
                        xT[k][:, :, :, a * P:(a + 1) * P],
                        turned[a % 2][:].bitcast(F16).rearrange("p (s c q) -> p s c q", s=2, c=EC),
                        ACT.Copy).then_inc(xT_ready, 1)

            def up(u, k):
                for i in range(IC):
                    n = 4 * u + 2 * k + i
                    act.wait_ge(up_ready, n + 4)
                    act.wait_ge(h_ready, n + 1)
                    nc.scalar.activation(gate[i][:], gates[i][:], ACT.Silu).then_inc(gate_ready, 1)
                    if i == 0:
                        act.wait_ge(y_ready, 8 * u + 4 * k + 1)
                    act.wait_ge(h_ready, n + 3)
                    nc.scalar.activation(parts[k][:, i, 0, :], h[i][:], ACT.Copy).then_inc(high_ready, 1)

            def store(u, k):
                act.wait_ge(y_copied, 8 * u + 4 * k + 4 + 2)
                act.dma_start(dst[bass.ds(2 * u + k, 1)].rearrange("o p a e -> p (o a) e"),
                              y[k][:]).then_inc(stored[k], 16)

            turn(0, 0)
            up(0, 0)
            turn(0, 1)
            with nc.scalar.Fori(0, NE // 2 - 1) as u:
                up(u, 1)
                turn(u + 1, 0)
                store(u, 0)
                up(u + 1, 0)
                turn(u + 1, 1)
                store(u, 1)
            up(NE // 2 - 1, 1)
            for k in range(2):
                store(NE // 2 - 1, k)
            for k in range(2):
                act.wait_ge(stored[k], 16 * NE // 2 + 1)

        @block.vector
        def _(dve):
            dve.sem_inc(h_ready, 2)
            dve.sem_inc(y_copied, 2)

            def up(u, k):
                for i in range(IC):
                    n = 4 * u + 2 * k + i
                    dve.wait_ge(gate_ready, n + 1)
                    nc.vector.scalar_tensor_tensor(out=h[i][:], in0=gate[i][:], scalar=H_SCALE, in1=ups[i][:],
                                                   op0=ALU.mult, op1=ALU.mult).then_inc(h_ready, 1)
                    dve.wait_ge(high_ready, n + 1)
                    nc.vector.tensor_tensor(parts[k][:, i, 1, :], h[i][:], parts[k][:, i, 0, :],
                                            ALU.subtract).then_inc(low_ready, 1)

            def down(u, k):
                dve.wait_ge(stored[k], 16 * u + 1)
                for a in range(A):
                    dve.wait_ge(y_ready, 8 * u + 4 * k + a + 6)
                    nc.vector.tensor_scalar(y[k][:, a, :], ys[a % 2][:], 1.0 / H_SCALE, None, ALU.mult).then_inc(y_copied, 1)

            up(0, 0)
            with nc.vector.Fori(0, NE // 2 - 1) as u:
                up(u, 1)
                down(u, 0)
                up(u + 1, 0)
                down(u, 1)
            up(NE // 2 - 1, 1)
            down(NE // 2 - 1, 0)
            down(NE // 2 - 1, 1)


def combine_stage(nc, io, keep):
    with ExitStack() as ctx:
        t = Tools(nc, ctx, "s7")
        IC = I // P
        w1, w3, w2 = t.sb("w1", [P, EC, I], BF16), t.sb("w3", [P, EC, I], BF16), t.sb("w2", [P, IC, E], BF16)
        xT = t.pair("xT", [P, 2, EC, G], F16)
        gate, h = t.pair("gate", [P, G]), t.pair("h", [P, G])
        parts = t.pair("parts", [P, IC, 2, G], F16)
        slots = t.pair("slots", [P, A * K], U32)
        weights = t.pair("weights", [P, A * K])
        total = t.pair("total", [P, A, E])
        x1 = t.pair("x1", [P, A, E])
        picked = [t.sb(f"picked{a}", [P, K, E]) for a in range(A)]
        stats, mv = t.sb("stats", [P, A, 6]), t.sb("mv", [P, A, 2])
        rstd, shift, power = (t.sb(n, [P, A]) for n in ("rstd", "shift", "power"))
        gates = [t.psum(f"gates{b}") for b in range(2)]
        ups = [t.psum(f"ups{b}") for b in range(2)]
        ys = [t.psum(f"ys{b}") for b in range(2)]
        w_loaded = t.sem("w_loaded")
        xT_loaded, s_loaded, weights_loaded, x1_loaded, out_stored = (
            [t.sem(f"{n}{k}") for k in range(2)]
            for n in ("xT_loaded", "s_loaded", "weights_loaded", "x1_loaded", "out_stored"))
        gathered = [t.sem(f"gathered{a}") for a in range(A)]
        up_ready, gate_ready, h_ready, high_ready, low_ready, y_ready, y_used, w2_ready = (
            t.sem(n) for n in ("up_ready", "gate_ready", "h_ready", "high_ready", "low_ready", "y_ready", "y_used",
                               "w2_ready"))
        cleared, summed, stats_ready, mv_ready, var_ready, rstd_ready, shift_ready, z_ready, out_ready, pace = (
            t.sem(n) for n in ("cleared", "summed", "stats_ready", "mv_ready", "var_ready", "rstd_ready",
                               "shift_ready", "z_ready", "out_ready", "pace"))
        power_ready = t.sem("power_ready")
        LAST = (NG // 2 - 1, 1)
        block = ctx.enter_context(nc.Block())

        @block.sync
        def _(sp):
            sp.dma_start(w1[:], io["sw1"].rearrange("(c p) i -> p c i", p=P)).then_inc(w_loaded, 16)
            sp.dma_start(w3[:], io["sw3"].rearrange("(c p) i -> p c i", p=P)).then_inc(w_loaded, 16)
            sp.dma_start(w2[:], io["sw2"].rearrange("(c p) i -> p c i", p=P)).then_inc(w_loaded, 16)

            def load_xT(u, k):
                hold(sp, up_ready, 4 * u + 2 * k + 1, pace)
                sp.dma_start(xT[k][:].rearrange("p s c q -> p (s c q)"),
                             io["xT2"][bass.ds(2 * u + k, 1)].rearrange("o p n -> p (o n)")).then_inc(xT_loaded[k], 16)

            def group(this, before, after):
                u, k = this
                n = bass.ds(2 * u + k, 1)
                if after:
                    load_xT(*after)
                hold(sp, summed, (2 * u + k) * A * K + 1, pace)
                sp.dma_start(slots[k][:], io["slots"][n].rearrange("o p n -> p (o n)")).then_inc(s_loaded[k], 16)
                sp.dma_start(weights[k][:], io["weights"][n].rearrange("o p n -> p (o n)")
                             ).then_inc(weights_loaded[k], 16)
                hold(sp, out_stored[k], 16 * u + 1, pace)
                sp.dma_start(x1[k][:], io["x1"][bass.ds((2 * u + k) * G, G), :].rearrange("(a p) e -> p a e", p=P)
                             ).then_inc(x1_loaded[k], 16)

            load_xT(0, 0)
            chained(nc.sync, group)

        @block.gpsimd
        def _(pool):
            nc.gpsimd.memset(power[:], -0.5).then_inc(power_ready, 1)
            pool.wait_ge(power_ready, 1)
            pool.wait_ge(cleared, A)

            def gather(u, k, a):
                hold(pool, summed, (2 * u + k) * A * K + a * K + K + 1, pace)
                for j in range(K):
                    nc.gpsimd.indirect_dma_start(
                        out=picked[a][:, j, :], out_offset=None, in_=io["ye"],
                        in_offset=bass.IndirectOffsetOnAxis(ap=slots[k][:, a * K + j:a * K + j + 1], axis=0),
                        bounds_check=NSLOT - 1, oob_is_err=False).then_inc(gathered[a], 16)

            def group(this, before, after):
                n = 2 * this[0] + this[1]
                if after:
                    hold(pool, s_loaded[after[1]], 16 * after[0] + 16, pace)
                    for a in range(A - 1):
                        gather(*after, a)
                hold(pool, mv_ready, n + 1, pace)
                nc.gpsimd.tensor_scalar(rstd[:], mv[:, :, 1], 1e-5, None, ALU.add).then_inc(var_ready, 1)
                pool.wait_ge(var_ready, n + 1)
                nc.gpsimd.tensor_tensor(rstd[:], rstd[:], power[:], ALU.pow).then_inc(rstd_ready, 1)
                if after:
                    gather(*after, A - 1)

            hold(pool, s_loaded[0], 16, pace)
            for a in range(A):
                gather(0, 0, a)
            chained(nc.gpsimd, group)

        @block.tensor
        def _(pe):
            pe.sem_inc(up_ready, 3)
            pe.wait_ge(w_loaded, 48)
            pe.wait_ge(w2_ready, 1)

            def up(u, k):
                pe.wait_ge(xT_loaded[k], 16 * u + 16)
                for i in range(IC):
                    pe.wait_ge(h_ready, 4 * u + 2 * k + i + 1)
                    for bank, w in ((gates[i], w1), (ups[i], w3)):
                        for c in range(EC):
                            for s in range(2):
                                mm = nc.tensor.matmul(bank[:], w[:, c, i * P:(i + 1) * P], xT[k][:, s, c, :],
                                                      start=(c == 0 and s == 0), stop=(c == EC - 1 and s == 1))
                    mm.then_inc(up_ready, 1)

            def down(u, k):
                pe.wait_ge(low_ready, 4 * u + 2 * k + 2)
                for a in range(A):
                    pe.wait_ge(y_used, 8 * u + 4 * k + a + 1)
                    for i in range(IC):
                        for s in range(2):
                            mm = nc.tensor.matmul(ys[a % 2][:], parts[k][:, i, s, a * P:(a + 1) * P], w2[:, i, :],
                                                  start=(i == 0 and s == 0), stop=(i == IC - 1 and s == 1))
                    mm.then_inc(y_ready, 1)

            def group(this, before, after):
                if after:
                    up(*after)
                down(*this)

            up(0, 0)
            chained(nc.tensor, group)

        @block.scalar
        def _(act):
            for k in range(2):
                act.sem_inc(out_stored[k], 1)

            act.wait_ge(w_loaded, 48)
            nc.scalar.activation(w2[:], w2[:], ACT.Copy, scale=1.0 / H_SCALE).then_inc(w2_ready, 1)

            def silu(u, k, i):
                act.wait_ge(up_ready, 4 * u + 2 * k + i + 4)
                act.wait_ge(h_ready, 4 * u + 2 * k + i + 1)
                nc.scalar.activation(gate[i][:], gates[i][:], ACT.Silu).then_inc(gate_ready, 1)

            def make_high(u, k, i):
                act.wait_ge(h_ready, 4 * u + 2 * k + i + 3)
                nc.scalar.activation(parts[k][:, i, 0, :], h[i][:], ACT.Copy).then_inc(high_ready, 1)

            def scale(u, k):
                act.wait_ge(shift_ready, 2 * u + k + 1)
                for a in range(A):
                    ins = nc.scalar.activation(total[k][:, a, :], total[k][:, a, :], ACT.Identity,
                                               bias=shift[:, a:a + 1], scale=rstd[:, a:a + 1])
                ins.then_inc(z_ready, 1)

            def store(u, k):
                act.wait_ge(out_ready, 2 * u + k + 1)
                act.dma_start(io["out"][bass.ds((2 * u + k) * G, G), :].rearrange("(a p) e -> p a e", p=P),
                              x1[k][:]).then_inc(out_stored[k], 16)

            def group(this, before, after):
                if after:
                    for i in range(IC):
                        silu(*after, i)
                    make_high(*after, 0)
                if before:
                    scale(*before)
                if after:
                    make_high(*after, 1)
                if before:
                    store(*before)

            for i in range(IC):
                silu(0, 0, i)
            for i in range(IC):
                make_high(0, 0, i)
            chained(nc.scalar, group)
            scale(*LAST)
            store(*LAST)
            for k in range(2):
                act.wait_ge(out_stored[k], 16 * NG // 2 + 1)

        @block.vector
        def _(dve):
            for a in range(A):
                nc.vector.memset(picked[a][:].rearrange("p j e -> p (j e)"), 0.0).then_inc(cleared, 1)
            dve.wait_ge(cleared, A)
            dve.sem_inc(summed, A * K + 1)
            dve.sem_inc(h_ready, 2)
            dve.sem_inc(y_used, 2)

            def hidden(u, k, i):
                n = 4 * u + 2 * k + i
                dve.wait_ge(gate_ready, n + 1)
                nc.vector.scalar_tensor_tensor(out=h[i][:], in0=gate[i][:], scalar=H_SCALE, in1=ups[i][:],
                                               op0=ALU.mult, op1=ALU.mult).then_inc(h_ready, 1)

            def low(u, k, i):
                dve.wait_ge(high_ready, 4 * u + 2 * k + i + 1)
                nc.vector.tensor_tensor(parts[k][:, i, 1, :], h[i][:], parts[k][:, i, 0, :],
                                        ALU.subtract).then_inc(low_ready, 1)

            def weigh(u, k, a):
                g = 2 * u + k
                dve.wait_ge(gathered[a], 16 * K * (g + 1))
                for j in range(K):
                    if j == 0:
                        dve.wait_ge(y_ready, 4 * g + a + 1)
                    nc.vector.scalar_tensor_tensor(
                        out=total[k][:, a, :], in0=picked[a][:, j, :], scalar=weights[k][:, a * K + j:a * K + j + 1],
                        in1=ys[a % 2][:] if j == 0 else total[k][:, a, :], op0=ALU.mult,
                        op1=ALU.add).then_inc(summed, 1)
                    dve.wait_ge(summed, (g * A + a) * K + j + 1 + A * K + 1)
                    if j == 0:
                        dve.sem_inc(y_used, 1)
                ins = nc.vector.bn_stats(stats[:, a, :], total[k][:, a, :])
                if a == A - 1:
                    ins.then_inc(stats_ready, 1)

            def aggregate(u, k):
                hold(dve, stats_ready, 2 * u + k + 1, pace)
                for a in range(A):
                    ins = nc.vector.bn_aggr(mv[:, a, :], stats[:, a, :])
                ins.then_inc(mv_ready, 1)

            def make_shift(u, k):
                dve.wait_ge(rstd_ready, 2 * u + k + 1)
                nc.vector.scalar_tensor_tensor(out=shift[:], in0=mv[:, :, 0], scalar=-1.0, in1=rstd[:], op0=ALU.mult,
                                               op1=ALU.mult).then_inc(shift_ready, 1)

            def add(u, k):
                dve.wait_ge(z_ready, 2 * u + k + 1)
                dve.wait_ge(x1_loaded[k], 16 * u + 16)
                nc.vector.tensor_tensor(x1[k][:], x1[k][:], total[k][:], ALU.add).then_inc(out_ready, 1)

            def group(this, before, after):
                dve.wait_ge(weights_loaded[this[1]], 16 * this[0] + 16)
                if after:
                    hidden(*after, 0)
                weigh(*this, 0)
                if after:
                    low(*after, 0)
                if before:
                    make_shift(*before)
                weigh(*this, 1)
                if after:
                    hidden(*after, 1)
                weigh(*this, 2)
                if after:
                    low(*after, 1)
                if before:
                    add(*before)
                weigh(*this, 3)
                aggregate(*this)

            for i in range(IC):
                hidden(0, 0, i)
            for i in range(IC):
                low(0, 0, i)
            dve.wait_ge(low_ready, IC)
            chained(nc.vector, group)
            make_shift(*LAST)
            add(*LAST)


SCRATCH = {
    "qk": ([NG, 2, 2 * E, G], F16),
    "v": ([NG, P, A, E], F32),
    "en": ([NG, P, A, 2 * H], F32),
    "sums": ([C, P, 2 * H * (D + 1)], F16),
    "largest": ([C, P, H], F32),
    "x1": ([T, E], F32),
    "xT2": ([NG, P, 2 * EC * G], F16),
    "rows": ([T, 2 * E], F16),
    "slot_token": ([NSLOT, 1], U32),
    "slots": ([NG, P, A * K], U32),
    "weights": ([NG, P, A * K], F32),
    "ye": ([NSLOT, E], F32),
}
CONSTS = {
    "ident16": ([P, P], F16), "ident32": ([P, P], F32), "heads": ([P, HPC], F16),
    "tri": ([P, P], F16), "ones": ([P, P], F16), "gate": ([P, EC * NE], BF16), "expert": ([P, 2 * NE], F32),
    "bias": ([P, NE], F32),
}


def build(nc, io):
    for name, (shape, dt) in SCRATCH.items():
        io[name] = nc.dram_tensor(f"{name}_dram", shape, dt, kind="Internal").ap()
    with ExitStack() as ctx:
        keep = {n: ctx.enter_context(nc.sbuf_tensor(f"keep_{n}", s, d)) for n, (s, d) in CONSTS.items()}
        keep["wqkv"] = ctx.enter_context(nc.sbuf_tensor("keep_wqkv", [P, 2, EC, 3 * E], F16))
        keep["wo"] = ctx.enter_context(nc.sbuf_tensor("keep_wo", [P, EC, E], F32))
        keep["feat"] = ctx.enter_context(nc.sbuf_tensor("keep_feat", [96, H, M], F16))
        setup_stage(nc, io, keep)
        project_stage(nc, io, keep)
        sums_stage(nc, io, keep)
        attend_stage(nc, io, keep)
        route_stage(nc, io, keep)
        expert_stage(nc, io, keep)
        combine_stage(nc, io, keep)


def shape_constants():
    import numpy as np

    had = np.ones((1, 1), np.float32)
    while had.shape[0] < HP:
        had = np.block([[had, had], [had, -had]])
    d = np.arange(P) % D
    freq = (np.float32(10000.0) ** (-np.arange(0, D, 2, dtype=np.float32) / np.float32(D))).astype(np.float32)
    angle = np.arange(L - 1, dtype=np.float32)[:, None] * freq
    cos = np.concatenate([np.ones((1, D // 2), np.float32), np.cos(angle)]).T[d // 2]
    sin = np.concatenate([np.zeros((1, D // 2), np.float32), np.sin(angle)]).T[d // 2]
    sin = sin * np.where(d % 2 == 0, -1, 1)[:, None]
    turns = np.stack([cos, sin], 1).reshape(P, 2, GPC, G).transpose(2, 0, 1, 3)
    heads = np.arange(P)[:, None] // D == np.arange(HPC)
    expert = np.concatenate([np.arange(NE), np.arange(NE) * CAP])[None].astype(np.float32)
    token = np.arange(T, dtype=np.uint32).reshape(NG, A, P).transpose(0, 2, 1)
    return {
        "had": had.astype(np.float32), "turns": turns.astype(np.float32), "ident16": np.eye(P, dtype=np.float16),
        "ident32": np.eye(P, dtype=np.float32), "heads": heads.astype(np.float16),
        "tri": np.triu(np.ones((P, P)), 1).astype(np.float16),
        "ones": np.ones((P, P), np.float16), "expert": expert, "token": token,
    }


def kernel(**inputs):
    import concourse.bacc as _bacc
    import numpy as np
    from concourse.bass_utils import run_bass_kernel_spmd as _run

    v = {n[3:]: np.asarray(a) for n, a in inputs.items()}
    signs, scales = v["attn_sorf_signs"], v["attn_sorf_scales"]
    laid = {
        "x": v["attn_x"].reshape(T, E),
        "w_qkvT": v["attn_w_qkv"].T,
        "w_outT": v["attn_w_out"].T,
        "signs": signs[:, :M // HP].transpose(3, 2, 0, 1).reshape(HP, 3, H * M // HP),
        "scales": scales[:, :M // HP].reshape(1, -1),
        "gate": v["ffn_gate_w"].T.reshape(EC, P, NE).transpose(1, 0, 2).reshape(P, -1),
        "bias": v["ffn_bias"].reshape(1, -1),
        "W1": v["ffn_W1"], "W3": v["ffn_W3"], "W2": v["ffn_W2"],
        "sw1": v["ffn_sw1"].T, "sw3": v["ffn_sw3"].T, "sw2": v["ffn_sw2"].T,
        **shape_constants(),
    }
    nc = _bacc.Bacc("TRN2", target_bir_lowering=False, num_devices=1)
    arrays, io = {}, {}
    for name, a in laid.items():
        a = np.ascontiguousarray(a)
        arrays[f"{name}_in"] = a
        io[name] = nc.dram_tensor(f"{name}_in", a.shape, mybir.dt.from_np(a.dtype), kind="ExternalInput").ap()
    io["out"] = nc.dram_tensor("out_dram", [T, E], F32, kind="ExternalOutput").ap()
    build(nc, io)
    return _run(nc, [arrays], core_ids=[0]).results[0]["out_dram"].reshape(C, L, E)
```
